# Optimizing a Trainium2 kernel written in Bass

```python
import numpy as np
import jax
import jax.numpy as jnp

def _softmax(x, axis=-1):
    return jax.nn.softmax(x, axis=axis)

def _gelu(x):
    return jax.nn.gelu(x, approximate=True)

def _silu(x):
    return jax.nn.silu(x)

def _sigmoid(x):
    return jax.nn.sigmoid(x)

def _layernorm(x, axis=-1, eps=1e-05):
    m = jnp.mean(x, axis=axis, keepdims=True)
    v = jnp.var(x, axis=axis, keepdims=True)
    return (x - m) / jnp.sqrt(v + eps)

def _scatter_add(tgt, idx, src, axis=0):
    return tgt.at[idx].add(src)

def _segment_sum(src, seg, n):
    return jax.ops.segment_sum(src, seg, n)
kernel_name = 'mk_vit_tower_d2_tok_img768_r4_fab26f'

def setup_inputs(seed: int=0):
    np.random.seed(seed)
    _w = jnp.asarray

    def _rec_inputs():
        import jax
        import jax.numpy as jnp
        _rk = jax.random.key(seed)
        x = -0.000222058 + 0.999998 * jax.random.normal(jax.random.fold_in(_rk, 1), (64, 3, 128, 128), jnp.float32)
        return x
    x = _rec_inputs()

    def _L0_tok_setup():
        import jax, jax.numpy as jnp
        import numpy as np
        MAX_PATCH = 16

        def _create_patches(x, P):
            B, C, H, W = x.shape
            nH, nW = (H // P, W // P)
            x = x.reshape(B, C, nH, P, W).transpose(0, 1, 2, 4, 3)
            x = x.reshape(B, C, nH, nW, P, P).transpose(0, 1, 2, 3, 5, 4)
            x = x.reshape(B, nH * nW, P, P, C)
            x = x.transpose(0, 1, 4, 2, 3).reshape(B, nH * nW * C, P, P)
            return x
        key = jax.random.key(seed)
        k1, k2, k3 = jax.random.split(key, 3)
        B, C, H, Wd = (32, 3, 128, 128)
        P = min(H, Wd, MAX_PATCH)
        D_in = P * P * C
        D = 192
        x = jax.random.normal(k1, (B, C, H, Wd), dtype=jnp.float32)
        W = jax.random.normal(k2, (D, D_in), dtype=jnp.float32) * (1.0 / np.sqrt(D_in))
        b = jax.random.normal(k3, (D,), dtype=jnp.float32) * 0.01
        return {'x': x, 'W': W, 'b': b}
    _L0_tok_all = _L0_tok_setup()
    _L0_tok_in = {k: v for k, v in _L0_tok_all.items() if k in ('W', 'b')}
    del _L0_tok_all

    def _L0_attn_setup():
        import jax, jax.numpy as jnp
        import numpy as np
        B, T, D_MODEL = (2, 512, 192)
        N_HEADS = 12
        D_K = D_MODEL // N_HEADS
        MAX_SEQ_LEN = 512

        def _rotary_tables(dim, max_seq_len):
            angular_freq = (1.0 / 10000.0) ** jnp.linspace(0.0, 1.0, dim // 4, dtype=jnp.float32)
            angular_freq = jnp.concatenate([angular_freq, jnp.zeros(dim // 4, dtype=jnp.float32)])
            t = jnp.arange(max_seq_len, dtype=jnp.float32)
            theta = jnp.einsum('i,j->ij', t, angular_freq)
            return (jnp.cos(theta), jnp.sin(theta))

        def _apply_rotary(x, cos, sin):
            h = x.shape[-3]
            c = cos[None, :h, None, :]
            s = sin[None, :h, None, :]
            x1, x2 = jnp.split(x.astype(jnp.float32), 2, axis=-1)
            y1 = x1 * c + x2 * s
            y2 = -x1 * s + x2 * c
            return jnp.concatenate([y1, y2], axis=-1).astype(x.dtype)
        key = jax.random.key(seed)
        k1, k2, k3 = jax.random.split(key, 3)
        x = jax.random.normal(k1, (B, T, D_MODEL), dtype=jnp.float32)
        w_qkv = jax.random.normal(k2, (D_MODEL, 3 * D_MODEL), dtype=jnp.float32) * 0.02
        w_o = jax.random.normal(k3, (D_MODEL, D_MODEL), dtype=jnp.float32) * 0.02
        return {'x': x, 'w_qkv': w_qkv, 'w_o': w_o}
    _L0_attn_all = _L0_attn_setup()
    _L0_attn_in = {k: v for k, v in _L0_attn_all.items() if k in ('w_qkv', 'w_o')}
    del _L0_attn_all

    def _L0_ffn_setup():
        import jax, jax.numpy as jnp
        import numpy as np
        B_SZ, S, D = (8, 128, 192)
        H = 12
        N_EXP = 8
        RANK = 16
        ALPHA = 32
        TOP_K = 2
        key = jax.random.key(seed)
        ks = jax.random.split(key, 9)
        x = jax.random.normal(ks[0], (B_SZ, S, D), jnp.float32)
        W_qkv = jax.random.normal(ks[1], (3 * D, D), jnp.float32) * 0.02
        b_qkv = jnp.zeros((3 * D,), jnp.float32)
        W_gate = jax.random.normal(ks[2], (N_EXP, D), jnp.float32) * 0.02
        b_gate = jnp.zeros((N_EXP,), jnp.float32)
        A = jax.random.normal(ks[3], (N_EXP, RANK, D), jnp.float32) * 0.02
        B_lora = jax.random.normal(ks[4], (N_EXP, 3 * D, RANK), jnp.float32) * 0.02
        W_proj = jax.random.normal(ks[5], (D, D), jnp.float32) * 0.02
        b_proj = jnp.zeros((D,), jnp.float32)
        return {'x': x, 'W_qkv': W_qkv, 'b_qkv': b_qkv, 'W_gate': W_gate, 'b_gate': b_gate, 'A': A, 'B_lora': B_lora, 'W_proj': W_proj, 'b_proj': b_proj}
    _L0_ffn_all = _L0_ffn_setup()
    _L0_ffn_in = {k: v for k, v in _L0_ffn_all.items() if k in ('W_qkv', 'b_qkv', 'W_gate', 'b_gate', 'A', 'B_lora', 'W_proj', 'b_proj')}
    del _L0_ffn_all

    def _L1_attn_setup():
        import jax, jax.numpy as jnp
        import numpy as np
        N_HEADS = 12
        WINDOW = 12
        STRIDE = 3
        N_ANCHORS = 12
        EPS = 1e-06

        def fmap(x):
            return jax.nn.elu(x) + 1.0

        def _local_band(q, k, v, window):
            B, H, S, D = q.shape
            w = min(window, S)
            half = w // 2
            k_pad = jnp.pad(k, ((0, 0), (0, 0), (half, half), (0, 0)))
            v_pad = jnp.pad(v, ((0, 0), (0, 0), (half, half), (0, 0)))
            q_f = fmap(q)
            k_f = fmap(k_pad)
            idx = jnp.arange(S)[:, None] + jnp.arange(w)[None, :]
            k_unf = k_f[:, :, idx, :]
            v_unf = v_pad[:, :, idx, :]
            qk = jnp.einsum('bhsd,bhswd->bhsw', q_f, k_unf)
            out = jnp.einsum('bhsw,bhswd->bhsd', qk, v_unf)
            norm = jnp.clip(qk.sum(-1, keepdims=True), 1e-06, None)
            return out / norm

        def _stride_band(q, k, v, stride):
            k_s = fmap(k[:, :, ::stride])
            v_s = v[:, :, ::stride]
            q_f = fmap(q)
            kv = jnp.einsum('bhsd,bhse->bhde', k_s, v_s)
            out = jnp.einsum('bhsd,bhde->bhse', q_f, kv)
            k_sum = k_s.sum(axis=2)
            norm = jnp.clip(jnp.einsum('bhsd,bhd->bhs', q_f, k_sum)[..., None], 1e-06, None)
            return out / norm

        def _global_band(q, k, v, anchor_q, n_heads, n_anchors):
            B, H, S, D = q.shape
            aq = anchor_q.reshape(1, n_heads, n_anchors, D)
            aq = jnp.broadcast_to(aq, (B, n_heads, n_anchors, D))
            aq_f = fmap(aq)
            k_f = fmap(k)
            kv = jnp.einsum('bhsd,bhse->bhde', k_f, v)
            anchor_out = jnp.einsum('bhad,bhde->bhae', aq_f, kv)
            k_sum = k_f.sum(axis=2)
            anchor_norm = jnp.clip(jnp.einsum('bhad,bhd->bha', aq_f, k_sum)[..., None], 1e-06, None)
            anchor_out = anchor_out / anchor_norm
            q_f = fmap(q)
            anchor_k = fmap(aq)
            qk = jnp.einsum('bhsd,bhad->bhsa', q_f, anchor_k)
            out = jnp.einsum('bhsa,bhae->bhse', qk, anchor_out)
            qk_sum = jnp.clip(qk.sum(-1, keepdims=True), 1e-06, None)
            return out / qk_sum
        key = jax.random.key(seed)
        ks = jax.random.split(key, 4)
        B, S, D = (4, 512, 192)
        x = jax.random.normal(ks[0], (B, S, D), dtype=jnp.float32)
        qkv_w = jax.random.normal(ks[1], (3 * D, D), dtype=jnp.float32) * 0.02
        out_w = jax.random.normal(ks[2], (D, D), dtype=jnp.float32) * 0.02
        anchor_q = jax.random.normal(ks[3], (1, N_ANCHORS, D), dtype=jnp.float32) * 0.02
        w_local = jnp.float32(1.0 / 2.0)
        w_stride = jnp.float32(1.0 / 3.0)
        w_global = jnp.float32(1.0 / 6.0)
        return {'x': x, 'qkv_w': qkv_w, 'out_w': out_w, 'anchor_q': anchor_q, 'w_local': w_local, 'w_stride': w_stride, 'w_global': w_global}
    _L1_attn_all = _L1_attn_setup()
    _L1_attn_in = {k: v for k, v in _L1_attn_all.items() if k in ('qkv_w', 'out_w', 'anchor_q', 'w_local', 'w_stride', 'w_global')}
    del _L1_attn_all

    def _L1_ffn_setup():
        import jax, jax.numpy as jnp
        import numpy as np
        B, T, H, F, E = (128, 32, 192, 768, 3)
        key = jax.random.key(seed)
        ks = jax.random.split(key, 4)
        s = 0.02
        return {'x': jax.random.normal(ks[0], (B, T, H), jnp.float32), 'Wg': jax.random.normal(ks[1], (E, H), jnp.float32) * s, 'W1': jax.random.normal(ks[2], (E, H, F), jnp.float32) * s, 'b1': jnp.zeros((E, F), jnp.float32), 'W2': jax.random.normal(ks[3], (E, F, H), jnp.float32) * s, 'b2': jnp.zeros((E, H), jnp.float32)}
    _L1_ffn_all = _L1_ffn_setup()
    _L1_ffn_in = {k: v for k, v in _L1_ffn_all.items() if k in ('Wg', 'W1', 'b1', 'W2', 'b2')}
    del _L1_ffn_all
    return {'x': x, 'L0_tok_W': _L0_tok_in['W'], 'L0_tok_b': _L0_tok_in['b'], 'L0_attn_w_qkv': _L0_attn_in['w_qkv'], 'L0_attn_w_o': _L0_attn_in['w_o'], 'L0_ffn_W_qkv': _L0_ffn_in['W_qkv'], 'L0_ffn_b_qkv': _L0_ffn_in['b_qkv'], 'L0_ffn_W_gate': _L0_ffn_in['W_gate'], 'L0_ffn_b_gate': _L0_ffn_in['b_gate'], 'L0_ffn_A': _L0_ffn_in['A'], 'L0_ffn_B_lora': _L0_ffn_in['B_lora'], 'L0_ffn_W_proj': _L0_ffn_in['W_proj'], 'L0_ffn_b_proj': _L0_ffn_in['b_proj'], 'L1_attn_qkv_w': _L1_attn_in['qkv_w'], 'L1_attn_out_w': _L1_attn_in['out_w'], 'L1_attn_anchor_q': _L1_attn_in['anchor_q'], 'L1_attn_w_local': _L1_attn_in['w_local'], 'L1_attn_w_stride': _L1_attn_in['w_stride'], 'L1_attn_w_global': _L1_attn_in['w_global'], 'L1_ffn_Wg': _L1_ffn_in['Wg'], 'L1_ffn_W1': _L1_ffn_in['W1'], 'L1_ffn_b1': _L1_ffn_in['b1'], 'L1_ffn_W2': _L1_ffn_in['W2'], 'L1_ffn_b2': _L1_ffn_in['b2']}

def reference(x, L0_tok_W, L0_tok_b, L0_attn_w_qkv, L0_attn_w_o, L0_ffn_W_qkv, L0_ffn_b_qkv, L0_ffn_W_gate, L0_ffn_b_gate, L0_ffn_A, L0_ffn_B_lora, L0_ffn_W_proj, L0_ffn_b_proj, L1_attn_qkv_w, L1_attn_out_w, L1_attn_anchor_q, L1_attn_w_local, L1_attn_w_stride, L1_attn_w_global, L1_ffn_Wg, L1_ffn_W1, L1_ffn_b1, L1_ffn_W2, L1_ffn_b2):
    import jax
    import jax.numpy as jnp

    def _L0_tok_ref(x, W, b):
        import jax, jax.numpy as jnp
        import numpy as np
        MAX_PATCH = 16

        def _create_patches(x, P):
            B, C, H, W = x.shape
            nH, nW = (H // P, W // P)
            x = x.reshape(B, C, nH, P, W).transpose(0, 1, 2, 4, 3)
            x = x.reshape(B, C, nH, nW, P, P).transpose(0, 1, 2, 3, 5, 4)
            x = x.reshape(B, nH * nW, P, P, C)
            x = x.transpose(0, 1, 4, 2, 3).reshape(B, nH * nW * C, P, P)
            return x
        B, C, H, Wd = x.shape
        P = min(H, Wd, MAX_PATCH)
        patches = _create_patches(x, P)
        tokens = patches.reshape(B, -1, P * P * C)
        return jnp.einsum('bsd,ed->bse', tokens, W) + b

    def _L0_attn_ref(x, w_qkv, w_o):
        import jax, jax.numpy as jnp
        import numpy as np
        B, T, D_MODEL = (2, 512, 192)
        N_HEADS = 12
        D_K = D_MODEL // N_HEADS
        MAX_SEQ_LEN = 512

        def _rotary_tables(dim, max_seq_len):
            angular_freq = (1.0 / 10000.0) ** jnp.linspace(0.0, 1.0, dim // 4, dtype=jnp.float32)
            angular_freq = jnp.concatenate([angular_freq, jnp.zeros(dim // 4, dtype=jnp.float32)])
            t = jnp.arange(max_seq_len, dtype=jnp.float32)
            theta = jnp.einsum('i,j->ij', t, angular_freq)
            return (jnp.cos(theta), jnp.sin(theta))

        def _apply_rotary(x, cos, sin):
            h = x.shape[-3]
            c = cos[None, :h, None, :]
            s = sin[None, :h, None, :]
            x1, x2 = jnp.split(x.astype(jnp.float32), 2, axis=-1)
            y1 = x1 * c + x2 * s
            y2 = -x1 * s + x2 * c
            return jnp.concatenate([y1, y2], axis=-1).astype(x.dtype)
        b, t, _ = x.shape
        cos, sin = _rotary_tables(D_K, MAX_SEQ_LEN)
        qkv = (x @ w_qkv).reshape(b, t, 3, N_HEADS, D_K)
        qkv = jnp.transpose(qkv, (2, 0, 3, 1, 4))
        q, k, v = (qkv[0], qkv[1], qkv[2])
        q = _apply_rotary(q, cos, sin)
        k = _apply_rotary(k, cos, sin)
        scores = jnp.einsum('bhqd,bhkd->bhqk', q, k) / jnp.sqrt(jnp.float32(D_K))
        causal = jnp.tril(jnp.ones((t, t), dtype=bool))
        scores = jnp.where(causal[None, None], scores, -jnp.inf)
        attn = jax.nn.softmax(scores, axis=-1)
        out = jnp.einsum('bhqk,bhkd->bhqd', attn, v)
        out = jnp.transpose(out, (0, 2, 1, 3)).reshape(b, t, D_MODEL)
        return out @ w_o

    def _L0_ffn_ref(x, W_qkv, b_qkv, W_gate, b_gate, A, B_lora, W_proj, b_proj):
        import jax, jax.numpy as jnp
        import numpy as np
        B_SZ, S, D = (8, 128, 192)
        H = 12
        N_EXP = 8
        RANK = 16
        ALPHA = 32
        TOP_K = 2
        b, s, d = x.shape
        n_exp, rank = (A.shape[0], A.shape[1])
        scaling = ALPHA / rank
        head_dim = d // H
        scale = head_dim ** (-0.5)
        t = b * s
        x_flat = x.reshape(t, d)
        qkv_base = x @ W_qkv.T + b_qkv
        logits = x_flat @ W_gate.T + b_gate
        router_probs = jax.nn.softmax(logits, axis=-1)
        top_k_weights, top_k_indices = jax.lax.top_k(router_probs, TOP_K)
        a_down = jnp.einsum('td,nrd->tnr', x_flat, A)
        expert_out = jnp.einsum('tnr,nor->tno', a_down, B_lora) * scaling
        dispatch = jnp.zeros((t, n_exp), x.dtype).at[jnp.arange(t)[:, None], top_k_indices].add(top_k_weights)
        sparse_out = jnp.einsum('tno,tn->to', expert_out, dispatch)
        qkv = qkv_base + sparse_out.reshape(b, s, 3 * d)
        qkv = qkv.reshape(b, s, 3, H, head_dim).transpose(2, 0, 3, 1, 4)
        q, k, v = (qkv[0], qkv[1], qkv[2])
        attn = jax.nn.softmax(jnp.einsum('bhqd,bhkd->bhqk', q, k) * scale, axis=-1)
        out = jnp.einsum('bhqk,bhkd->bhqd', attn, v)
        out = out.transpose(0, 2, 1, 3).reshape(b, s, d)
        return out @ W_proj.T + b_proj

    def _L1_attn_ref(x, qkv_w, out_w, anchor_q, w_local, w_stride, w_global):
        import jax, jax.numpy as jnp
        import numpy as np
        N_HEADS = 12
        WINDOW = 12
        STRIDE = 3
        N_ANCHORS = 12
        EPS = 1e-06

        def fmap(x):
            return jax.nn.elu(x) + 1.0

        def _local_band(q, k, v, window):
            B, H, S, D = q.shape
            w = min(window, S)
            half = w // 2
            k_pad = jnp.pad(k, ((0, 0), (0, 0), (half, half), (0, 0)))
            v_pad = jnp.pad(v, ((0, 0), (0, 0), (half, half), (0, 0)))
            q_f = fmap(q)
            k_f = fmap(k_pad)
            idx = jnp.arange(S)[:, None] + jnp.arange(w)[None, :]
            k_unf = k_f[:, :, idx, :]
            v_unf = v_pad[:, :, idx, :]
            qk = jnp.einsum('bhsd,bhswd->bhsw', q_f, k_unf)
            out = jnp.einsum('bhsw,bhswd->bhsd', qk, v_unf)
            norm = jnp.clip(qk.sum(-1, keepdims=True), 1e-06, None)
            return out / norm

        def _stride_band(q, k, v, stride):
            k_s = fmap(k[:, :, ::stride])
            v_s = v[:, :, ::stride]
            q_f = fmap(q)
            kv = jnp.einsum('bhsd,bhse->bhde', k_s, v_s)
            out = jnp.einsum('bhsd,bhde->bhse', q_f, kv)
            k_sum = k_s.sum(axis=2)
            norm = jnp.clip(jnp.einsum('bhsd,bhd->bhs', q_f, k_sum)[..., None], 1e-06, None)
            return out / norm

        def _global_band(q, k, v, anchor_q, n_heads, n_anchors):
            B, H, S, D = q.shape
            aq = anchor_q.reshape(1, n_heads, n_anchors, D)
            aq = jnp.broadcast_to(aq, (B, n_heads, n_anchors, D))
            aq_f = fmap(aq)
            k_f = fmap(k)
            kv = jnp.einsum('bhsd,bhse->bhde', k_f, v)
            anchor_out = jnp.einsum('bhad,bhde->bhae', aq_f, kv)
            k_sum = k_f.sum(axis=2)
            anchor_norm = jnp.clip(jnp.einsum('bhad,bhd->bha', aq_f, k_sum)[..., None], 1e-06, None)
            anchor_out = anchor_out / anchor_norm
            q_f = fmap(q)
            anchor_k = fmap(aq)
            qk = jnp.einsum('bhsd,bhad->bhsa', q_f, anchor_k)
            out = jnp.einsum('bhsa,bhae->bhse', qk, anchor_out)
            qk_sum = jnp.clip(qk.sum(-1, keepdims=True), 1e-06, None)
            return out / qk_sum
        B, S, D = x.shape
        H = N_HEADS
        hd = D // H
        qkv = (x @ qkv_w.T).reshape(B, S, 3, H, hd)
        qkv = jnp.transpose(qkv, (2, 0, 3, 1, 4))
        q, k, v = (qkv[0], qkv[1], qkv[2])
        wn = jax.nn.softmax(jnp.stack([w_local, w_stride, w_global]))
        wl, ws, wg = (wn[0], wn[1], wn[2])
        out_local = _local_band(q, k, v, WINDOW)
        out_stride = _stride_band(q, k, v, STRIDE)
        out_global = _global_band(q, k, v, anchor_q, H, N_ANCHORS)
        out = wl * out_local + ws * out_stride + wg * out_global
        out = jnp.transpose(out, (0, 2, 1, 3)).reshape(B, S, D)
        return out @ out_w.T

    def _L1_ffn_ref(x, Wg, W1, b1, W2, b2):
        import jax, jax.numpy as jnp
        import numpy as np
        B, T, H, F, E = (128, 32, 192, 768, 3)
        scores = jax.nn.softmax(jnp.mean(x, axis=1) @ Wg.T, axis=-1)
        _, idx = jax.lax.top_k(scores, 1)
        sel = idx[:, 0]
        h = jax.nn.gelu(jnp.einsum('bth,ehf->betf', x, W1) + b1[None, :, None, :], approximate=False)
        y = jnp.einsum('betf,efh->beth', h, W2) + b2[None, :, None, :]
        w = scores * jax.nn.one_hot(sel, E, dtype=scores.dtype)
        out = jnp.einsum('beth,be->bth', y, w)
        return out
    h = _L0_tok_ref(x, L0_tok_W, L0_tok_b)
    h = h + _L0_attn_ref(_layernorm(h, axis=-1), L0_attn_w_qkv, L0_attn_w_o)
    h = h + _L0_ffn_ref(_layernorm(h, axis=-1), L0_ffn_W_qkv, L0_ffn_b_qkv, L0_ffn_W_gate, L0_ffn_b_gate, L0_ffn_A, L0_ffn_B_lora, L0_ffn_W_proj, L0_ffn_b_proj)
    h = h + _L1_attn_ref(_layernorm(h, axis=-1), L1_attn_qkv_w, L1_attn_out_w, L1_attn_anchor_q, L1_attn_w_local, L1_attn_w_stride, L1_attn_w_global)
    h = h + _L1_ffn_ref(_layernorm(h, axis=-1), L1_ffn_Wg, L1_ffn_W1, L1_ffn_b1, L1_ffn_W2, L1_ffn_b2)
    return h

_drawn_inputs = setup_inputs


def setup_inputs(seed=0):
    import zlib

    import numpy as np

    out = dict(_drawn_inputs(seed))
    spreads = {'L0_ffn_b_qkv': (0.0, 0.276),
     'L0_ffn_b_gate': (0.0, 0.8),
     'L0_ffn_b_proj': (0.0, 0.1),
     'L1_ffn_b1': (0.0, 0.76),
     'L1_ffn_b2': (0.0, 0.269)}
    factors = {'L0_tok_b': 5.519,
     'L0_attn_w_qkv': 2.729,
     'L0_ffn_W_qkv': 5.966,
     'L0_ffn_W_gate': 8.0,
     'L0_ffn_A': 8.0,
     'L0_ffn_B_lora': 8.0,
     'L1_attn_qkv_w': 3.473,
     'L1_attn_out_w': 3.84,
     'L1_attn_anchor_q': 64.0}
    for name, (base, spread) in spreads.items():
        noise = np.random.default_rng([zlib.crc32(name.encode()), seed]).standard_normal(out[name].shape)
        drawn = base * np.exp(spread * noise) if base else spread * noise
        out[name] = jnp.asarray(drawn.astype(out[name].dtype))
    for name, factor in factors.items():
        out[name] = (out[name] * factor).astype(out[name].dtype)
    return out
```

```python
from contextlib import ExitStack
from collections import namedtuple

import numpy as np
import concourse.bass as bass
from concourse import mybir

F32 = mybir.dt.float32
BF16 = mybir.dt.bfloat16
ALU = mybir.AluOpType
ACT = mybir.ActivationFunctionType
AX = mybir.AxisListType

BATCH, CHANNELS, IMAGE, PATCH = 64, 3, 128, 16
SEQ = (IMAGE // PATCH) ** 2
TOKENS = BATCH * SEQ
D, HEADS = 192, 12
HD = D // HEADS
D_IN = PATCH * PATCH * CHANNELS
KIN = D_IN // 128
TILE = 128
GROUP = 4
GT = GROUP * TILE
STEPS = TOKENS // GT
HALF = D // 2
VAUG = HD + 1
LORA_EXPERTS, RANK, LORA_SCALE = 8, 16, 2.0
GATE = LORA_EXPERTS + LORA_EXPERTS * RANK
WINDOW, STRIDE, ANCHORS = 12, 3, 12
HG = 4
NHG = HEADS // HG
AROWS = HG * ANCHORS
EXPERTS, FF = 3, 768
MF = FF // 128
LN_EPS, NORM_MIN = 1e-5, 1e-6
CHOICE = 11
MASKED = -1e30
BANK = 512

C_ID = 0
C_BAND = C_ID + 128
C_COS = C_BAND + 128
C_SIN = C_COS + 4 * 2 * HEADS
C_STRIDE = C_SIN + 4 * 2 * HEADS
C_PAD = C_STRIDE + 1
C_HEAD = C_PAD + 1
C_TRI = C_HEAD + HG
C_HALFNEG = C_TRI + 64
C_END = C_HALFNEG + 1


def build(nc, a):
    ctx = ExitStack()
    with ctx:
        def sb(name, shape, dt=F32):
            return ctx.enter_context(nc.sbuf_tensor(name, shape, dt))

        def sem(name):
            return ctx.enter_context(nc.semaphore(name))

        def sems(prefix, names):
            return namedtuple(prefix.rstrip("_"), names)(*(sem(prefix + n) for n in names.split()))

        tok_w = sb("tok_w", [128, KIN, D])
        tok_b = sb("tok_b", [128, D])
        cst = sb("cst", [128, C_END])
        causal = sb("causal", [128, NHG * SEQ], BF16)
        identb = sb("identb", [128, 128], BF16)
        qkv_w = [sb(f"qkv_w{i}", [HALF + 1, 2, 3 * D]) for i in range(3)]
        out_w = [sb(f"out_w{i}", [HALF + 1, 2, D]) for i in range(3)]
        gate_w = sb("gate_w", [HALF + 1, 2, GATE])
        lora_up = sb("lora_up", [128, 3 * D])
        anc_k = sb("anc_k", [128, NHG, AROWS])
        anc_b = sb("anc_b", [AROWS, NHG, 128])
        anc_km = sb("anc_km", [128, NHG, AROWS])
        anc_bm = sb("anc_bm", [AROWS, NHG, 128])
        anc_ke = sb("anc_ke", [128, NHG, AROWS])
        anc_be = sb("anc_be", [AROWS, NHG, 128])
        band_w = sb("band_w", [128, 3])
        band_s = sb("band_s", [128, 4])
        w1 = sb("w1", [HALF + 1, 2, EXPERTS, FF])
        w2 = sb("w2", [128, EXPERTS, MF, D])
        b2 = sb("b2", [128, EXPERTS, D])
        top_w = sb("top_w", [HALF, 2, EXPERTS])

        ident = cst[:, C_ID:C_ID + 128]
        band = cst[:, C_BAND:C_BAND + 128]
        cos = cst[0:HALF, C_COS:C_SIN].rearrange("p (u f) -> p u f", f=4)
        sin = cst[0:HALF, C_SIN:C_STRIDE].rearrange("p (u f) -> p u f", f=4)
        stride_rows = cst[:, C_STRIDE:C_STRIDE + 1]
        pad_count = cst[:, C_PAD:C_PAD + 1]
        head_rows = cst[:, C_HEAD:C_HEAD + HG]
        tri = cst[:, C_TRI:C_TRI + 64].rearrange("p (n m) -> p n m", n=8)
        half_neg = cst[:, C_HALFNEG:C_HALFNEG + 1]

        x_t = sb("x_t", [128, KIN, GT])
        h = sb("h", [128, GROUP, D])
        ln = sb("ln", [128, GROUP, D])
        stats = sb("stats", [128, GROUP, 6])
        both = sb("both", [128, GROUP, 2])
        apart = sb("apart", [128, GROUP])
        mean = sb("mean", [128, GROUP])
        within = sb("within", [128, GROUP])
        between = sb("between", [128, GROUP])
        var_eps = sb("var_eps", [128, GROUP])
        rstd = sb("rstd", [128, GROUP])
        ln_t = sb("ln_t", [HALF + 1, 2, GT])
        qk = sb("qk", [128, GROUP, 2 * HEADS, 32])
        arena = sb("arena", [128, 3 * EXPERTS * MF // 3 * GT])
        vals = sb("vals", [128, GROUP, 2, HEADS // 2, VAUG])
        rot_a = sb("rot_a", [HALF, 2 * HEADS, 2, 4])
        rot_b = sb("rot_b", [HALF, 2 * HEADS, 2, 4])
        row_max = sb("row_max", [128, GROUP, HEADS])
        row_inv = sb("row_inv", [128, GROUP, HEADS])
        o = sb("o", [128, GROUP, D])
        o_t = sb("o_t", [HALF + 1, 2, GT])
        gates = sb("gates", [128, GROUP, GATE])
        lgt = sb("lgt", [128, GROUP, 8])
        lgt_m = sb("lgt_m", [128, GROUP])
        lgt_s = sb("lgt_s", [128, GROUP])
        lgt_i = sb("lgt_i", [128, GROUP])
        above = sb("above", [128, GROUP, 8, 8])
        ties = sb("ties", [128, GROUP, 8, 8])
        rank = sb("rank", [128, GROUP, 8])
        picked = sb("picked", [128, GROUP, 8])
        down = sb("down", [128, GROUP, 128])
        down_t = sb("down_t", [128, GROUP, 128])
        vcat = sb("vcat", [128, GROUP, 2, HEADS, VAUG])
        kvb = sb("kvb", [128, GROUP, 2, NHG, 2, HG, VAUG])
        kvc = sb("kvc", [128, GROUP, NHG, 2, VAUG])
        ao = sb("ao", [AROWS, GROUP, 2 * NHG, VAUG])
        ao_n = sb("ao_n", [AROWS, GROUP, 2 * NHG])
        ao_i = sb("ao_i", [AROWS, GROUP, 2 * NHG])
        qf_sum = sb("qf_sum", [128, GROUP, HEADS])
        nrm = sb("nrm", [128, GROUP, 3, HEADS])
        nrm_c = sb("nrm_c", [128, GROUP, 3, HEADS])
        nrm_i = sb("nrm_i", [128, GROUP, 3, HEADS])
        nrm_w = sb("nrm_w", [128, GROUP, 3, HEADS])
        o_glob = sb("o_glob", [128, GROUP, D])
        o_str = sb("o_str", [128, GROUP, D])
        ln_sum = sb("ln_sum", [HALF, 2, GROUP, 2])
        ln_rep = sb("ln_rep", [HALF, 2, GROUP, 2, SEQ])
        tlg = sb("tlg", [128, GROUP, EXPERTS])

        qk_t = arena[:, 0:GROUP * 6 * 128].rearrange("p (g c n) -> p g c n", g=GROUP, c=6)
        late = arena[:, GROUP * 6 * 128:]
        prob = late[:, 0:GROUP * 768].rearrange("p (g n) -> p g n", g=GROUP)
        prob_t = late[:, GROUP * 768:GROUP * 1536].rearrange("p (g c n) -> p g c n", g=GROUP, c=6)
        loc_t = late.rearrange("p (g n) -> p g n", g=GROUP)
        fe = late[:, 0:GROUP * 2 * D].rearrange("p (g n) -> p g n", g=GROUP)
        fr = late[:, GROUP * 2 * D:GROUP * 4 * D].rearrange("p (g n) -> p g n", g=GROUP)
        hid = arena[:, :].rearrange("p (u n) -> p u n", u=EXPERTS * MF)

        ps = [ctx.enter_context(nc.psum_tensor(f"ps{i}", [128, 4 * BANK], F32)) for i in range(2)]

        x_loaded, tok_w_loaded, weights_loaded, mlp_w_loaded, stored = (
            sem(n) for n in "x_loaded tok_w_loaded weights_loaded mlp_w_loaded stored".split())
        setup = sem("setup")
        setup_anchor_exp, setup_anchor_relu = sem("setup_anchor_exp"), sem("setup_anchor_relu")
        rotated = sem("rotated")
        setup_dve, setup_band_exp = sem("setup_dve"), sem("setup_band_exp")
        tok_mm, embedded = sem("tok_mm"), sem("embedded")
        LN = [sems(f"ln{i}_", "stats joined parts eps rstd normed turned copied") for i in range(4)]
        AT = [sems(f"at{i}_", "qkv copied turned turned_copied scores max shifted "
                              "exp probs_turned probs_copied av inv normed") for i in range(2)]
        OUT = [sems(f"out{i}_", "turned copied mm added") for i in range(3)]
        RT = sems("route_", "mm copied chain shifted exp down turned turned_copied")
        LA = sems("la_", "qkv relu copied strided heads turned turned_copied local local_masked kv kvb "
                         "kvc anchors anchor_n anchor_i ao globals gbd out qsum n_loc n_max "
                         "n_inv n_w loc glob str sum1 sum2")
        ML = sems("ml_", "sum rep gate logits chain shifted exp biased acc0 acc1 up gelu outputs down")

        block = ctx.enter_context(nc.Block())
        N_W = 14

        @block.sync
        def _(sp):
            sp.dma_start(x_t[:, :, :], a["x"][0]).then_inc(x_loaded, 16)
            sp.dma_start(tok_w[:, :, :], a["tok_w"]).then_inc(tok_w_loaded, 16)
            sp.dma_start(tok_b[:, :], a["tok_b"]).then_inc(tok_w_loaded, 16)
            sp.dma_start(cst[:, :], a["cst"]).then_inc(weights_loaded, 16)
            for i in range(3):
                sp.dma_start(qkv_w[i][:, :, :], a[f"qkv_w{i}"]).then_inc(weights_loaded, 16)
                sp.dma_start(out_w[i][:, :, :], a[f"out_w{i}"]).then_inc(weights_loaded, 16)
            for dst, src in ((causal[:, :], "causal"), (identb[:, :], "identb"), (gate_w[:, :, :], "gate_w"),
                             (lora_up[:, :], "lora_up"), (anc_k[:, :, :], "anc_k"), (anc_b[:, :, :], "anc_b"),
                             (band_w[:, :], "band_w")):
                sp.dma_start(dst, a[src]).then_inc(weights_loaded, 16)
            for dst, src in ((anc_km[:, :, :], "anc_km"), (anc_bm[:, :, :], "anc_bm"), (top_w[:, :, :], "top_w"),
                             (w1[:, :, :, :], "w1"), (w2[:, :, :, :], "w2"), (b2[:, :, :], "b2")):
                sp.dma_start(dst, a[src]).then_inc(mlp_w_loaded, 16)
            with sp.Fori(0, STEPS - 1) as i:
                done = [sp.snap(i * GROUP + t + 1) for t in range(GROUP)]
                sp.wait_ge(tok_mm, done[GROUP - 1])
                sp.dma_start(x_t[:, :, :], a["x"][bass.ds(i + 1, 1)].rearrange("o p k n -> (o p) k n")).then_inc(x_loaded, 16)
                for t in range(GROUP):
                    sp.wait_ge(ML.down, sp.snap(i * GROUP + t + 2))
                    sp.dma_start(a["out"][bass.ds(i * GROUP + t, 1)].rearrange("o p n -> (o p) n"),
                                 h[:, t, :]).then_inc(stored, 16)
            for t in range(GROUP):
                sp.wait_ge(ML.down, (STEPS - 1) * GROUP + t + 2)
                sp.dma_start(a["out"][(STEPS - 1) * GROUP + t], h[:, t, :]).then_inc(stored, 16)
            sp.wait_ge(stored, 16 * STEPS * GROUP + 16)

        @block.tensor
        def _(pe):
            def bank(t, k, n=BANK):
                return ps[t % 2][:, k * BANK:k * BANK + n]

            def tok(t):
                return slice(t * TILE, (t + 1) * TILE)

            def turn_halves(src, t):
                for c in range(2):
                    mm = pe.transpose(bank(t, 0)[0:HALF, c * TILE:(c + 1) * TILE],
                                      src[:, t, c * HALF:(c + 1) * HALF], ident)
                return mm

            def turn_heads(t):
                for c in range(6):
                    mm = pe.transpose(ps[t % 2][:, c * TILE:(c + 1) * TILE],
                                      qk[:, t, 4 * c:4 * c + 4, :].rearrange("p a b -> p (a b)"), ident)
                return mm

            def norm_turn(s, prev, t, free):
                pe.wait_ge(s.normed, done[t])
                free(t)
                turn_halves(ln, t).then_inc(s.turned, 1)

            def attention(s, heads, o_s, out_wt, causal_mask):
                for t in range(GROUP):
                    pe.wait_ge(heads, done[t])
                    pe.wait_ge(*(s.turned_copied, done[t - 2]) if t >= 2 else (s.copied, done[t + 2]))
                    turn_heads(t).then_inc(s.turned, 1)
                for t in range(GROUP):
                    pe.wait_ge(s.turned_copied, done[t])
                    pe.wait_ge(*(s.shifted, done[t - 2]) if t >= 2 else (s.turned_copied, done[t + 2]))
                    if causal_mask:
                        for j in range(HG):
                            pe.matmul(bank(t, j, NHG * SEQ), identb[:, :], causal[:, :], start=True, stop=False,
                                      skip_group_check=True)
                    for g in range(NHG):
                        for b in range(2):
                            for j in range(HG):
                                r = slice(32 * j, 32 * j + 32)
                                mm = pe.matmul(bank(t, j)[64 * b:64 * b + 64, g * SEQ:(g + 1) * SEQ],
                                               qk_t[r, t, g, b * SEQ:(b + 1) * SEQ],
                                               qk_t[r, t, NHG + g, b * SEQ:(b + 1) * SEQ],
                                               start=not causal_mask, stop=True, skip_group_check=True)
                    mm.then_inc(s.scores, 1)
                for t in range(GROUP):
                    pe.wait_ge(s.exp, done[t])
                    pe.wait_ge(*(s.probs_copied, done[t - 2]) if t >= 2 else (s.shifted, done[t + 2]))
                    for c in range(6):
                        mm = pe.transpose(ps[t % 2][:, c * TILE:(c + 1) * TILE],
                                          prob[:, t, c * TILE:(c + 1) * TILE], ident)
                    mm.then_inc(s.probs_turned, 1)
                for t in range(GROUP):
                    pe.wait_ge(s.probs_copied, done[t])
                    pe.wait_ge(*(s.normed, done[t - 2]) if t >= 2 else (s.probs_copied, done[t + 2]))
                    pe.matmul(bank(t, 0)[:, BANK - 2:BANK], identb[:, :], identb[:, 0:2], start=True, stop=True,
                              skip_group_check=True)
                    for c in range(6):
                        for b in range(2):
                            for e in range(2):
                                r = slice(64 * e, 64 * e + 64)
                                mm = pe.matmul(bank(t, e)[64 * b:64 * b + 64, c * VAUG:(c + 1) * VAUG],
                                               prob_t[r, t, c, b * SEQ:(b + 1) * SEQ], vals[r, t, b, c, :],
                                               start=True, stop=True, skip_group_check=True)
                    mm.then_inc(s.av, 1)
                project(s.normed, o_s, out_wt, HALF + 1)

            def project(o_ready, o_s, out_wt, k_last):
                for t in range(GROUP):
                    pe.wait_ge(o_ready, done[t])
                    pe.wait_ge(*(o_s.copied, done[t - 2]) if t >= 2 else (o_ready, done[t + 2]))
                    turn_halves(o, t).then_inc(o_s.turned, 1)
                for t in range(GROUP):
                    pe.wait_ge(o_s.copied, done[t])
                    pe.wait_ge(*(o_s.added, done[t - 2]) if t >= 2 else (o_s.copied, done[t + 2]))
                    pe.matmul(bank(t, 0, D), o_t[0:HALF, 0, tok(t)], out_wt[0:HALF, 0, :], start=True, stop=False)
                    pe.matmul(bank(t, 0, D), o_t[0:k_last, 1, tok(t)], out_wt[0:k_last, 1, :],
                              start=False, stop=True).then_inc(o_s.mm, 1)

            def norm_stage(s, freed):
                for t in range(GROUP):
                    pe.wait_ge(s.normed, done[t])
                    pe.wait_ge(*(s.copied, done[t - 2]) if t >= 2 else (freed, done[t + 2]))
                    turn_halves(ln, t).then_inc(s.turned, 1)

            def qkv_stage(s, ln_s, w, k_last, lora):
                for t in range(GROUP):
                    pe.wait_ge(*((RT.turned_copied if lora else ln_s.copied), done[t]))
                    pe.wait_ge(*(s.copied, done[t - 2]) if t >= 2
                               else ((RT.turned_copied if lora else ln_s.copied), done[t + 2]))
                    pe.matmul(bank(t, 0, 2 * D), ln_t[0:HALF, 0, tok(t)], w[0:HALF, 0, 0:2 * D],
                              start=True, stop=False)
                    pe.matmul(bank(t, 0, 2 * D), ln_t[0:k_last, 1, tok(t)], w[0:k_last, 1, 0:2 * D],
                              start=False, stop=not lora)
                    if lora:
                        pe.matmul(bank(t, 0, 2 * D), down_t[:, t, :], lora_up[:, 0:2 * D], start=False, stop=True)
                    for b in range(2):
                        for e in range(2):
                            cols = slice(2 * D + e * HALF, 2 * D + (e + 1) * HALF)
                            img = slice(t * TILE + b * SEQ, t * TILE + (b + 1) * SEQ)
                            dst = bank(t, 1)[64 * e:64 * e + 64, b * HALF:(b + 1) * HALF]
                            pe.matmul(dst, ln_t[0:HALF, 0, img], w[0:HALF, 0, cols], start=True, stop=False)
                            mm = pe.matmul(dst, ln_t[0:k_last, 1, img], w[0:k_last, 1, cols],
                                           start=False, stop=not lora)
                            if lora:
                                mm = pe.matmul(dst, down_t[:, t, b * SEQ:(b + 1) * SEQ], lora_up[:, cols],
                                               start=False, stop=True)
                    mm.then_inc(s.qkv, 1)

            pe.wait_ge(tok_w_loaded, 32)
            with pe.Fori(0, STEPS) as i:
                base = pe.snap(i * GROUP + 1)
                done = [pe.snap(i * GROUP + t + 1) for t in range(GROUP)]
                pe.wait_ge(x_loaded, pe.snap(i * 16 + 16))
                for t in range(GROUP):
                    pe.wait_ge(*(embedded, done[t - 2]) if t >= 2 else (ML.down, base))
                    for k in range(KIN):
                        mm = pe.matmul(bank(t, 0, D), x_t[:, k, tok(t)], tok_w[:, k, :],
                                       start=(k == 0), stop=(k == KIN - 1))
                    mm.then_inc(tok_mm, 1)
                pe.wait_ge(weights_loaded, 16 * N_W)
                pe.wait_ge(setup, 6)
                pe.wait_ge(rotated, 4)
                pe.wait_ge(setup_dve, 11)
                norm_stage(LN[0], embedded)
                qkv_stage(AT[0], LN[0], qkv_w[0], HALF, False)
                attention(AT[0], AT[0].copied, OUT[0], out_w[0], True)
                norm_stage(LN[1], OUT[0].added)
                for t in range(GROUP):
                    pe.wait_ge(LN[1].copied, done[t])
                    pe.wait_ge(*(RT.copied, done[t - 2]) if t >= 2 else (LN[1].copied, done[t + 2]))
                    pe.matmul(bank(t, 0, GATE), ln_t[0:HALF, 0, tok(t)], gate_w[0:HALF, 0, :], start=True, stop=False)
                    pe.matmul(bank(t, 0, GATE), ln_t[:, 1, tok(t)], gate_w[:, 1, :],
                              start=False, stop=True).then_inc(RT.mm, 1)
                for t in range(GROUP):
                    pe.wait_ge(RT.down, done[t])
                    pe.wait_ge(*(RT.turned_copied, done[t - 2]) if t >= 2 else (RT.copied, done[t + 2]))
                    pe.transpose(bank(t, 0, TILE), down[:, t, :], ident).then_inc(RT.turned, 1)
                qkv_stage(AT[1], LN[1], qkv_w[1], HALF + 1, True)
                attention(AT[1], AT[1].copied, OUT[1], out_w[1], False)
                norm_stage(LN[2], OUT[1].added)
                w = qkv_w[2]
                for t in range(GROUP):
                    pe.wait_ge(LN[2].copied, done[t])
                    pe.wait_ge(*(LA.copied, done[t - 2]) if t >= 2 else (LN[2].copied, done[t + 2]))
                    for c in range(2):
                        pe.matmul(bank(t, 0, 2 * D), ln_t[0:HALF, c, tok(t)], w[0:HALF, c, 0:2 * D],
                                  start=(c == 0), stop=(c == 1))
                    for c in range(2):
                        mm = pe.matmul(bank(t, 1, D), ln_t[0:HALF, c, tok(t)], w[0:HALF, c, 2 * D:],
                                       start=(c == 0), stop=(c == 1))
                    mm.then_inc(LA.qkv, 1)
                for t in range(GROUP):
                    pe.wait_ge(LA.heads, done[t])
                    pe.wait_ge(*(LA.turned_copied, done[t - 2]) if t >= 2 else (LA.copied, done[t + 2]))
                    turn_heads(t).then_inc(LA.turned, 1)
                for t in range(GROUP):
                    pe.wait_ge(LA.strided, done[t])
                    pe.wait_ge(*(LA.kvb, done[t - 2]) if t >= 2 else (LA.turned_copied, done[t + 2]))
                    for g in range(NHG):
                        for b in range(2):
                            r = slice(64 * b, 64 * b + 64)
                            mm = pe.matmul(bank(t, b)[:, g * 136:(g + 1) * 136],
                                           qk[r, t, HEADS + HG * g:HEADS + HG * (g + 1), :].rearrange("p a b -> p (a b)"),
                                           vcat[r, t, :, HG * g:HG * (g + 1), :].rearrange("p k h v -> p k (h v)"),
                                           start=True, stop=True, skip_group_check=True)
                    mm.then_inc(LA.kv, 1)
                for t in range(GROUP):
                    pe.wait_ge(LA.turned_copied, done[t])
                    pe.wait_ge(*(LA.local_masked, done[t - 2]) if t >= 2 else (LA.kvb, done[t + 2]))
                    for g in range(NHG):
                        for j in range(HG):
                            r = slice(32 * j, 32 * j + 32)
                            mm = pe.matmul(bank(t, j)[:, g * TILE:(g + 1) * TILE], qk_t[r, t, NHG + g, :],
                                           qk_t[r, t, g, :], start=True, stop=True, skip_group_check=True)
                    mm.then_inc(LA.local, 1)
                for t in range(GROUP):
                    pe.wait_ge(LA.kvc, done[t])
                    pe.wait_ge(*(LA.ao, done[t - 2]) if t >= 2 else (LA.local_masked, done[t + 2]))
                    for g in range(NHG):
                        mm = pe.matmul(bank(t, 0)[0:AROWS, g * 34:(g + 1) * 34], anc_k[:, g, :],
                                       kvc[:, t, g, :, :].rearrange("p b v -> p (b v)"),
                                       start=True, stop=True, skip_group_check=True)
                    mm.then_inc(LA.anchors, 1)
                for t in range(GROUP):
                    pe.wait_ge(LA.ao, done[t])
                    pe.wait_ge(*(LA.gbd, done[t - 2]) if t >= 2 else (LA.ao, done[t + 2]))
                    for g in range(NHG):
                        mm = pe.matmul(bank(t, 0)[:, g * 34:(g + 1) * 34], anc_b[:, g, :],
                                       ao[:, t, 2 * g:2 * g + 2, :].rearrange("p b v -> p (b v)"),
                                       start=True, stop=True, skip_group_check=True)
                    mm.then_inc(LA.globals, 1)
                for t in range(GROUP):
                    pe.wait_ge(LA.gbd, done[t])
                    pe.wait_ge(LA.local_masked, done[t])
                    pe.wait_ge(*(LA.str, done[t - 2]) if t >= 2 else (LA.gbd, done[t + 2]))
                    for j in range(HG):
                        for g in range(NHG):
                            hh = HG * g + j
                            pe.matmul(bank(t, 0)[:, hh * VAUG:(hh + 1) * VAUG],
                                      loc_t[:, t, (j * NHG + g) * TILE:(j * NHG + g + 1) * TILE],
                                      vcat[:, t, 0, hh, :], start=True, stop=True, skip_group_check=True)
                    for g in range(NHG):
                        for b in range(2):
                            mm = pe.matmul(bank(t, 1)[64 * b:64 * b + 64, g * 136:(g + 1) * 136],
                                           qk_t[:, t, g, b * SEQ:(b + 1) * SEQ],
                                           kvb[:, t, b, g, :, :, :].rearrange("p k h v -> p (k h v)"),
                                           start=True, stop=True, skip_group_check=True)
                    mm.then_inc(LA.out, 1)
                project(LA.sum2, OUT[2], out_w[2], HALF)
                pe.wait_ge(mlp_w_loaded, 16 * 6)
                norm_stage(LN[3], OUT[2].added)
                for t in range(GROUP):
                    pe.wait_ge(ML.rep, done[t])
                    pe.wait_ge(*(ML.logits, done[t - 2]) if t >= 2 else (LN[3].copied, done[t + 2]))
                    for c in range(2):
                        mm = pe.matmul(bank(t, 0, EXPERTS), ln_rep[:, c, t, :, :].rearrange("p b s -> p (b s)"),
                                       top_w[:, c, :], start=(c == 0), stop=(c == 1))
                    mm.then_inc(ML.gate, 1)
                units = pe.snap(i * (EXPERTS * MF))
                for u in range(EXPERTS * MF):
                    e, m = u // MF, u % MF
                    if u >= 2:
                        pe.wait_ge(ML.gelu, units + (u - 1))
                    else:
                        pe.wait_ge(ML.logits, done[u + 2])
                    cols = slice(m * 128, (m + 1) * 128)
                    pe.matmul(bank(u, 0), w1[0:HALF, 0, e, cols], ln_t[0:HALF, 0, :], start=True, stop=False)
                    pe.matmul(bank(u, 0), w1[:, 1, e, cols], ln_t[:, 1, :], start=False, stop=True).then_inc(ML.up, 1)
                pe.wait_ge(ML.gelu, units + EXPERTS * MF)
                for t in range(GROUP):
                    if t >= 2:
                        pe.wait_ge(ML.down, pe.snap(i * GROUP + t))
                    for e in range(EXPERTS):
                        for m in range(MF):
                            mm = pe.matmul(bank(t, e, D), hid[:, e * MF + m, tok(t)], w2[:, e, m, :],
                                           start=(m == 0), stop=(m == MF - 1))
                    mm.then_inc(ML.outputs, 1)

        @block.scalar
        def _(act):
            def bank(t, k, n=BANK):
                return ps[t % 2][:, k * BANK:k * BANK + n]

            def tok(t):
                return slice(t * TILE, (t + 1) * TILE)

            def copy_halves(dst, turned, copied):
                for t in range(GROUP):
                    act.wait_ge(turned, done[t])
                    act.activation(dst[0:HALF, :, tok(t)],
                                   bank(t, 0)[0:HALF, 0:2 * TILE].rearrange("p (c n) -> p c n", c=2),
                                   ACT.Copy).then_inc(copied, 1)

            def copy_wide(dst, turned, copied):
                for t in range(GROUP):
                    act.wait_ge(turned, done[t])
                    act.activation(dst[:, t, :, :].rearrange("p c n -> p (c n)"), ps[t % 2][:, 0:6 * TILE],
                                   ACT.Copy).then_inc(copied, 1)

            def attention(s, ln_s):
                for t in range(GROUP):
                    act.wait_ge(s.qkv, done[t])
                    act.activation(qk[:, t, :, 0:HD], bank(t, 0, 2 * D).rearrange("p (u f) -> p u f", f=HD), ACT.Copy)
                    act.activation(vals[:, t, :, :, 0:HD],
                                   bank(t, 1, D).rearrange("p (b c f) -> p b c f", b=2, c=HEADS // 2),
                                   ACT.Copy).then_inc(s.copied, 1)
                copy_wide(qk_t, s.turned, s.turned_copied)
                for t in range(GROUP):
                    act.wait_ge(s.shifted, done[t])
                    act.activation(prob[:, t, :], prob[:, t, :], ACT.Exp, scale=HD ** -0.5).then_inc(s.exp, 1)
                copy_wide(prob_t, s.probs_turned, s.probs_copied)

            act.wait_ge(weights_loaded, 16 * N_W)
            act.activation(anc_ke[:, :, :], anc_k[:, :, :], ACT.Exp).then_inc(setup_anchor_exp, 1)
            act.activation(anc_be[:, :, :], anc_b[:, :, :], ACT.Exp).then_inc(setup_anchor_exp, 1)
            act.wait_ge(setup_dve, 2)
            act.activation(band_w[:, :], band_w[:, :], ACT.Exp).then_inc(setup_band_exp, 1)
            act.wait_ge(setup, 6)
            with act.Fori(0, STEPS) as i:
                done = [act.snap(i * GROUP + t + 1) for t in range(GROUP)]
                copy_halves(ln_t, LN[0].turned, LN[0].copied)
                attention(AT[0], LN[0])
                copy_halves(o_t, OUT[0].turned, OUT[0].copied)
                copy_halves(ln_t, LN[1].turned, LN[1].copied)
                for t in range(GROUP):
                    act.wait_ge(RT.mm, done[t])
                    act.activation(gates[:, t, :], bank(t, 0, GATE), ACT.Copy).then_inc(RT.copied, 1)
                act.wait_ge(RT.shifted, done[GROUP - 1])
                act.activation(lgt[:, :, :], lgt[:, :, :], ACT.Exp).then_inc(RT.exp, GROUP)
                for t in range(GROUP):
                    act.wait_ge(RT.turned, done[t])
                    act.activation(down_t[:, t, :], bank(t, 0, TILE), ACT.Copy).then_inc(RT.turned_copied, 1)
                attention(AT[1], LN[1])
                copy_halves(o_t, OUT[1].turned, OUT[1].copied)
                copy_halves(ln_t, LN[2].turned, LN[2].copied)
                for t in range(GROUP):
                    act.wait_ge(LA.qkv, done[t])
                    act.activation(fe[:, t, :], bank(t, 0, 2 * D), ACT.Exp)
                    act.activation(fr[:, t, :], bank(t, 0, 2 * D), ACT.Relu).then_inc(LA.relu, 1)
                    act.activation(vcat[:, t, 0, :, 0:HD], bank(t, 1, D).rearrange("p (u f) -> p u f", f=HD),
                                   ACT.Copy).then_inc(LA.copied, 1)
                copy_wide(qk_t, LA.turned, LA.turned_copied)
                copy_halves(o_t, OUT[2].turned, OUT[2].copied)
                copy_halves(ln_t, LN[3].turned, LN[3].copied)
                for t in range(GROUP):
                    act.wait_ge(ML.gate, done[t])
                    act.activation(tlg[:, t, :], bank(t, 0, EXPERTS), ACT.Copy, scale=1.0 / SEQ).then_inc(ML.logits, 1)
                act.wait_ge(ML.shifted, done[GROUP - 1])
                act.activation(lgt[:, :, 0:EXPERTS], lgt[:, :, 0:EXPERTS], ACT.Exp).then_inc(ML.exp, GROUP)
                units = act.snap(i * (EXPERTS * MF))
                for u in range(EXPERTS * MF):
                    act.wait_ge(ML.up, units + (u + 1))
                    act.activation(hid[:, u, :], bank(u, 0), ACT.Gelu).then_inc(ML.gelu, 1)

        @block.gpsimd
        def _(pool):
            margins = ((ln_t[HALF:HALF + 1, :, :], 1.0), (o_t[HALF:HALF + 1, :, :], 1.0), (qk[:, :, :, HD:32], 0.0),
                       (vals[:, :, :, :, HD:VAUG], 1.0), (vcat[:, :, 0, :, HD:VAUG], 1.0), (ao[:, :, :, HD:VAUG], 1.0))
            for n, (margin, value) in enumerate(margins):
                if n:
                    pool.wait_ge(setup, n)
                pool.memset(margin, value).then_inc(setup, 1)
            pool.wait_ge(weights_loaded, 16 * N_W)
            pool.wait_ge(setup, 6)

            def root(s):
                pool.wait_ge(s.eps, done[GROUP - 1])
                pool.tensor_tensor(rstd[:, :], var_eps[:, :], half_neg.to_broadcast([128, GROUP]),
                                   ALU.pow).then_inc(s.rstd, GROUP)

            with pool.Fori(0, STEPS) as i:
                done = [pool.snap(i * GROUP + t + 1) for t in range(GROUP)]
                root(LN[0])
                root(LN[1])
                root(LN[2])
                for t in range(GROUP):
                    pool.wait_ge(LA.copied, done[t])
                    pool.tensor_tensor(vcat[:, t, 1, :, :].rearrange("p h v -> p (h v)"),
                                       vcat[:, t, 0, :, :].rearrange("p h v -> p (h v)"),
                                       stride_rows.to_broadcast([128, HEADS * VAUG]), ALU.mult).then_inc(LA.strided, 1)
                root(LN[3])

        @block.vector
        def _(dve):
            def bank(t, k, n=BANK):
                return ps[t % 2][:, k * BANK:k * BANK + n]

            def all_tiles():
                return range(GROUP)

            def layer_norm(s, h_ready):
                for t in all_tiles():
                    dve.wait_ge(h_ready, done[t])
                    dve.bn_stats(stats[:, t, :], h[:, t, :]).then_inc(s.stats, 1)
                dve.wait_ge(s.stats, done[GROUP - 1])
                dve.tensor_tensor(both[:, :, :], stats[:, :, 1:3], stats[:, :, 4:6], ALU.add)
                dve.tensor_tensor(apart[:, :], stats[:, :, 1], stats[:, :, 4], ALU.subtract).then_inc(s.joined, GROUP)
                dve.wait_ge(s.joined, done[GROUP - 1])
                dve.tensor_scalar(mean[:, :], both[:, :, 0], 0.5, None, ALU.mult)
                dve.tensor_scalar(within[:, :], both[:, :, 1], 1.0 / D, LN_EPS, ALU.mult, ALU.add)
                dve.scalar_tensor_tensor(out=between[:, :], in0=apart[:, :], scalar=0.25, in1=apart[:, :],
                                         op0=ALU.mult, op1=ALU.mult).then_inc(s.parts, GROUP)
                dve.wait_ge(s.parts, done[GROUP - 1])
                dve.tensor_tensor(var_eps[:, :], within[:, :], between[:, :], ALU.add).then_inc(s.eps, GROUP)
                for t in all_tiles():
                    dve.wait_ge(s.rstd, done[t])
                    dve.tensor_scalar(ln[:, t, :], h[:, t, :], mean[:, t:t + 1], rstd[:, t:t + 1],
                                      ALU.subtract, ALU.mult).then_inc(s.normed, 1)

            def attention(s):
                for t in all_tiles():
                    scores = ps[t % 2][:, :].rearrange("p (j n) -> p j n", j=HG)[:, :, 0:NHG * SEQ]\
                        .rearrange("p j (g k) -> p j g k", g=NHG)
                    dve.wait_ge(s.scores, done[t])
                    dve.tensor_reduce(row_max[:, t, :].rearrange("p (j g) -> p j g", j=HG), scores, AX.X,
                                      ALU.max).then_inc(s.max, 1)
                    dve.wait_ge(s.max, done[t])
                    dve.tensor_tensor(prob[:, t, :].rearrange("p (j g k) -> p j g k", j=HG, g=NHG), scores,
                                      row_max[:, t, :].rearrange("p (j g) -> p j g", j=HG).unsqueeze(3)
                                      .to_broadcast([128, HG, NHG, SEQ]), ALU.subtract).then_inc(s.shifted, 1)
                for t in all_tiles():
                    av = ps[t % 2][:, 0:2 * BANK].rearrange("p (e n) -> p e n", e=2)[:, :, 0:6 * VAUG]\
                        .rearrange("p e (c v) -> p e c v", v=VAUG)
                    inv = row_inv[:, t, :].rearrange("p (e c) -> p e c", e=2)
                    dve.wait_ge(s.av, done[t])
                    dve.reciprocal(inv, av[:, :, :, HD]).then_inc(s.inv, 1)
                    dve.wait_ge(s.inv, done[t])
                    dve.tensor_tensor(o[:, t, :].rearrange("p (e c f) -> p e c f", e=2, c=6), av[:, :, :, 0:HD],
                                      inv.unsqueeze(3).to_broadcast([128, 2, 6, HD]), ALU.mult).then_inc(s.normed, 1)

            def add_out(o_s):
                for t in all_tiles():
                    dve.wait_ge(o_s.mm, done[t])
                    dve.tensor_tensor(h[:, t, :], bank(t, 0, D), h[:, t, :], ALU.add).then_inc(o_s.added, 1)

            def choose(logits, n, keep, factor, s):
                cells = [128, GROUP, n, n]
                lower = tri[:, 0:n, 0:n].unsqueeze(1).to_broadcast(cells)
                rivals = logits.unsqueeze(2).to_broadcast(cells)
                own = logits.unsqueeze(3).to_broadcast(cells)
                at = dve.snap(i * CHOICE)
                n8 = slice(0, n)
                dve.tensor_reduce(lgt_m[:, :], logits, AX.X, ALU.max).then_inc(s.chain, 1)
                dve.tensor_tensor(above[:, :, n8, n8], rivals, own, ALU.is_gt).then_inc(s.chain, 1)
                dve.tensor_tensor(ties[:, :, n8, n8], rivals, own, ALU.is_equal).then_inc(s.chain, 1)
                dve.wait_ge(s.chain, at + 1)
                dve.tensor_tensor(lgt[:, :, n8], logits, lgt_m[:, :].unsqueeze(2).to_broadcast([128, GROUP, n]),
                                  ALU.subtract).then_inc(s.shifted, GROUP)
                dve.wait_ge(s.chain, at + 3)
                dve.tensor_tensor(ties[:, :, n8, n8], ties[:, :, n8, n8], lower, ALU.mult).then_inc(s.chain, 1)
                dve.wait_ge(s.chain, at + 4)
                dve.tensor_tensor(above[:, :, n8, n8], above[:, :, n8, n8], ties[:, :, n8, n8],
                                  ALU.add).then_inc(s.chain, 1)
                dve.wait_ge(s.chain, at + 5)
                dve.tensor_reduce(rank[:, :, n8], above[:, :, n8, n8], AX.X, ALU.add).then_inc(s.chain, 1)
                dve.wait_ge(s.chain, at + 6)
                dve.tensor_scalar(picked[:, :, n8], rank[:, :, n8], keep - 0.5, factor, ALU.is_lt,
                                  ALU.mult).then_inc(s.chain, 1)
                dve.wait_ge(s.exp, done[GROUP - 1])
                dve.tensor_reduce(lgt_s[:, :], lgt[:, :, n8], AX.X, ALU.add).then_inc(s.chain, 1)
                dve.wait_ge(s.chain, at + 7)
                dve.tensor_tensor(picked[:, :, n8], picked[:, :, n8], lgt[:, :, n8], ALU.mult).then_inc(s.chain, 1)
                dve.wait_ge(s.chain, at + 8)
                dve.reciprocal(lgt_i[:, :], lgt_s[:, :]).then_inc(s.chain, 1)
                dve.wait_ge(s.chain, at + 10)
                dve.tensor_tensor(picked[:, :, n8], picked[:, :, n8],
                                  lgt_i[:, :].unsqueeze(2).to_broadcast([128, GROUP, n]), ALU.mult)\
                    .then_inc(s.chain, 1)
                dve.wait_ge(s.chain, at + 11)

            dve.wait_ge(weights_loaded, 16 * N_W)
            for c in range(2):
                pair = qkv_w[0][0:HALF, c, 0:2 * D].rearrange("p (u s f) -> p u s f", s=2, f=HD // 2)[:, :, :, 0:4]
                if c:
                    dve.wait_ge(rotated, 2 * c)
                dve.tensor_tensor(rot_b[:, :, 0, :], pair[:, :, 1, :], sin, ALU.mult)
                dve.tensor_tensor(rot_b[:, :, 1, :], pair[:, :, 0, :], sin, ALU.mult)
                dve.tensor_tensor(rot_a[:, :, 0, :], pair[:, :, 0, :], cos, ALU.mult)
                dve.tensor_tensor(rot_a[:, :, 1, :], pair[:, :, 1, :], cos, ALU.mult).then_inc(rotated, 1)
                dve.wait_ge(rotated, 2 * c + 1)
                dve.tensor_tensor(pair[:, :, 0, :], rot_a[:, :, 0, :], rot_b[:, :, 0, :], ALU.add)
                dve.tensor_tensor(pair[:, :, 1, :], rot_a[:, :, 1, :], rot_b[:, :, 1, :],
                                  ALU.subtract).then_inc(rotated, 1)
            dve.wait_ge(weights_loaded, 16 * N_W)
            dve.wait_ge(mlp_w_loaded, 16 * 6)
            dve.tensor_reduce(band_s[:, 0:1], band_w[:, :], AX.X, ALU.max).then_inc(setup_dve, 1)
            dve.wait_ge(setup_dve, 1)
            dve.tensor_scalar(band_w[:, :], band_w[:, :], band_s[:, 0:1], None, ALU.subtract).then_inc(setup_dve, 1)
            dve.wait_ge(setup_anchor_exp, 2)
            for x, e, m in ((anc_k, anc_ke, anc_km), (anc_b, anc_be, anc_bm)):
                n = 3 if x is anc_k else 6
                dve.tensor_scalar(e[:, :, :], e[:, :, :], 1.0, None, ALU.min).then_inc(setup_dve, 1)
                dve.wait_ge(setup_dve, n)
                dve.scalar_tensor_tensor(out=x[:, :, :], in0=x[:, :, :], scalar=0.0, in1=e[:, :, :],
                                         op0=ALU.max, op1=ALU.add).then_inc(setup_dve, 1)
                dve.wait_ge(setup_dve, n + 1)
                dve.tensor_tensor(x[:, :, :], x[:, :, :], m[:, :, :], ALU.mult).then_inc(setup_dve, 1)
            dve.wait_ge(setup_band_exp, 1)
            dve.tensor_reduce(band_s[:, 1:2], band_w[:, :], AX.X, ALU.add).then_inc(setup_dve, 1)
            dve.wait_ge(setup_dve, 9)
            dve.reciprocal(band_s[:, 2:3], band_s[:, 1:2]).then_inc(setup_dve, 1)
            dve.wait_ge(setup_dve, 10)
            dve.tensor_scalar(band_w[:, :], band_w[:, :], band_s[:, 2:3], None, ALU.mult).then_inc(setup_dve, 1)
            dve.wait_ge(setup_dve, 11)
            dve.memset(band_s[:, 3:4], 0.0).then_inc(ML.down, 1)
            dve.memset(band_s[:, 0:1], 0.0).then_inc(stored, 16)
            dve.wait_ge(setup, 6)
            dve.wait_ge(tok_w_loaded, 32)

            with dve.Fori(0, STEPS) as i:
                done = [dve.snap(i * GROUP + t + 1) for t in range(GROUP)]
                dve.wait_ge(stored, dve.snap(i * (16 * GROUP) + 16))
                for t in all_tiles():
                    dve.wait_ge(tok_mm, done[t])
                    dve.tensor_tensor(h[:, t, :], bank(t, 0, D), tok_b[:, :], ALU.add).then_inc(embedded, 1)
                layer_norm(LN[0], embedded)
                attention(AT[0])
                add_out(OUT[0])
                layer_norm(LN[1], OUT[0].added)
                dve.wait_ge(RT.copied, done[GROUP - 1])
                choose(gates[:, :, 0:LORA_EXPERTS], LORA_EXPERTS, 2, LORA_SCALE, RT)
                for t in all_tiles():
                    dve.tensor_tensor(down[:, t, :].rearrange("p (n r) -> p n r", r=RANK),
                                      gates[:, t, LORA_EXPERTS:].rearrange("p (n r) -> p n r", r=RANK),
                                      picked[:, t, :].unsqueeze(2).to_broadcast([128, LORA_EXPERTS, RANK]),
                                      ALU.mult).then_inc(RT.down, 1)
                attention(AT[1])
                add_out(OUT[1])
                layer_norm(LN[2], OUT[1].added)
                for t in all_tiles():
                    dve.wait_ge(LA.relu, done[t])
                    dve.scalar_tensor_tensor(out=qk[:, t, :, 0:HD], in0=fe[:, t, :].rearrange("p (u f) -> p u f", f=HD),
                                             scalar=1.0, in1=fr[:, t, :].rearrange("p (u f) -> p u f", f=HD),
                                             op0=ALU.min, op1=ALU.add).then_inc(LA.heads, 1)
                for t in all_tiles():
                    dve.wait_ge(LA.heads, done[t])
                    dve.tensor_reduce(qf_sum[:, t, :], qk[:, t, 0:HEADS, 0:HD], AX.X, ALU.add).then_inc(LA.qsum, 1)
                for t in all_tiles():
                    dve.wait_ge(LA.kv, done[t])
                    for b in range(2):
                        op = dve.tensor_tensor(
                            kvb[:, t, b, :, :, :, :].rearrange("p g k h v -> p (g k) h v"),
                            bank(t, b, 408).rearrange("p (g h v) -> p g h v", h=HG, v=VAUG),
                            head_rows.unsqueeze(1).unsqueeze(3).to_broadcast([128, 2 * NHG, HG, VAUG]), ALU.mult)
                    op.then_inc(LA.kvb, 1)
                for t in all_tiles():
                    dve.wait_ge(LA.kvb, done[t])
                    for b in range(2):
                        op = dve.tensor_reduce(kvc[:, t, :, b, :],
                                               kvb[:, t, b, :, 0, :, :].rearrange("p g h v -> p g v h"), AX.X, ALU.add)
                    op.then_inc(LA.kvc, 1)
                for t in all_tiles():
                    dve.wait_ge(LA.local, done[t])
                    dve.tensor_tensor(loc_t[:, t, :].rearrange("p (j g n) -> p j g n", j=HG, g=NHG),
                                      ps[t % 2][:, :].rearrange("p (j n) -> p j n", j=HG)[:, :, 0:NHG * TILE]
                                      .rearrange("p j (g n) -> p j g n", g=NHG),
                                      band.unsqueeze(1).unsqueeze(1).to_broadcast([128, HG, NHG, TILE]),
                                      ALU.mult).then_inc(LA.local_masked, 1)
                for t in all_tiles():
                    anc = bank(t, 0)[0:AROWS, 0:2 * NHG * VAUG].rearrange("p (u v) -> p u v", v=VAUG)
                    dve.wait_ge(LA.anchors, done[t])
                    dve.tensor_scalar(ao_n[:, t, :], anc[:, :, HD], NORM_MIN, None, ALU.max).then_inc(LA.anchor_n, 1)
                    dve.wait_ge(LA.anchor_n, done[t])
                    dve.reciprocal(ao_i[:, t, :], ao_n[:, t, :]).then_inc(LA.anchor_i, 1)
                    dve.wait_ge(LA.anchor_i, done[t])
                    dve.tensor_tensor(ao[:, t, :, 0:HD], anc[:, :, 0:HD],
                                      ao_i[:, t, :].unsqueeze(2).to_broadcast([AROWS, 2 * NHG, HD]),
                                      ALU.mult).then_inc(LA.ao, 1)
                for t in all_tiles():
                    dve.wait_ge(LA.globals, done[t])
                    dve.wait_ge(LA.kvc, done[t])
                    for b in range(2):
                        op = dve.tensor_tensor(
                            kvb[:, t, b, :, 0, :, :],
                            bank(t, 0, 2 * NHG * VAUG).rearrange("p (g b v) -> p g b v", b=2, v=VAUG)[:, :, b, :]
                            .unsqueeze(2).to_broadcast([128, NHG, HG, VAUG]),
                            head_rows.unsqueeze(1).unsqueeze(3).to_broadcast([128, NHG, HG, VAUG]), ALU.mult)
                    op.then_inc(LA.gbd, 1)
                for t in all_tiles():
                    loc = bank(t, 0, HEADS * VAUG).rearrange("p (h v) -> p h v", v=VAUG)
                    lin = bank(t, 1, 2 * HEADS * VAUG).rearrange("p (g k h v) -> p g k h v", k=2, h=HG, v=VAUG)
                    dve.wait_ge(LA.out, done[t])
                    dve.wait_ge(LA.qsum, done[t])
                    for k in range(2):
                        dve.tensor_scalar(nrm_c[:, t, 1 + k, :].rearrange("p (g h) -> p g h", h=HG),
                                          lin[:, :, k, :, HD], NORM_MIN, None, ALU.max)
                    dve.scalar_tensor_tensor(out=nrm[:, t, 0, :], in0=qf_sum[:, t, :], scalar=pad_count,
                                             in1=loc[:, :, HD], op0=ALU.mult, op1=ALU.add).then_inc(LA.n_loc, 1)
                    dve.wait_ge(LA.n_loc, done[t])
                    dve.tensor_scalar(nrm_c[:, t, 0, :], nrm[:, t, 0, :], NORM_MIN, None, ALU.max).then_inc(LA.n_max, 1)
                    dve.wait_ge(LA.n_max, done[t])
                    dve.reciprocal(nrm_i[:, t, :, :], nrm_c[:, t, :, :]).then_inc(LA.n_inv, 1)
                    dve.wait_ge(LA.n_inv, done[t])
                    dve.tensor_tensor(nrm_w[:, t, :, :], nrm_i[:, t, :, :],
                                      band_w[:, :].unsqueeze(2).to_broadcast([128, 3, HEADS]), ALU.mult).then_inc(LA.n_w, 1)
                    dve.wait_ge(LA.n_w, done[t])

                    def weigh(dst, src, k, s):
                        dve.tensor_tensor(dst, src, nrm_w[:, t, k, :].unsqueeze(2).to_broadcast([128, HEADS, HD])
                                          if k == 0 else nrm_w[:, t, k, :].rearrange("p (g h) -> p g h", h=HG)
                                          .unsqueeze(3).to_broadcast([128, NHG, HG, HD]), ALU.mult).then_inc(s, 1)

                    weigh(o[:, t, :].rearrange("p (h f) -> p h f", f=HD), loc[:, :, 0:HD], 0, LA.loc)
                    weigh(o_glob[:, t, :].rearrange("p (g h f) -> p g h f", h=HG, f=HD), lin[:, :, 0, :, 0:HD], 1, LA.glob)
                    weigh(o_str[:, t, :].rearrange("p (g h f) -> p g h f", h=HG, f=HD), lin[:, :, 1, :, 0:HD], 2, LA.str)
                    dve.wait_ge(LA.glob, done[t])
                    dve.tensor_tensor(o[:, t, :], o[:, t, :], o_glob[:, t, :], ALU.add).then_inc(LA.sum1, 1)
                    dve.wait_ge(LA.str, done[t])
                    dve.wait_ge(LA.sum1, done[t])
                    dve.tensor_tensor(o[:, t, :], o[:, t, :], o_str[:, t, :], ALU.add).then_inc(LA.sum2, 1)
                add_out(OUT[2])
                layer_norm(LN[3], OUT[2].added)
                for t in all_tiles():
                    dve.wait_ge(LN[3].copied, done[t])
                    dve.tensor_reduce(ln_sum[:, :, t, :], ln_t[0:HALF, :, t * TILE:(t + 1) * TILE]
                                      .rearrange("p c (b s) -> p c b s", b=2), AX.X, ALU.add).then_inc(ML.sum, 1)
                    dve.wait_ge(ML.sum, done[t])
                    dve.tensor_copy(ln_rep[:, :, t, :, :], ln_sum[:, :, t, :].unsqueeze(3).to_broadcast([HALF, 2, 2, SEQ]))\
                        .then_inc(ML.rep, 1)
                dve.wait_ge(ML.logits, done[GROUP - 1])
                choose(tlg[:, :, :], EXPERTS, 1, 1.0, ML)
                biases = dve.snap(i * (EXPERTS * GROUP))
                for e in range(EXPERTS):
                    for t in all_tiles():
                        if e:
                            dve.wait_ge(ML.biased, biases + ((e - 1) * GROUP + t + 1))
                        dve.scalar_tensor_tensor(out=h[:, t, :], in0=b2[:, e, :], scalar=picked[:, t, e:e + 1],
                                                 in1=h[:, t, :], op0=ALU.mult, op1=ALU.add).then_inc(ML.biased, 1)
                for t in all_tiles():
                    dve.wait_ge(ML.outputs, done[t])
                    dve.wait_ge(ML.biased, biases + ((EXPERTS - 1) * GROUP + t + 1))
                    for e in range(EXPERTS):
                        if e:
                            dve.wait_ge((ML.acc0, ML.acc1)[e - 1], done[t])
                        dve.scalar_tensor_tensor(out=h[:, t, :], in0=bank(t, e, D), scalar=picked[:, t, e:e + 1],
                                                 in1=h[:, t, :], op0=ALU.mult, op1=ALU.add)\
                            .then_inc((ML.acc0, ML.acc1, ML.down)[e], 1)


def kernel(**inp):
    import ml_dtypes
    import concourse.bacc as bacc
    from concourse.bass_utils import run_bass_kernel_spmd

    f = {k: np.asarray(v) for k, v in inp.items()}
    one = np.float32

    x = f["x"].reshape(BATCH, CHANNELS, 8, PATCH, 8, PATCH).transpose(0, 1, 2, 4, 3, 5).reshape(TOKENS, D_IN)
    x = np.ascontiguousarray(x.reshape(STEPS, GT, KIN, 128).transpose(0, 3, 2, 1))
    tok_w = f["L0_tok_W"].reshape(D, CHANNELS, 256).transpose(2, 1, 0).reshape(KIN, 128, D).transpose(1, 0, 2)

    def halves(w, bias=None):
        out = np.zeros((HALF + 1, 2, w.shape[1]), one)
        out[0:HALF, 0], out[0:HALF, 1] = w[0:HALF], w[HALF:]
        if bias is not None:
            out[HALF, 1] = bias
        return out

    def by_head(w):
        return w.reshape(w.shape[0], 3, HEADS, HD)

    place = [NHG * (u % HG) + u // HG for u in range(HEADS)]
    pairs = [2 * c + e for e in range(2) for c in range(HEADS // 2)]

    def softmax_columns(w):
        b = by_head(w)
        return np.concatenate([b[:, 0][:, place], b[:, 1][:, place], b[:, 2][:, pairs]], 1).reshape(w.shape[0], 3 * D)

    def pair_rows(w):
        return w.reshape(HEADS, HD, D)[pairs].reshape(D, D)

    lora_up = f["L0_ffn_B_lora"].transpose(0, 2, 1).reshape(128, 3 * D)
    gate = np.concatenate([f["L0_ffn_W_gate"].T, f["L0_ffn_A"].reshape(128, D).T], 1)
    gate_b = np.concatenate([f["L0_ffn_b_gate"], np.zeros(128, one)])
    aq = f["L1_attn_anchor_q"].reshape(HEADS, ANCHORS, HD)
    anc_k = np.zeros((128, NHG, AROWS), one)
    anc_km = np.zeros_like(anc_k)
    for g in range(NHG):
        for j in range(HG):
            anc_k[32 * j:32 * j + HD, g, j * ANCHORS:(j + 1) * ANCHORS] = aq[HG * g + j].T
            anc_km[32 * j:32 * j + HD, g, j * ANCHORS:(j + 1) * ANCHORS] = 1.0
    w1 = np.zeros((HALF + 1, 2, EXPERTS, FF), one)
    w1[0:HALF] = f["L1_ffn_W1"].reshape(EXPERTS, 2, HALF, FF).transpose(2, 1, 0, 3)
    w1[HALF, 1] = f["L1_ffn_b1"]

    pos = np.arange(128) % SEQ
    img = np.arange(128) // SEQ
    freq = (1.0 / 10000.0) ** np.linspace(0.0, 1.0, HD // 4, dtype=one)
    theta = (np.array(place + place, one)[:, None] * freq[None, :]).astype(one).reshape(-1)
    cst = np.zeros((128, C_END), one)
    cst[:, C_ID:C_ID + 128] = np.eye(128)
    off = pos[:, None] - pos[None, :]
    cst[:, C_BAND:C_BAND + 128] = (off >= -(WINDOW // 2)) & (off < WINDOW - WINDOW // 2) & (img[:, None] == img[None, :])
    cst[:, C_COS:C_SIN], cst[:, C_SIN:C_STRIDE] = np.cos(theta), np.sin(theta)
    cst[:, C_STRIDE] = pos % STRIDE == 0
    cst[:, C_PAD] = np.maximum(WINDOW // 2 - pos, 0) + np.maximum(pos + WINDOW - WINDOW // 2 - SEQ, 0)
    cst[:, C_HEAD:C_HEAD + HG] = np.arange(128)[:, None] // 32 == np.arange(HG)[None, :]
    cst[:, C_TRI:C_TRI + 64] = (np.arange(8)[None, :] < np.arange(8)[:, None]).reshape(64)
    cst[:, C_HALFNEG] = -0.5
    causal = np.where(np.arange(SEQ)[None, :] > pos[:, None], MASKED, 0.0)

    arrays = {
        "x": x, "tok_w": tok_w, "tok_b": np.broadcast_to(f["L0_tok_b"], (128, D)), "cst": cst,
        "qkv_w0": halves(softmax_columns(f["L0_attn_w_qkv"])),
        "qkv_w1": halves(softmax_columns(f["L0_ffn_W_qkv"].T), softmax_columns(f["L0_ffn_b_qkv"][None])[0]),
        "qkv_w2": halves(f["L1_attn_qkv_w"].T),
        "out_w0": halves(pair_rows(f["L0_attn_w_o"])),
        "out_w1": halves(pair_rows(f["L0_ffn_W_proj"].T), f["L0_ffn_b_proj"]),
        "out_w2": halves(f["L1_attn_out_w"].T),
        "causal": np.tile(causal, (1, NHG)).astype(ml_dtypes.bfloat16), "identb": np.eye(128).astype(ml_dtypes.bfloat16),
        "gate_w": halves(gate, gate_b), "lora_up": softmax_columns(lora_up),
        "anc_k": anc_k, "anc_b": anc_k.transpose(2, 1, 0), "anc_km": anc_km, "anc_bm": anc_km.transpose(2, 1, 0),
        "band_w": np.broadcast_to(np.stack([f["L1_attn_w_local"], f["L1_attn_w_global"], f["L1_attn_w_stride"]]), (128, 3)),
        "top_w": halves(f["L1_ffn_Wg"].T)[0:HALF], "w1": w1,
        "w2": f["L1_ffn_W2"].reshape(EXPERTS, MF, 128, D).transpose(2, 0, 1, 3),
        "b2": np.broadcast_to(f["L1_ffn_b2"], (128, EXPERTS, D)),
    }
    nc = bacc.Bacc("TRN2", target_bir_lowering=False, num_devices=1)
    feed, aps = {}, {}
    for name, v in arrays.items():
        v = np.ascontiguousarray(v)
        feed["in_" + name] = v
        aps[name] = nc.dram_tensor("in_" + name, v.shape, mybir.dt.from_np(v.dtype), kind="ExternalInput").ap()
    aps["out"] = nc.dram_tensor("out_h", (TOKENS // TILE, TILE, D), F32, kind="ExternalOutput").ap()
    build(nc, aps)
    r = run_bass_kernel_spmd(nc, [feed], core_ids=[0])
    return r.results[0]["out_h"].reshape(BATCH, SEQ, D)
```

```python
from contextlib import ExitStack
from collections import namedtuple

import numpy as np
import concourse.bass as bass
from concourse import mybir

F32 = mybir.dt.float32
F32R = mybir.dt.float32r
BF16 = mybir.dt.bfloat16
ALU = mybir.AluOpType
ACT = mybir.ActivationFunctionType
AX = mybir.AxisListType

BATCH, CHANNELS, IMAGE, PATCH = 64, 3, 128, 16
SEQ = (IMAGE // PATCH) ** 2
TOKENS = BATCH * SEQ
D, HEADS = 192, 12
HD = D // HEADS
D_IN = PATCH * PATCH * CHANNELS
KIN = D_IN // 128
TILE = 128
GROUP = 4
GT = GROUP * TILE
STEPS = TOKENS // GT
HALF = D // 2
VAUG = HD + 1
LORA_EXPERTS, RANK, LORA_SCALE = 8, 16, 2.0
GATE = LORA_EXPERTS + LORA_EXPERTS * RANK
TERMS = ((0, 0), (1, 1), (0, 2), (1, 3), (2, 0), (3, 1))
WINDOW, STRIDE, ANCHORS = 12, 3, 12
HG = 4
NHG = HEADS // HG
AROWS = HG * ANCHORS
EXPERTS, FF = 3, 768
MF = FF // 128
LN_EPS, NORM_MIN = 1e-5, 1e-6
CHOICE = 11
MASKED = -1e30
BANK = 512

C_ID = 0
C_BAND = C_ID + 128
C_COS = C_BAND + 128
C_SIN = C_COS + 4 * 2 * HEADS
C_STRIDE = C_SIN + 4 * 2 * HEADS
C_PAD = C_STRIDE + 1
C_HEAD = C_PAD + 1
C_TRI = C_HEAD + HG
C_HALFNEG = C_TRI + 64
C_MEAN = C_HALFNEG + 1
C_END = C_MEAN + 128


def build(nc, a):
    ctx = ExitStack()
    with ctx:
        def sb(name, shape, dt=F32):
            return ctx.enter_context(nc.sbuf_tensor(name, shape, dt))

        def sem(name):
            return ctx.enter_context(nc.semaphore(name))

        def sems(prefix, names):
            return namedtuple(prefix.rstrip("_"), names)(*(sem(prefix + n) for n in names.split()))

        tok_w = sb("tok_w", [128, KIN, D])
        tok_b = sb("tok_b", [128, D])
        cst = sb("cst", [128, C_END])
        causal = sb("causal", [128, BANK], BF16)
        identb = sb("identb", [128, 128], BF16)
        qkv_w = [sb(f"qkv_w{i}", [HALF + 1, 4, 3 * D], F32R) for i in range(3)]
        out_w = [sb(f"out_w{i}", [128, 2, D]) for i in range(3)]
        gate_w = sb("gate_w", [HALF + 1, 4, GATE], F32R)
        qkv_b = sb("qkv_b", [128, 3 * D])
        lora_up = sb("lora_up", [128, 3 * D])
        anc_k = sb("anc_k", [128, NHG, AROWS])
        anc_b = sb("anc_b", [AROWS, NHG, 128])
        band_w = sb("band_w", [128, 3])
        band_s = sb("band_s", [128, 4])
        w1 = sb("w1", [HALF + 1, 4, EXPERTS * FF], F32R)
        w2 = sb("w2", [128, EXPERTS, MF, D])
        b2 = sb("b2", [128, EXPERTS, D])
        top_w = sb("top_w", [HALF + 1, 4, 4], F32R)

        ident = cst[:, C_ID:C_ID + 128]
        band = cst[:, C_BAND:C_BAND + 128]
        cos = cst[0:HALF, C_COS:C_SIN].rearrange("p (u f) -> p u f", f=4)
        sin = cst[0:HALF, C_SIN:C_STRIDE].rearrange("p (u f) -> p u f", f=4)
        stride_rows = cst[:, C_STRIDE:C_STRIDE + 1]
        pad_count = cst[:, C_PAD:C_PAD + 1]
        head_rows = cst[:, C_HEAD:C_HEAD + HG]
        tri = cst[:, C_TRI:C_TRI + 64].rearrange("p (n m) -> p n m", n=8)
        image_mean = cst[:, C_MEAN:C_MEAN + 128]
        half_neg = cst[:, C_HALFNEG:C_HALFNEG + 1]

        x_or_kv = sb("x_or_kv", [128, GROUP * 2 * 2 * HEADS * VAUG])
        h = sb("h", [128, GROUP, D])
        ln = sb("ln", [128, GROUP, D])
        stats = sb("stats", [128, GROUP, 6])
        mean_var = sb("mean_var", [128, GROUP, 2])
        scrap = sb("scrap", [128, 2])
        neg_mr = sb("neg_mr", [128, GROUP])
        var_eps = sb("var_eps", [128, GROUP])
        rstd = sb("rstd", [128, GROUP])
        ln_t = sb("ln_t", [HALF + 1, 4, GT], F32R)
        qk = sb("qk", [128, GROUP, 2 * HEADS, 32])
        arena = sb("arena", [128, 3 * EXPERTS * MF // 3 * GT])
        vals = sb("vals", [128, GROUP, 2, 2, HALF])
        row_max = sb("row_max", [128, GROUP, HEADS])
        row_sum = sb("row_sum", [128, GROUP, HEADS])
        row_inv = sb("row_inv", [128, GROUP, HEADS])
        o_t = sb("o_t", [128, 2, GT])
        spare = sb("spare", [128, GROUP * (GATE + 256)])
        lgt = sb("lgt", [128, GROUP, 8])
        lgt_m = sb("lgt_m", [128, GROUP])
        lgt_s = sb("lgt_s", [128, GROUP])
        lgt_i = sb("lgt_i", [128, GROUP])
        above = sb("above", [128, GROUP, 8, 8])
        ties = sb("ties", [128, GROUP, 8, 8])
        rank = sb("rank", [128, GROUP, 8])
        picked = sb("picked", [128, GROUP, 8])
        vcat = sb("vcat", [128, GROUP, 2, HEADS, VAUG])
        kvc = sb("kvc", [128, GROUP, NHG, 2, VAUG])
        ao = sb("ao", [AROWS, GROUP, 2 * NHG, VAUG])
        ao_n = sb("ao_n", [AROWS, GROUP, 2 * NHG])
        ao_i = sb("ao_i", [AROWS, GROUP, 2 * NHG])
        qf_sum = sb("qf_sum", [128, GROUP, HEADS])
        nrm = sb("nrm", [128, GROUP, 3, HEADS])
        nrm_c = sb("nrm_c", [128, GROUP, 3, HEADS])
        nrm_i = sb("nrm_i", [128, GROUP, 3, HEADS])
        nrm_w = sb("nrm_w", [128, GROUP, 3, HEADS])
        tok_lg = sb("tok_lg", [128, GROUP, 4])
        tlg = sb("tlg", [128, GROUP, 4])

        x_t = x_or_kv[:, 0:KIN * GT].rearrange("p (k n) -> p k n", k=KIN)
        kvb = x_or_kv[:, :].rearrange("p (t b g k h v) -> p t b g k h v", t=GROUP, b=2, g=NHG, k=2, h=HG)
        ln_s = spare[:, 0:GROUP * 2 * D].rearrange("p (t s n) -> p t s n", t=GROUP, s=2)
        gates = spare[:, 0:GROUP * GATE].rearrange("p (t n) -> p t n", t=GROUP)
        down = spare[:, GROUP * GATE:GROUP * (GATE + 128)].rearrange("p (t n) -> p t n", t=GROUP)
        down_t = spare[:, GROUP * (GATE + 128):].rearrange("p (t n) -> p t n", t=GROUP)
        o_glob = spare[:, 0:GROUP * D].rearrange("p (t n) -> p t n", t=GROUP)
        o_str = spare[:, GROUP * D:2 * GROUP * D].rearrange("p (t n) -> p t n", t=GROUP)
        v_tok = o = ln

        BLOCKS = 2 * HEADS * SEQ
        q_t = arena[:, 0:2 * NHG * TILE].rearrange("p (s g n) -> p s g n", s=2, g=NHG)
        k_blk = arena[:, 768:768 + 2 * BLOCKS].rearrange("p (s b g n) -> p s b g n", s=2, b=2, g=NHG)
        prob = arena[:, 3840:3840 + GROUP * 768].rearrange("p (g n) -> p g n", g=GROUP)
        prob_t = arena[:, 6912:6912 + 2 * 768].rearrange("p (s c n) -> p s c n", s=2, c=6)
        qk_t = arena[:, 0:GROUP * 6 * TILE].rearrange("p (g c n) -> p g c n", g=GROUP, c=6)
        q_blk = arena[:, 3072:6144].rearrange("p (s g n) -> p s g n", s=2, g=NHG)
        loc_t = arena[:, 6144:9216].rearrange("p (s h n) -> p s h n", s=2, h=HEADS)
        fe = arena[:, 3072:3072 + GROUP * 2 * D].rearrange("p (g n) -> p g n", g=GROUP)
        fr = arena[:, 3072 + GROUP * 2 * D:3072 + GROUP * 4 * D].rearrange("p (g n) -> p g n", g=GROUP)
        hid = arena[:, :].rearrange("p (u n) -> p u n", u=EXPERTS * MF)

        QK_AT = 2 * EXPERTS * FF
        w1_raw = arena[0:HALF + 1, 0:QK_AT].rearrange("p (c n) -> p c n", c=2)
        qkv_raw = [arena[0:HALF + 1, QK_AT + i * 6 * D:QK_AT + (i + 1) * 6 * D].rearrange("p (c n) -> p c n", c=2)
                   for i in range(3)]
        GATE_AT = QK_AT + 18 * D
        gate_raw = arena[0:HALF + 1, GATE_AT:GATE_AT + 2 * GATE].rearrange("p (c n) -> p c n", c=2)
        TOP_AT = GATE_AT + 2 * GATE
        top_raw = arena[0:HALF + 1, TOP_AT:TOP_AT + 8].rearrange("p (c n) -> p c n", c=2)
        ANC_AT = TOP_AT + 8
        anc_km = arena[:, ANC_AT:ANC_AT + NHG * AROWS].rearrange("p (g n) -> p g n", g=NHG)
        BM_AT = ANC_AT + NHG * AROWS
        anc_bm = arena[0:AROWS, BM_AT:BM_AT + NHG * 128].rearrange("p (g n) -> p g n", g=NHG)
        anc_ke = spare[:, 0:NHG * AROWS].rearrange("p (g n) -> p g n", g=NHG)
        anc_be = spare[0:AROWS, 144:144 + NHG * 128].rearrange("p (g n) -> p g n", g=NHG)
        rot_a = spare[0:HALF, 528:720].rearrange("p (u s f) -> p u s f", s=2, f=4)
        rot_b = spare[0:HALF, 720:912].rearrange("p (u s f) -> p u s f", s=2, f=4)
        split_w = ((qkv_raw[1], qkv_w[1]), (gate_raw, gate_w), (qkv_raw[2], qkv_w[2]), (qkv_raw[0], qkv_w[0]),
                   (w1_raw, w1), (top_raw, top_w))

        ps = [ctx.enter_context(nc.psum_tensor(f"ps{i}", [128, 4 * BANK], F32)) for i in range(2)]

        def slot(n, cols):
            return ps[n // 2][:, n % 2 * 2 * BANK:n % 2 * 2 * BANK + cols]

        def lora_bank(t, k, n):
            at = (t // 2 * 2 + k) * BANK
            return ps[t % 2][:, at:at + n]

        def la_out(t):
            at = ((0, 3), (1, 3)) if t % 2 == 0 else ((t // 2, 0), (t // 2, 1))
            return [ps[s][:, k * BANK:(k + 1) * BANK] for s, k in at]

        x_loaded, tok_w_loaded, weights_loaded, mlp_w_loaded, stored = (
            sem(n) for n in "x_loaded tok_w_loaded weights_loaded mlp_w_loaded stored".split())
        setup = sem("setup")
        setup_anchor_exp, setup_anchor_relu = sem("setup_anchor_exp"), sem("setup_anchor_relu")
        rotated = sem("rotated")
        setup_dve, setup_band_exp = sem("setup_dve"), sem("setup_band_exp")
        tok_mm, embedded = sem("tok_mm"), sem("embedded")
        LN = [sems(f"ln{i}_", "stats aggr eps rstd shift high full split turned copied") for i in range(4)]
        AT = [sems(f"at{i}_", "qkv copied laid turned q_copied k_laid scores max shifted exp sums inv normed "
                              "probs_turned probs_copied av") for i in range(2)]
        w_high, w_low = sem("w_high"), sem("w_low")
        OUT = [sems(f"out{i}_", "turned copied mm added") for i in range(3)]
        RT = sems("route_", "mm copied chain shifted exp down turned turned_copied")
        LA = sems("la_", "qkv relu copied strided heads turned turned_copied blocks local local_masked kv kvb "
                         "kvc anchors anchor_n anchor_i ao globals gbd out qsum n_loc n_max "
                         "n_inv n_w loc glob str sum1 sum2")
        ML = sems("ml_", "gate gathered mean logits chain shifted exp biased acc0 acc1 up gelu outputs down")

        block = ctx.enter_context(nc.Block())
        N_W = 17

        @block.sync
        def _(sp):
            sp.dma_start(x_t, a["x"][0]).then_inc(x_loaded, 16)
            sp.dma_start(tok_w[:, :, :], a["tok_w"]).then_inc(tok_w_loaded, 16)
            sp.dma_start(tok_b[:, :], a["tok_b"]).then_inc(tok_w_loaded, 16)
            sp.dma_start(cst[:, :], a["cst"]).then_inc(weights_loaded, 16)
            for dst, src in ([(qkv_raw[i], f"qkv_w{i}") for i in range(3)] + [(gate_raw, "gate_w")]
                             + [(out_w[i][:, :, :], f"out_w{i}") for i in range(3)]
                             + [(causal[:, :], "causal"), (identb[:, :], "identb"), (lora_up[:, :], "lora_up"),
                                (anc_k[:, :, :], "anc_k"), (anc_b[:, :, :], "anc_b"), (band_w[:, :], "band_w"),
                                (anc_km, "anc_km"), (anc_bm, "anc_bm"), (qkv_b[:, :], "qkv_b")]):
                sp.dma_start(dst, a[src]).then_inc(weights_loaded, 16)
            for dst, src in ((w1_raw, "w1"), (w2[:, :, :, :], "w2"), (top_raw, "top_w"), (b2[:, :, :], "b2")):
                sp.dma_start(dst, a[src]).then_inc(mlp_w_loaded, 16)

            def step(i, last):
                for s in AT:
                    sp.wait_ge(s.copied, i * GROUP + GROUP)
                    for b in range(2):
                        for e in range(2):
                            sp.dma_start(vals[64 * e:64 * e + 64, :, b, e, :],
                                         v_tok[64 * b:64 * b + 64, :, e * HALF:(e + 1) * HALF]).then_inc(s.laid, 16)
                if not last:
                    sp.wait_ge(LA.out, i * GROUP + GROUP)
                    sp.dma_start(x_t, a["x"][bass.ds(i + 1, 1)].rearrange("o p k n -> (o p) k n")).then_inc(x_loaded, 16)
                for t in range(GROUP):
                    sp.wait_ge(ML.down, i * GROUP + (t + 2))
                    sp.dma_start(a["out"][bass.ds(i * GROUP + t, 1)].rearrange("o p n -> (o p) n"),
                                 h[:, t, :]).then_inc(stored, 16)

            with sp.Fori(0, STEPS - 1) as i:
                step(i, False)
            step(STEPS - 1, True)
            sp.wait_ge(stored, 16 * STEPS * GROUP + 16)

        @block.tensor
        def _(pe):
            def bank(t, k, n=BANK):
                return ps[t % 2][:, k * BANK:k * BANK + n]

            def tok(t):
                return slice(t * TILE, (t + 1) * TILE)

            def products(dst, act_cols, w, w_cols, bias_row, stop=True):
                for n, (x_c, w_c) in enumerate(TERMS):
                    rows = slice(0, HALF + (1 if bias_row and x_c == 1 else 0))
                    mm = pe.matmul(dst, ln_t[rows, x_c, act_cols], w[rows, w_c, w_cols], start=(n == 0),
                                   stop=stop and n == len(TERMS) - 1)
                return mm

            def turn_heads(dst, t):
                for c in range(6):
                    mm = pe.transpose(dst[:, c // NHG * BANK + c % NHG * TILE:][:, 0:TILE],
                                      qk[:, t, 4 * c:4 * c + 4, :].rearrange("p a b -> p (a b)"), ident)
                return mm

            def attention(s, o_s, out_wt, causal_mask, bias_row):
                def turn(t):
                    pe.wait_ge(s.copied, done[t])
                    if t >= 2:
                        pe.wait_ge(s.q_copied, done[t - 2])
                        if t == 2:
                            pe.wait_ge(s.k_laid, done[1])
                    else:
                        pe.wait_ge(s.copied, done[2])
                    turn_heads(slot(t % 2, 2 * BANK), t).then_inc(s.turned, 1)

                def scores(t):
                    dst = slot(2 + t % 2, HEADS * SEQ)
                    pe.wait_ge(s.q_copied, done[t])
                    if t % 2 == 0:
                        pe.wait_ge(s.k_laid, done[t + 1])
                    pe.wait_ge(*(s.shifted, done[t - 2]) if t >= 2 else (s.copied, done[3]))
                    if causal_mask:
                        for n in (0, BANK):
                            cols = slice(n, min(n + BANK, HEADS * SEQ))
                            pe.matmul(dst[:, cols], identb[:, :], causal[:, 0:cols.stop - n], start=True, stop=False,
                                      skip_group_check=True)
                    for g in range(NHG):
                        for b in range(2):
                            mm = pe.matmul(dst[64 * b:64 * b + 64, g * HG * SEQ:(g + 1) * HG * SEQ],
                                           q_t[:, t % 2, g, b * SEQ:(b + 1) * SEQ], k_blk[:, t % 2, b, g, :],
                                           start=not causal_mask, stop=True, skip_group_check=True)
                    mm.then_inc(s.scores, 1)

                def turn_probs(t):
                    dst = slot(t % 2, 6 * TILE)
                    pe.wait_ge(s.normed, done[t])
                    pe.wait_ge(*(s.probs_copied, done[t - 2]) if t >= 2 else ((s.k_laid, s.q_copied)[t], done[3]))
                    for c in range(6):
                        mm = pe.transpose(dst[:, c * TILE:(c + 1) * TILE], prob[:, t, c * TILE:(c + 1) * TILE], ident)
                    mm.then_inc(s.probs_turned, 1)

                def weigh_values(t):
                    dst = slot(2 + t % 2, 2 * TILE)
                    pe.wait_ge(s.probs_copied, done[t])
                    pe.wait_ge(*(o_s.copied, done[t - 2]) if t >= 2 else (s.shifted, done[t + 2]))
                    if t == 0:
                        pe.wait_ge(s.laid, laid)
                    for c in range(6):
                        at = 32 * (c % HG)
                        for b in range(2):
                            mm = pe.matmul(dst[at:at + 32, c // HG * TILE + b * SEQ:c // HG * TILE + (b + 1) * SEQ],
                                           vals[:, t, b, :, :].rearrange("p e n -> p (e n)")[:, c::HEADS // 2],
                                           prob_t[:, t % 2, c, b * SEQ:(b + 1) * SEQ],
                                           start=True, stop=True, skip_group_check=True)
                    mm.then_inc(s.av, 1)

                turn(0)
                turn(1)
                scores(0)
                turn(2)
                scores(1)
                turn(3)
                scores(2)
                turn_probs(0)
                scores(3)
                turn_probs(1)
                weigh_values(0)
                turn_probs(2)
                weigh_values(1)
                turn_probs(3)
                weigh_values(2)
                weigh_values(3)
                project(o_s, out_wt, bias_row)

            def project(o_s, out_wt, bias_row):
                for t in range(GROUP):
                    pe.wait_ge(o_s.copied, done[t])
                    if t >= 2:
                        pe.wait_ge(o_s.added, done[t - 2])
                    rows = slice(0, 65 if bias_row else 64)
                    pe.matmul(bank(t, 1, D), o_t[:, 0, tok(t)], out_wt[:, 0, :], start=True, stop=False)
                    pe.matmul(bank(t, 1, D), o_t[rows, 1, tok(t)], out_wt[rows, 1, :],
                              start=False, stop=True).then_inc(o_s.mm, 1)

            def norm_stage(s):
                for t in range(GROUP):
                    pe.wait_ge(s.split, done[t])
                    if t >= 2:
                        pe.wait_ge(s.copied, done[t - 2])
                    for c in range(4):
                        mm = pe.transpose(bank(t, 0)[0:HALF, c * TILE:(c + 1) * TILE],
                                          ln_s[:, t, c // 2, c % 2 * HALF:(c % 2 + 1) * HALF], ident)
                    mm.then_inc(s.turned, 1)

            pe.wait_ge(tok_w_loaded, 32)
            with pe.Fori(0, STEPS) as i:
                base = pe.snap(i * GROUP + 1)
                done = [pe.snap(i * GROUP + t + 1) for t in range(GROUP)]
                laid = pe.snap(i * 64 + 64)
                pe.wait_ge(x_loaded, pe.snap(i * 16 + 16))
                for t in range(GROUP):
                    pe.wait_ge(*(embedded, done[t - 2]) if t >= 2 else (ML.down, base))
                    for k in range(KIN):
                        mm = pe.matmul(bank(t, 1, D), x_t[:, k, tok(t)], tok_w[:, k, :],
                                       start=(k == 0), stop=(k == KIN - 1))
                    mm.then_inc(tok_mm, 1)
                pe.wait_ge(weights_loaded, 16 * N_W)
                pe.wait_ge(mlp_w_loaded, 16 * 4)
                pe.wait_ge(setup, 6)
                pe.wait_ge(w_low, len(split_w))
                pe.wait_ge(setup_dve, 11)
                norm_stage(LN[0])
                for t in range(GROUP):
                    pe.wait_ge(LN[0].copied, done[t])
                    pe.wait_ge(*(AT[0].copied, done[t - 2]) if t >= 2 else (LN[0].copied, done[t + 2]))
                    products(bank(t, 0, 2 * D), tok(t), qkv_w[0], slice(0, 2 * D), False)
                    products(bank(t, 1, D), tok(t), qkv_w[0], slice(2 * D, 3 * D), False).then_inc(AT[0].qkv, 1)
                attention(AT[0], OUT[0], out_w[0], True, False)
                norm_stage(LN[1])
                for t in range(GROUP):
                    pe.wait_ge(LN[1].copied, done[t])
                    pe.wait_ge(*(RT.copied, done[t - 2]) if t >= 2 else (LN[1].copied, done[t + 2]))
                    products(bank(t, 0, GATE), tok(t), gate_w, slice(0, GATE), True).then_inc(RT.mm, 1)

                def base_qk(t):
                    products(lora_bank(t, 0, 2 * D), tok(t), qkv_w[1], slice(0, 2 * D), False, stop=False)

                def base_v(t):
                    products(lora_bank(t, 1, D), tok(t), qkv_w[1], slice(2 * D, 3 * D), False, stop=False)

                for t in range(3):
                    if t < 2:
                        pe.wait_ge(RT.copied, done[t + 2])
                    base_qk(t)
                    base_v(t)
                for t in range(GROUP):
                    pe.wait_ge(RT.down, done[t])
                    mm = pe.transpose(ps[1][:, 3 * BANK + t * TILE:3 * BANK + (t + 1) * TILE], down[:, t, :], ident)
                mm.then_inc(RT.turned, GROUP)
                base_qk(3)
                pe.wait_ge(RT.turned_copied, done[3])
                base_v(3)
                for t in range(GROUP):
                    pe.matmul(lora_bank(t, 0, 2 * D), down_t[:, t, :], lora_up[:, 0:2 * D], start=False, stop=True)
                    pe.matmul(lora_bank(t, 1, D), down_t[:, t, :], lora_up[:, 2 * D:], start=False,
                              stop=True).then_inc(AT[1].qkv, 1)
                attention(AT[1], OUT[1], out_w[1], False, True)
                norm_stage(LN[2])
                w = qkv_w[2]
                for t in range(GROUP):
                    pe.wait_ge(LN[2].copied, done[t])
                    pe.wait_ge(*(LA.copied, done[t - 2]) if t >= 2 else (LN[2].copied, done[t + 2]))
                    products(bank(t, 0, 2 * D), tok(t), w, slice(0, 2 * D), False)
                    products(bank(t, 1, D), tok(t), w, slice(2 * D, 3 * D), False).then_inc(LA.qkv, 1)
                for t in range(GROUP):
                    pe.wait_ge(LA.heads, done[t])
                    pe.wait_ge(*(LA.turned_copied, done[t - 2]) if t >= 2 else (LA.copied, done[t + 2]))
                    turn_heads(ps[t % 2], t).then_inc(LA.turned, 1)
                for t in range(GROUP):
                    pe.wait_ge(LA.strided, done[t])
                    if t >= 2:
                        pe.wait_ge(LA.kvb, done[t - 2])
                    for g in range(NHG):
                        for b in range(2):
                            r = slice(64 * b, 64 * b + 64)
                            mm = pe.matmul(bank(t, 2 + b)[:, g * 136:(g + 1) * 136],
                                           qk[r, t, HEADS + HG * g:HEADS + HG * (g + 1), :].rearrange("p a b -> p (a b)"),
                                           vcat[r, t, :, HG * g:HG * (g + 1), :].rearrange("p k h v -> p k (h v)"),
                                           start=True, stop=True, skip_group_check=True)
                    mm.then_inc(LA.kv, 1)

                def local(t):
                    pe.wait_ge(LA.turned_copied, done[t])
                    pe.wait_ge(LA.blocks, done[t])
                    if t >= 2:
                        pe.wait_ge(LA.local_masked, done[t - 2])
                    else:
                        pe.wait_ge(LA.turned_copied, done[t + 2])
                        pe.wait_ge(LA.kvb, done[t + 2])
                    for g in range(NHG):
                        mm = pe.matmul(bank(t, g), qk_t[:, t, NHG + g, :], q_blk[:, t % 2, g, :], start=True, stop=True)
                    mm.then_inc(LA.local, 1)

                def anchors(t):
                    pe.wait_ge(LA.kvc, done[t])
                    pe.wait_ge(*(LA.ao, done[t - 2]) if t >= 2 else (LA.kvb, done[t + 2]))
                    for g in range(NHG):
                        mm = pe.matmul(bank(t, 3)[0:AROWS, g * 34:(g + 1) * 34], anc_k[:, g, :],
                                       kvc[:, t, g, :, :].rearrange("p b v -> p (b v)"),
                                       start=True, stop=True, skip_group_check=True)
                    mm.then_inc(LA.anchors, 1)

                def global_states(t):
                    pe.wait_ge(LA.ao, done[t])
                    pe.wait_ge(*(LA.gbd, done[t - 2]) if t >= 2 else (LA.ao, done[t + 2]))
                    for g in range(NHG):
                        mm = pe.matmul(bank(t, 3)[:, g * 34:(g + 1) * 34], anc_b[:, g, :],
                                       ao[:, t, 2 * g:2 * g + 2, :].rearrange("p b v -> p (b v)"),
                                       start=True, stop=True, skip_group_check=True)
                    mm.then_inc(LA.globals, 1)

                def three_bands(t):
                    loc, lin = la_out(t)
                    pe.wait_ge(LA.gbd, done[3 if t == 0 else t])
                    pe.wait_ge(LA.local_masked, done[(0, 2, 2, 3)[t]])
                    if t == 2:
                        pe.wait_ge(LA.str, done[0])
                    for h_ in range(HEADS):
                        pe.matmul(loc[:, h_ * VAUG:(h_ + 1) * VAUG], loc_t[:, t % 2, h_, :],
                                  vcat[:, t, 0, h_, :], start=True, stop=True, skip_group_check=True)
                    for g in range(NHG):
                        for b in range(2):
                            mm = pe.matmul(lin[64 * b:64 * b + 64, g * 136:(g + 1) * 136],
                                           qk_t[:, t, g, b * SEQ:(b + 1) * SEQ],
                                           kvb[:, t, b, g, :, :, :].rearrange("p k h v -> p (k h v)"),
                                           start=True, stop=True, skip_group_check=True)
                    mm.then_inc(LA.out, 1)

                local(0)
                anchors(0)
                anchors(1)
                local(1)
                anchors(2)
                anchors(3)
                local(2)
                global_states(0)
                global_states(1)
                local(3)
                global_states(2)
                global_states(3)
                for t in range(GROUP):
                    three_bands(t)
                for t in range(GROUP):
                    pe.wait_ge(LA.sum2, done[t])
                    if t >= 2:
                        pe.wait_ge(OUT[2].copied, done[t - 2])
                    pe.transpose(bank(t, 2)[:, 0:TILE], o[:, t, 0:128], ident)
                    pe.transpose(bank(t, 2)[0:64, TILE:2 * TILE], o[:, t, 128:D], ident).then_inc(OUT[2].turned, 1)
                project(OUT[2], out_w[2], False)
                norm_stage(LN[3])
                for t in range(GROUP):
                    pe.wait_ge(LN[3].copied, done[t])
                    if t >= 2:
                        pe.wait_ge(ML.gathered, done[t - 2])
                    products(bank(t, 2, 4), tok(t), top_w, slice(0, 4), False).then_inc(ML.gate, 1)
                units = pe.snap(i * (EXPERTS * MF))
                for u in range(EXPERTS * MF):
                    if u >= 2:
                        pe.wait_ge(ML.gelu, units + (u - 1))
                    if u == 2:
                        pe.wait_ge(ML.gathered, done[3])
                        pe.matmul(bank(0, 2, GROUP * 4), image_mean, tok_lg[:, :, :].rearrange("p t n -> p (t n)"),
                                  start=True, stop=True).then_inc(ML.mean, GROUP)
                    for n, (x_c, w_c) in enumerate(TERMS):
                        rows = slice(0, HALF + (x_c == 1))
                        mm = pe.matmul(bank(u, 0), w1[rows, w_c, u * 128:(u + 1) * 128], ln_t[rows, x_c, :],
                                       start=(n == 0), stop=(n == len(TERMS) - 1))
                    mm.then_inc(ML.up, 1)
                pe.wait_ge(ML.gelu, units + EXPERTS * MF)
                for t in range(GROUP):
                    if t >= 2:
                        pe.wait_ge(ML.down, pe.snap(i * GROUP + t))
                    for e in range(EXPERTS):
                        for m in range(MF):
                            mm = pe.matmul(bank(t, e, D), hid[:, e * MF + m, tok(t)], w2[:, e, m, :],
                                           start=(m == 0), stop=(m == MF - 1))
                    mm.then_inc(ML.outputs, 1)

        @block.scalar
        def _(act):
            def bank(t, k, n=BANK):
                return ps[t % 2][:, k * BANK:k * BANK + n]

            def tok(t):
                return slice(t * TILE, (t + 1) * TILE)

            def copy_norm(s):
                for t in range(GROUP):
                    act.wait_ge(s.turned, done[t])
                    act.activation(ln_t[0:HALF, :, tok(t)], bank(t, 0)[0:HALF, :].rearrange("p (c n) -> p c n", c=4),
                                   ACT.Copy).then_inc(s.copied, 1)

            def copy_out(t, src, ready, copied):
                act.wait_ge(ready, done[t])
                act.activation(o_t[:, 0, tok(t)], src[:, 0:TILE], ACT.Copy)
                act.activation(o_t[0:64, 1, tok(t)], src[0:64, TILE:2 * TILE], ACT.Copy).then_inc(copied, 1)

            def split_high(s):
                for t in range(GROUP):
                    act.wait_ge(s.shift, done[t])
                    act.activation(ln_s[:, t, 0, :].bitcast(F32R), h[:, t, :], ACT.Identity,
                                   bias=neg_mr[:, t:t + 1], scale=rstd[:, t:t + 1]).then_inc(s.high, 1)

            def attention(s, o_s):
                def copy_q(t):
                    act.wait_ge(s.turned, done[t])
                    if t >= 2:
                        act.wait_ge(s.scores, done[t - 2])
                    op = act.activation(q_t[:, t % 2, :, :].rearrange("p g n -> p (g n)"), slot(t % 2, NHG * TILE),
                                   ACT.Copy)
                    if t % 2 == 0:
                        op.then_inc(s.q_copied, 1)
                        return
                    for j in range(HG):
                        op = act.activation(k_blk[:, 1, :, :, j * SEQ:(j + 1) * SEQ].rearrange("p b g n -> p g b n"),
                                            slot(1, 2 * BANK)[:, BANK:BANK + NHG * TILE]
                                            .rearrange("p (g b n) -> p g b n", g=NHG, b=2),
                                            ACT.Copy, scale=head_rows[:, j:j + 1])
                    op.then_inc(s.q_copied, 1)

                def exponentials(t):
                    act.wait_ge(s.shifted, done[t])
                    act.activation(prob[:, t, :], prob[:, t, :], ACT.Exp, scale=HD ** -0.5).then_inc(s.exp, 1)

                def copy_probs(t):
                    act.wait_ge(s.probs_turned, done[t])
                    if t >= 2:
                        act.wait_ge(s.av, done[t - 2])
                    act.activation(prob_t[:, t % 2, :, :].rearrange("p c n -> p (c n)"), slot(t % 2, 6 * TILE),
                                   ACT.Copy).then_inc(s.probs_copied, 1)

                def copy_output(t):
                    copy_out(t, slot(2 + t % 2, 2 * TILE), s.av, o_s.copied)

                copy_q(0)
                copy_q(1)
                copy_q(2)
                exponentials(0)
                copy_q(3)
                exponentials(1)
                copy_probs(0)
                exponentials(2)
                copy_probs(1)
                exponentials(3)
                copy_output(0)
                copy_probs(2)
                copy_output(1)
                copy_probs(3)
                copy_output(2)
                copy_output(3)

            act.wait_ge(weights_loaded, 16 * N_W)
            act.activation(anc_ke, anc_k[:, :, :], ACT.Exp).then_inc(setup_anchor_exp, 1)
            act.activation(anc_be, anc_b[:, :, :], ACT.Exp).then_inc(setup_anchor_exp, 1)
            act.wait_ge(setup_dve, 2)
            act.activation(band_w[:, :], band_w[:, :], ACT.Exp).then_inc(setup_band_exp, 1)
            for raw, w in split_w:
                if raw is qkv_raw[0]:
                    act.wait_ge(rotated, 4)
                if raw is w1_raw:
                    act.wait_ge(mlp_w_loaded, 16 * 4)
                act.activation(w[:, 0:2, :], raw, ACT.Copy).then_inc(w_high, 1)
            act.wait_ge(w_low, len(split_w))
            act.wait_ge(setup, 6)
            with act.Fori(0, STEPS) as i:
                done = [act.snap(i * GROUP + t + 1) for t in range(GROUP)]
                split_high(LN[0])
                copy_norm(LN[0])
                for t in range(GROUP):
                    act.wait_ge(AT[0].qkv, done[t])
                    act.activation(qk[:, t, :, 0:HD], bank(t, 0, 2 * D).rearrange("p (u f) -> p u f", f=HD), ACT.Copy)
                    act.activation(v_tok[:, t, :], bank(t, 1, D), ACT.Copy).then_inc(AT[0].copied, 1)
                attention(AT[0], OUT[0])
                split_high(LN[1])
                copy_norm(LN[1])
                for t in range(GROUP):
                    act.wait_ge(RT.mm, done[t])
                    act.activation(gates[:, t, :], bank(t, 0, GATE), ACT.Copy).then_inc(RT.copied, 1)
                act.wait_ge(RT.shifted, done[GROUP - 1])
                act.activation(lgt[:, :, :], lgt[:, :, :], ACT.Exp).then_inc(RT.exp, GROUP)
                act.wait_ge(RT.turned, done[3])
                act.activation(down_t.rearrange("p t n -> p (t n)"), ps[1][:, 3 * BANK:],
                               ACT.Copy).then_inc(RT.turned_copied, GROUP)
                attention(AT[1], OUT[1])
                split_high(LN[2])
                copy_norm(LN[2])
                for t in range(GROUP):
                    act.wait_ge(LA.qkv, done[t])
                    act.activation(fe[:, t, :], bank(t, 0, 2 * D), ACT.Exp)
                    act.activation(fr[:, t, :], bank(t, 0, 2 * D), ACT.Relu).then_inc(LA.relu, 1)
                    act.activation(vcat[:, t, 0, :, 0:HD], bank(t, 1, D).rearrange("p (u f) -> p u f", f=HD),
                                   ACT.Copy).then_inc(LA.copied, 1)
                for t in range(GROUP):
                    act.wait_ge(LA.turned, done[t])
                    act.activation(qk_t[:, t, :, :].rearrange("p (s g) n -> p s (g n)", s=2),
                                   ps[t % 2][:, 0:2 * BANK].rearrange("p (s n) -> p s n", s=2)[:, :, 0:NHG * TILE],
                                   ACT.Copy).then_inc(LA.turned_copied, 1)
                for t in range(GROUP):
                    copy_out(t, bank(t, 2), OUT[2].turned, OUT[2].copied)
                split_high(LN[3])
                copy_norm(LN[3])
                for t in range(GROUP):
                    act.wait_ge(ML.gate, done[t])
                    act.activation(tok_lg[:, t, :], bank(t, 2, 4), ACT.Copy).then_inc(ML.gathered, 1)
                units = act.snap(i * (EXPERTS * MF))
                for u in range(EXPERTS * MF):
                    act.wait_ge(ML.up, units + (u + 1))
                    act.activation(hid[:, u, :], bank(u, 0), ACT.Gelu).then_inc(ML.gelu, 1)
                    if u == 1:
                        act.wait_ge(ML.mean, done[3])
                        act.activation(tlg[:, :, :].rearrange("p t n -> p (t n)"), bank(0, 2, GROUP * 4),
                                       ACT.Copy).then_inc(ML.logits, GROUP)
                    if u == 4:
                        act.wait_ge(ML.shifted, done[3])
                        act.activation(lgt[:, :, 0:EXPERTS], lgt[:, :, 0:EXPERTS], ACT.Exp).then_inc(ML.exp, GROUP)

        @block.gpsimd
        def _(pool):
            margins = ((ln_t[HALF:HALF + 1, 1, :].bitcast(F32), 1.0), (o_t[64:65, 1, :], 1.0), (qk[:, :, :, HD:32], 0.0),
                       (vals[:, :, :, :, :], 0.0), (vcat[:, :, 0, :, HD:VAUG], 1.0), (ao[:, :, :, HD:VAUG], 1.0))
            for n, (margin, value) in enumerate(margins):
                if n:
                    pool.wait_ge(setup, n)
                pool.memset(margin, value).then_inc(setup, 1)
            pool.wait_ge(weights_loaded, 16 * N_W)
            pool.wait_ge(setup, 6)

            def root(s):
                for p in range(0, GROUP, 2):
                    pool.wait_ge(s.eps, done[p + 1])
                    pool.tensor_tensor(rstd[:, p:p + 2], var_eps[:, p:p + 2], half_neg.to_broadcast([128, 2]),
                                       ALU.pow).then_inc(s.rstd, 2)

            def divide(s):
                for t in range(GROUP):
                    weights = prob[:, t, :].rearrange("p (h k) -> p h k", h=HEADS)
                    pool.wait_ge(s.inv, done[t])
                    pool.tensor_tensor(weights, weights, row_inv[:, t, :].unsqueeze(2)
                                       .to_broadcast([128, HEADS, SEQ]), ALU.mult).then_inc(s.normed, 1)

            with pool.Fori(0, STEPS) as i:
                done = [pool.snap(i * GROUP + t + 1) for t in range(GROUP)]
                root(LN[0])
                divide(AT[0])
                root(LN[1])
                divide(AT[1])
                root(LN[2])
                for t in range(GROUP):
                    pool.wait_ge(LA.copied, done[t])
                    pool.tensor_tensor(vcat[:, t, 1, :, :].rearrange("p h v -> p (h v)"),
                                       vcat[:, t, 0, :, :].rearrange("p h v -> p (h v)"),
                                       stride_rows.to_broadcast([128, HEADS * VAUG]), ALU.mult).then_inc(LA.strided, 1)
                pool.wait_ge(LA.heads, done[3])
                for t in range(GROUP):
                    pool.wait_ge(LA.turned_copied, done[t])
                    if t >= 2:
                        pool.wait_ge(LA.local, done[t - 2])
                    for g in range(NHG):
                        op = pool.tensor_tensor(q_blk[:, t % 2, g, :].rearrange("p (j n) -> p j n", j=HG),
                                                qk_t[:, t, g, :].unsqueeze(1).to_broadcast([128, HG, TILE]),
                                                head_rows.unsqueeze(2).to_broadcast([128, HG, TILE]), ALU.mult)
                    op.then_inc(LA.blocks, 1)
                root(LN[3])

        @block.vector
        def _(dve):
            def bank(t, k, n=BANK):
                return ps[t % 2][:, k * BANK:k * BANK + n]

            def all_tiles():
                return range(GROUP)

            def norm_stage(s, mm, src, added):
                def add(t):
                    dve.wait_ge(mm, done[t])
                    dve.tensor_tensor(h[:, t, :], bank(t, 1, D), src(t), ALU.add).then_inc(added, 1)

                def count(t):
                    dve.wait_ge(added, done[t])
                    dve.bn_stats(stats[:, t, :], h[:, t, :]).then_inc(s.stats, 1)

                def join(p):
                    for t in (p, p + 1):
                        dve.bn_aggr(mean_var[:, t, :], stats[:, t, :]).then_inc(s.aggr, 1)

                def add_eps(p):
                    dve.wait_ge(s.aggr, done[p + 1])
                    dve.tensor_scalar(var_eps[:, p:p + 2], mean_var[:, p:p + 2, 1], LN_EPS, None,
                                      ALU.add).then_inc(s.eps, 2)

                def shift(p):
                    dve.wait_ge(s.rstd, done[p + 1])
                    dve.scalar_tensor_tensor(out=neg_mr[:, p:p + 2], in0=mean_var[:, p:p + 2, 0], scalar=-1.0,
                                             in1=rstd[:, p:p + 2], op0=ALU.mult, op1=ALU.mult).then_inc(s.shift, 2)

                def normalise(t):
                    dve.tensor_scalar(ln[:, t, :], h[:, t, :], mean_var[:, t, 0:1], rstd[:, t:t + 1],
                                      ALU.subtract, ALU.mult).then_inc(s.full, 1)

                def low(t):
                    dve.wait_ge(s.high, done[t])
                    dve.wait_ge(s.full, done[t])
                    dve.tensor_tensor(ln_s[:, t, 1, :].bitcast(F32R), ln[:, t, :], ln_s[:, t, 0, :],
                                      ALU.subtract).then_inc(s.split, 1)

                add(0)
                add(1)
                count(0)
                count(1)
                add(2)
                dve.wait_ge(s.stats, done[1])
                add(3)
                join(0)
                count(2)
                count(3)
                dve.wait_ge(s.stats, done[3])
                add_eps(0)
                join(2)
                add_eps(2)
                shift(0)
                normalise(0)
                normalise(1)
                shift(2)
                low(0)
                low(1)
                normalise(2)
                normalise(3)
                low(2)
                low(3)

            def attention(s):
                def lay_k(t):
                    dve.wait_ge(s.turned, done[t])
                    if t >= 2:
                        dve.wait_ge(s.scores, done[t - 2])
                    k_in = slot(t % 2, 2 * BANK)[:, BANK:BANK + NHG * TILE].rearrange("p (g n) -> p g n", g=NHG)
                    for b in range(2):
                        cells = [128, NHG, HG, SEQ]
                        op = dve.tensor_tensor(
                            k_blk[:, t % 2, b, :, :].rearrange("p g (j n) -> p g j n", j=HG),
                            k_in[:, :, b * SEQ:(b + 1) * SEQ].unsqueeze(2).to_broadcast(cells),
                            head_rows.unsqueeze(1).unsqueeze(3).to_broadcast(cells), ALU.mult)
                    op.then_inc(s.k_laid, 2)

                def shift(t):
                    scores = slot(2 + t % 2, HEADS * SEQ).rearrange("p (h k) -> p h k", h=HEADS)
                    dve.wait_ge(s.scores, done[t])
                    dve.tensor_reduce(row_max[:, t, :], scores, AX.X, ALU.max).then_inc(s.max, 1)
                    dve.wait_ge(s.max, done[t])
                    dve.tensor_tensor(prob[:, t, :].rearrange("p (h k) -> p h k", h=HEADS), scores,
                                      row_max[:, t, :].unsqueeze(2).to_broadcast([128, HEADS, SEQ]),
                                      ALU.subtract).then_inc(s.shifted, 1)

                def sums(t):
                    dve.wait_ge(s.exp, done[t])
                    dve.tensor_reduce(row_sum[:, t, :], prob[:, t, :].rearrange("p (h k) -> p h k", h=HEADS),
                                      AX.X, ALU.add).then_inc(s.sums, 1)
                    dve.wait_ge(s.sums, done[t])
                    dve.reciprocal(row_inv[:, t, :], row_sum[:, t, :]).then_inc(s.inv, 1)

                lay_k(0)
                shift(0)
                lay_k(2)
                shift(1)
                sums(0)
                sums(1)
                shift(2)
                shift(3)
                sums(2)
                sums(3)

            def choose(logits, n, keep, factor, s):
                cells = [128, GROUP, n, n]
                lower = tri[:, 0:n, 0:n].unsqueeze(1).to_broadcast(cells)
                rivals = logits.unsqueeze(2).to_broadcast(cells)
                own = logits.unsqueeze(3).to_broadcast(cells)
                at = dve.snap(i * CHOICE)
                n8 = slice(0, n)
                dve.tensor_reduce(lgt_m[:, :], logits, AX.X, ALU.max).then_inc(s.chain, 1)
                dve.tensor_tensor(above[:, :, n8, n8], rivals, own, ALU.is_gt).then_inc(s.chain, 1)
                dve.tensor_tensor(ties[:, :, n8, n8], rivals, own, ALU.is_equal).then_inc(s.chain, 1)
                dve.wait_ge(s.chain, at + 1)
                dve.tensor_tensor(lgt[:, :, n8], logits, lgt_m[:, :].unsqueeze(2).to_broadcast([128, GROUP, n]),
                                  ALU.subtract).then_inc(s.shifted, GROUP)
                dve.wait_ge(s.chain, at + 3)
                dve.tensor_tensor(ties[:, :, n8, n8], ties[:, :, n8, n8], lower, ALU.mult).then_inc(s.chain, 1)
                dve.wait_ge(s.chain, at + 4)
                dve.tensor_tensor(above[:, :, n8, n8], above[:, :, n8, n8], ties[:, :, n8, n8],
                                  ALU.add).then_inc(s.chain, 1)
                dve.wait_ge(s.chain, at + 5)
                dve.tensor_reduce(rank[:, :, n8], above[:, :, n8, n8], AX.X, ALU.add).then_inc(s.chain, 1)
                dve.wait_ge(s.chain, at + 6)
                dve.tensor_scalar(picked[:, :, n8], rank[:, :, n8], keep - 0.5, factor, ALU.is_lt,
                                  ALU.mult).then_inc(s.chain, 1)
                dve.wait_ge(s.exp, done[GROUP - 1])
                dve.tensor_reduce(lgt_s[:, :], lgt[:, :, n8], AX.X, ALU.add).then_inc(s.chain, 1)
                dve.wait_ge(s.chain, at + 7)
                dve.tensor_tensor(picked[:, :, n8], picked[:, :, n8], lgt[:, :, n8], ALU.mult).then_inc(s.chain, 1)
                dve.wait_ge(s.chain, at + 8)
                dve.reciprocal(lgt_i[:, :], lgt_s[:, :]).then_inc(s.chain, 1)
                dve.wait_ge(s.chain, at + 10)
                dve.tensor_tensor(picked[:, :, n8], picked[:, :, n8],
                                  lgt_i[:, :].unsqueeze(2).to_broadcast([128, GROUP, n]), ALU.mult)\
                    .then_inc(s.chain, 1)
                dve.wait_ge(s.chain, at + 11)

            dve.wait_ge(weights_loaded, 16 * N_W)
            for c in range(2):
                pair = qkv_raw[0][0:HALF, c, 0:2 * D].rearrange("p (u s f) -> p u s f", s=2, f=HD // 2)[:, :, :, 0:4]
                if c:
                    dve.wait_ge(rotated, 2 * c)
                dve.tensor_tensor(rot_b[:, :, 0, :], pair[:, :, 1, :], sin, ALU.mult)
                dve.tensor_tensor(rot_b[:, :, 1, :], pair[:, :, 0, :], sin, ALU.mult)
                dve.tensor_tensor(rot_a[:, :, 0, :], pair[:, :, 0, :], cos, ALU.mult)
                dve.tensor_tensor(rot_a[:, :, 1, :], pair[:, :, 1, :], cos, ALU.mult).then_inc(rotated, 1)
                dve.wait_ge(rotated, 2 * c + 1)
                dve.tensor_tensor(pair[:, :, 0, :], rot_a[:, :, 0, :], rot_b[:, :, 0, :], ALU.add)
                dve.tensor_tensor(pair[:, :, 1, :], rot_a[:, :, 1, :], rot_b[:, :, 1, :],
                                  ALU.subtract).then_inc(rotated, 1)
            dve.wait_ge(weights_loaded, 16 * N_W)
            dve.tensor_reduce(band_s[:, 0:1], band_w[:, :], AX.X, ALU.max).then_inc(setup_dve, 1)
            dve.wait_ge(setup_dve, 1)
            dve.tensor_scalar(band_w[:, :], band_w[:, :], band_s[:, 0:1], None, ALU.subtract).then_inc(setup_dve, 1)
            dve.wait_ge(setup_anchor_exp, 2)
            for x, e, m in ((anc_k, anc_ke, anc_km), (anc_b, anc_be, anc_bm)):
                n = 3 if x is anc_k else 6
                dve.tensor_scalar(e, e, 1.0, None, ALU.min).then_inc(setup_dve, 1)
                dve.wait_ge(setup_dve, n)
                dve.scalar_tensor_tensor(out=x[:, :, :], in0=x[:, :, :], scalar=0.0, in1=e,
                                         op0=ALU.max, op1=ALU.add).then_inc(setup_dve, 1)
                dve.wait_ge(setup_dve, n + 1)
                dve.tensor_tensor(x[:, :, :], x[:, :, :], m, ALU.mult).then_inc(setup_dve, 1)
            dve.wait_ge(setup_band_exp, 1)
            dve.tensor_reduce(band_s[:, 1:2], band_w[:, :], AX.X, ALU.add).then_inc(setup_dve, 1)
            dve.wait_ge(setup_dve, 9)
            dve.reciprocal(band_s[:, 2:3], band_s[:, 1:2]).then_inc(setup_dve, 1)
            dve.wait_ge(setup_dve, 10)
            dve.tensor_scalar(band_w[:, :], band_w[:, :], band_s[:, 2:3], None, ALU.mult).then_inc(setup_dve, 1)
            dve.wait_ge(setup_dve, 11)
            dve.memset(band_s[:, 3:4], 0.0).then_inc(ML.down, 1)
            dve.memset(band_s[:, 0:1], 0.0).then_inc(stored, 16)
            for n, (raw, w) in enumerate(split_w):
                dve.wait_ge(w_high, n + 1)
                dve.tensor_tensor(w[:, 2:4, :], raw, w[:, 0:2, :].bitcast(F32), ALU.subtract).then_inc(w_low, 1)
            dve.wait_ge(w_low, len(split_w))
            dve.wait_ge(setup, 6)
            dve.wait_ge(tok_w_loaded, 32)

            with dve.Fori(0, STEPS) as i:
                done = [dve.snap(i * GROUP + t + 1) for t in range(GROUP)]
                dve.wait_ge(stored, dve.snap(i * (16 * GROUP) + 16))
                norm_stage(LN[0], tok_mm, lambda t: tok_b[:, :], embedded)
                attention(AT[0])
                norm_stage(LN[1], OUT[0].mm, lambda t: h[:, t, :], OUT[0].added)
                dve.wait_ge(RT.copied, done[GROUP - 1])
                choose(gates[:, :, 0:LORA_EXPERTS], LORA_EXPERTS, 2, LORA_SCALE, RT)
                for t in all_tiles():
                    dve.tensor_tensor(down[:, t, :].rearrange("p (n r) -> p n r", r=RANK),
                                      gates[:, t, LORA_EXPERTS:].rearrange("p (n r) -> p n r", r=RANK),
                                      picked[:, t, :].unsqueeze(2).to_broadcast([128, LORA_EXPERTS, RANK]),
                                      ALU.mult).then_inc(RT.down, 1)
                for t in all_tiles():
                    dve.wait_ge(AT[1].qkv, done[t])
                    dve.tensor_tensor(qk[:, t, :, 0:HD], lora_bank(t, 0, 2 * D).rearrange("p (u f) -> p u f", f=HD),
                                      qkv_b[:, 0:2 * D].rearrange("p (u f) -> p u f", f=HD), ALU.add)
                    dve.tensor_tensor(v_tok[:, t, :], lora_bank(t, 1, D), qkv_b[:, 2 * D:], ALU.add).then_inc(AT[1].copied, 1)
                attention(AT[1])
                norm_stage(LN[2], OUT[1].mm, lambda t: h[:, t, :], OUT[1].added)
                for t in all_tiles():
                    dve.wait_ge(LA.relu, done[t])
                    dve.scalar_tensor_tensor(out=qk[:, t, :, 0:HD], in0=fe[:, t, :].rearrange("p (u f) -> p u f", f=HD),
                                             scalar=1.0, in1=fr[:, t, :].rearrange("p (u f) -> p u f", f=HD),
                                             op0=ALU.min, op1=ALU.add).then_inc(LA.heads, 1)
                for t in all_tiles():
                    dve.wait_ge(LA.heads, done[t])
                    dve.tensor_reduce(qf_sum[:, t, :], qk[:, t, 0:HEADS, 0:HD], AX.X, ALU.add).then_inc(LA.qsum, 1)
                for t in all_tiles():
                    dve.wait_ge(LA.kv, done[t])
                    for b in range(2):
                        op = dve.tensor_tensor(
                            kvb[:, t, b, :, :, :, :].rearrange("p g k h v -> p (g k) h v"),
                            bank(t, 2 + b, 408).rearrange("p (g h v) -> p g h v", h=HG, v=VAUG),
                            head_rows.unsqueeze(1).unsqueeze(3).to_broadcast([128, 2 * NHG, HG, VAUG]), ALU.mult)
                    op.then_inc(LA.kvb, 1)
                for t in all_tiles():
                    dve.wait_ge(LA.kvb, done[t])
                    for b in range(2):
                        op = dve.tensor_reduce(kvc[:, t, :, b, :],
                                               kvb[:, t, b, :, 0, :, :].rearrange("p g h v -> p g v h"), AX.X, ALU.add)
                    op.then_inc(LA.kvc, 1)

                def mask(t):
                    dve.wait_ge(LA.local, done[t])
                    if t >= 2:
                        dve.wait_ge(LA.out, done[t - 2])
                    dve.tensor_tensor(loc_t[:, t % 2, :, :],
                                      ps[t % 2][:, 0:HEADS * TILE].rearrange("p (h n) -> p h n", h=HEADS),
                                      band.unsqueeze(1).to_broadcast([128, HEADS, TILE]),
                                      ALU.mult).then_inc(LA.local_masked, 1)

                def anchor_outputs(t):
                    anc = bank(t, 3)[0:AROWS, 0:2 * NHG * VAUG].rearrange("p (u v) -> p u v", v=VAUG)
                    dve.wait_ge(LA.anchors, done[t])
                    dve.tensor_scalar(ao_n[:, t, :], anc[:, :, HD], NORM_MIN, None, ALU.max).then_inc(LA.anchor_n, 1)
                    dve.wait_ge(LA.anchor_n, done[t])
                    dve.reciprocal(ao_i[:, t, :], ao_n[:, t, :]).then_inc(LA.anchor_i, 1)
                    dve.wait_ge(LA.anchor_i, done[t])
                    dve.tensor_tensor(ao[:, t, :, 0:HD], anc[:, :, 0:HD],
                                      ao_i[:, t, :].unsqueeze(2).to_broadcast([AROWS, 2 * NHG, HD]),
                                      ALU.mult).then_inc(LA.ao, 1)

                def lay_globals(t):
                    dve.wait_ge(LA.globals, done[t])
                    dve.wait_ge(LA.kvc, done[t])
                    for b in range(2):
                        op = dve.tensor_tensor(
                            kvb[:, t, b, :, 0, :, :],
                            bank(t, 3, 2 * NHG * VAUG).rearrange("p (g b v) -> p g b v", b=2, v=VAUG)[:, :, b, :]
                            .unsqueeze(2).to_broadcast([128, NHG, HG, VAUG]),
                            head_rows.unsqueeze(1).unsqueeze(3).to_broadcast([128, NHG, HG, VAUG]), ALU.mult)
                    op.then_inc(LA.gbd, 1)

                def combine(t):
                    loc, lin = la_out(t)
                    loc = loc[:, 0:HEADS * VAUG].rearrange("p (h v) -> p h v", v=VAUG)
                    lin = lin[:, 0:2 * HEADS * VAUG].rearrange("p (g k h v) -> p g k h v", k=2, h=HG, v=VAUG)
                    dve.wait_ge(LA.out, done[t])
                    dve.wait_ge(LA.qsum, done[t])
                    for k in range(2):
                        dve.tensor_scalar(nrm_c[:, t, 1 + k, :].rearrange("p (g h) -> p g h", h=HG),
                                          lin[:, :, k, :, HD], NORM_MIN, None, ALU.max)
                    dve.scalar_tensor_tensor(out=nrm[:, t, 0, :], in0=qf_sum[:, t, :], scalar=pad_count,
                                             in1=loc[:, :, HD], op0=ALU.mult, op1=ALU.add).then_inc(LA.n_loc, 1)
                    dve.wait_ge(LA.n_loc, done[t])
                    dve.tensor_scalar(nrm_c[:, t, 0, :], nrm[:, t, 0, :], NORM_MIN, None, ALU.max).then_inc(LA.n_max, 1)
                    dve.wait_ge(LA.n_max, done[t])
                    dve.reciprocal(nrm_i[:, t, :, :], nrm_c[:, t, :, :]).then_inc(LA.n_inv, 1)
                    dve.wait_ge(LA.n_inv, done[t])
                    dve.tensor_tensor(nrm_w[:, t, :, :], nrm_i[:, t, :, :],
                                      band_w[:, :].unsqueeze(2).to_broadcast([128, 3, HEADS]), ALU.mult).then_inc(LA.n_w, 1)
                    dve.wait_ge(LA.n_w, done[t])

                    def weigh(dst, src, k, s):
                        dve.tensor_tensor(dst, src, nrm_w[:, t, k, :].unsqueeze(2).to_broadcast([128, HEADS, HD])
                                          if k == 0 else nrm_w[:, t, k, :].rearrange("p (g h) -> p g h", h=HG)
                                          .unsqueeze(3).to_broadcast([128, NHG, HG, HD]), ALU.mult).then_inc(s, 1)

                    weigh(o[:, t, :].rearrange("p (h f) -> p h f", f=HD), loc[:, :, 0:HD], 0, LA.loc)
                    weigh(o_glob[:, t, :].rearrange("p (g h f) -> p g h f", h=HG, f=HD), lin[:, :, 0, :, 0:HD], 1, LA.glob)
                    weigh(o_str[:, t, :].rearrange("p (g h f) -> p g h f", h=HG, f=HD), lin[:, :, 1, :, 0:HD], 2, LA.str)
                    dve.wait_ge(LA.glob, done[t])
                    dve.tensor_tensor(o[:, t, :], o[:, t, :], o_glob[:, t, :], ALU.add).then_inc(LA.sum1, 1)
                    dve.wait_ge(LA.str, done[t])
                    dve.wait_ge(LA.sum1, done[t])
                    dve.tensor_tensor(o[:, t, :], o[:, t, :], o_str[:, t, :], ALU.add).then_inc(LA.sum2, 1)

                mask(0)
                anchor_outputs(0)
                anchor_outputs(1)
                mask(1)
                anchor_outputs(2)
                anchor_outputs(3)
                for t in all_tiles():
                    lay_globals(t)
                mask(2)
                combine(0)
                mask(3)
                combine(1)
                combine(2)
                combine(3)
                norm_stage(LN[3], OUT[2].mm, lambda t: h[:, t, :], OUT[2].added)
                dve.wait_ge(ML.logits, done[GROUP - 1])
                choose(tlg[:, :, 0:EXPERTS], EXPERTS, 1, 1.0, ML)
                biases = dve.snap(i * (EXPERTS * GROUP))
                for e in range(EXPERTS):
                    for t in all_tiles():
                        if e:
                            dve.wait_ge(ML.biased, biases + ((e - 1) * GROUP + t + 1))
                        dve.scalar_tensor_tensor(out=h[:, t, :], in0=b2[:, e, :], scalar=picked[:, t, e:e + 1],
                                                 in1=h[:, t, :], op0=ALU.mult, op1=ALU.add).then_inc(ML.biased, 1)
                for t in all_tiles():
                    dve.wait_ge(ML.outputs, done[t])
                    dve.wait_ge(ML.biased, biases + ((EXPERTS - 1) * GROUP + t + 1))
                    for e in range(EXPERTS):
                        if e:
                            dve.wait_ge((ML.acc0, ML.acc1)[e - 1], done[t])
                        dve.scalar_tensor_tensor(out=h[:, t, :], in0=bank(t, e, D), scalar=picked[:, t, e:e + 1],
                                                 in1=h[:, t, :], op0=ALU.mult, op1=ALU.add)\
                            .then_inc((ML.acc0, ML.acc1, ML.down)[e], 1)


def kernel(**inp):
    import ml_dtypes
    import concourse.bacc as bacc
    from concourse.bass_utils import run_bass_kernel_spmd

    f = {k: np.asarray(v) for k, v in inp.items()}
    one = np.float32

    x = f["x"].reshape(BATCH, CHANNELS, 8, PATCH, 8, PATCH).transpose(0, 1, 2, 4, 3, 5).reshape(TOKENS, D_IN)
    x = np.ascontiguousarray(x.reshape(STEPS, GT, KIN, 128).transpose(0, 3, 2, 1))
    tok_w = f["L0_tok_W"].reshape(D, CHANNELS, 256).transpose(2, 1, 0).reshape(KIN, 128, D).transpose(1, 0, 2)

    def halves(w, bias=None):
        out = np.zeros((HALF + 1, 2, w.shape[1]), one)
        out[0:HALF, 0], out[0:HALF, 1] = w[0:HALF], w[HALF:]
        if bias is not None:
            out[HALF, 1] = bias
        return out

    def by_head(w):
        return w.reshape(w.shape[0], 3, HEADS, HD)

    def softmax_columns(w):
        b = by_head(w)
        v = b[:, 2].reshape(-1, HEADS // 2, 2, HD).transpose(0, 2, 3, 1).reshape(-1, HEADS, HD)
        return np.concatenate([b[:, 0], b[:, 1], v], 1).reshape(w.shape[0], 3 * D)

    def rows_128(w, bias=None):
        out = np.zeros((128, 2, D), one)
        out[:, 0], out[0:64, 1] = w[0:128], w[128:]
        if bias is not None:
            out[64, 1] = bias
        return out

    lora_up = f["L0_ffn_B_lora"].transpose(0, 2, 1).reshape(128, 3 * D)
    gate = np.concatenate([f["L0_ffn_W_gate"].T, f["L0_ffn_A"].reshape(128, D).T], 1)
    gate_b = np.concatenate([f["L0_ffn_b_gate"], np.zeros(128, one)])
    aq = f["L1_attn_anchor_q"].reshape(HEADS, ANCHORS, HD)
    anc_k = np.zeros((128, NHG, AROWS), one)
    anc_km = np.zeros_like(anc_k)
    for g in range(NHG):
        for j in range(HG):
            anc_k[32 * j:32 * j + HD, g, j * ANCHORS:(j + 1) * ANCHORS] = aq[HG * g + j].T
            anc_km[32 * j:32 * j + HD, g, j * ANCHORS:(j + 1) * ANCHORS] = 1.0
    w1 = np.zeros((HALF + 1, 2, EXPERTS, FF), one)
    w1[0:HALF] = f["L1_ffn_W1"].reshape(EXPERTS, 2, HALF, FF).transpose(2, 1, 0, 3)
    w1[HALF, 1] = f["L1_ffn_b1"]

    pos = np.arange(128) % SEQ
    img = np.arange(128) // SEQ
    freq = (1.0 / 10000.0) ** np.linspace(0.0, 1.0, HD // 4, dtype=one)
    theta = (np.tile(np.arange(HEADS, dtype=one), 2)[:, None] * freq[None, :]).astype(one).reshape(-1)
    cst = np.zeros((128, C_END), one)
    cst[:, C_ID:C_ID + 128] = np.eye(128)
    off = pos[:, None] - pos[None, :]
    cst[:, C_BAND:C_BAND + 128] = (off >= -(WINDOW // 2)) & (off < WINDOW - WINDOW // 2) & (img[:, None] == img[None, :])
    cst[:, C_COS:C_SIN], cst[:, C_SIN:C_STRIDE] = np.cos(theta), np.sin(theta)
    cst[:, C_STRIDE] = pos % STRIDE == 0
    cst[:, C_PAD] = np.maximum(WINDOW // 2 - pos, 0) + np.maximum(pos + WINDOW - WINDOW // 2 - SEQ, 0)
    cst[:, C_HEAD:C_HEAD + HG] = np.arange(128)[:, None] // 32 == np.arange(HG)[None, :]
    cst[:, C_TRI:C_TRI + 64] = (np.arange(8)[None, :] < np.arange(8)[:, None]).reshape(64)
    cst[:, C_HALFNEG] = -0.5
    cst[:, C_MEAN:C_MEAN + 128] = (img[:, None] == img[None, :]) / SEQ
    causal = np.where(np.arange(SEQ)[None, :] > pos[:, None], MASKED, 0.0)

    arrays = {
        "x": x, "tok_w": tok_w, "tok_b": np.broadcast_to(f["L0_tok_b"], (128, D)), "cst": cst,
        "qkv_w0": halves(softmax_columns(f["L0_attn_w_qkv"])),
        "qkv_w1": halves(softmax_columns(f["L0_ffn_W_qkv"].T)),
        "qkv_w2": halves(f["L1_attn_qkv_w"].T),
        "out_w0": rows_128(f["L0_attn_w_o"]),
        "out_w1": rows_128(f["L0_ffn_W_proj"].T, f["L0_ffn_b_proj"]),
        "out_w2": rows_128(f["L1_attn_out_w"].T),
        "causal": np.tile(causal, (1, BANK // SEQ)).astype(ml_dtypes.bfloat16), "identb": np.eye(128).astype(ml_dtypes.bfloat16),
        "qkv_b": np.broadcast_to(softmax_columns(f["L0_ffn_b_qkv"][None])[0], (128, 3 * D)),
        "gate_w": halves(gate, gate_b), "lora_up": softmax_columns(lora_up),
        "anc_k": anc_k, "anc_b": anc_k.transpose(2, 1, 0), "anc_km": anc_km, "anc_bm": anc_km.transpose(2, 1, 0),
        "band_w": np.broadcast_to(np.stack([f["L1_attn_w_local"], f["L1_attn_w_global"], f["L1_attn_w_stride"]]), (128, 3)),
        "top_w": halves(np.pad(f["L1_ffn_Wg"].T, ((0, 0), (0, 1)))), "w1": w1.reshape(HALF + 1, 2, EXPERTS * FF),
        "w2": f["L1_ffn_W2"].reshape(EXPERTS, MF, 128, D).transpose(2, 0, 1, 3),
        "b2": np.broadcast_to(f["L1_ffn_b2"], (128, EXPERTS, D)),
    }
    nc = bacc.Bacc("TRN2", target_bir_lowering=False, num_devices=1)
    feed, aps = {}, {}
    for name, v in arrays.items():
        v = np.ascontiguousarray(v)
        feed["in_" + name] = v
        aps[name] = nc.dram_tensor("in_" + name, v.shape, mybir.dt.from_np(v.dtype), kind="ExternalInput").ap()
    aps["out"] = nc.dram_tensor("out_h", (TOKENS // TILE, TILE, D), F32, kind="ExternalOutput").ap()
    build(nc, aps)
    r = run_bass_kernel_spmd(nc, [feed], core_ids=[0])
    return r.results[0]["out_h"].reshape(BATCH, SEQ, D)
```

```python
from contextlib import ExitStack
from collections import namedtuple

import numpy as np
import concourse.bass as bass
from concourse import mybir

F32 = mybir.dt.float32
F32R = mybir.dt.float32r
BF16 = mybir.dt.bfloat16
ALU = mybir.AluOpType
ACT = mybir.ActivationFunctionType
AX = mybir.AxisListType

BATCH, CHANNELS, IMAGE, PATCH = 64, 3, 128, 16
SEQ = (IMAGE // PATCH) ** 2
TOKENS = BATCH * SEQ
D, HEADS = 192, 12
HD = D // HEADS
D_IN = PATCH * PATCH * CHANNELS
KIN = D_IN // 128
TILE = 128
GROUP = 4
GT = GROUP * TILE
STEPS = TOKENS // GT
HALF = D // 2
REST = D - 128
VAUG = HD + 1
LORA_EXPERTS, RANK, LORA_SCALE = 8, 16, 2.0
GATE = LORA_EXPERTS + LORA_EXPERTS * RANK
TERMS = ((0, 0, 128), (1, 1, 128), (2, 0, 128), (0, 2, 128), (1, 3, REST))
WINDOW, STRIDE, ANCHORS = 12, 3, 12
HG = 4
NHG = HEADS // HG
AROWS = HG * ANCHORS
EXPERTS, FF = 3, 768
MF = FF // 128
LN_EPS, NORM_MIN = 1e-5, 1e-6
CHOICE = 11
MASKED = -1e30
BANK = 512

C_ID = 0
C_BAND = C_ID + 128
C_COS = C_BAND + 128
C_SIN = C_COS + 4 * 2 * HEADS
C_STRIDE = C_SIN + 4 * 2 * HEADS
C_PAD = C_STRIDE + 1
C_HEAD = C_PAD + 1
C_TRI = C_HEAD + HG
C_HALFNEG = C_TRI + 64
C_MEAN = C_HALFNEG + 1
C_END = C_MEAN + 128


def build(nc, a):
    ctx = ExitStack()
    with ctx:
        def sb(name, shape, dt=F32):
            return ctx.enter_context(nc.sbuf_tensor(name, shape, dt))

        def sem(name):
            return ctx.enter_context(nc.semaphore(name))

        def sems(prefix, names):
            return namedtuple(prefix.rstrip("_"), names)(*(sem(prefix + n) for n in names.split()))

        tok_w = sb("tok_w", [128, KIN, D])
        tok_b = sb("tok_b", [128, D])
        cst = sb("cst", [128, C_END])
        causal = sb("causal", [128, BANK], BF16)
        identb = sb("identb", [128, 128], BF16)
        qkv_w = [sb(f"qkv_w{i}", [128, 4, 3 * D], F32R) for i in range(3)]
        out_w = [sb(f"out_w{i}", [128, 3 if i == 2 else 2, D]) for i in range(3)]
        gate_w = sb("gate_w", [128, 4, GATE], F32R)
        qkv_b = sb("qkv_b", [128, 3 * D])
        lora_up = sb("lora_up", [128, 3 * D])
        anc_k = sb("anc_k", [128, NHG, AROWS])
        anc_b = sb("anc_b", [AROWS, NHG, 128])
        gate_b = sb("gate_b", [128, LORA_EXPERTS])
        b1 = sb("b1", [128, EXPERTS * MF])
        band_w = sb("band_w", [128, 3])
        band_s = sb("band_s", [128, 4])
        w1 = sb("w1", [128, 4, EXPERTS * FF], F32R)
        w2 = sb("w2", [128, EXPERTS, MF, D])
        b2 = sb("b2", [128, EXPERTS, D])
        top_w = sb("top_w", [128, 4, 4], F32R)

        ident = cst[:, C_ID:C_ID + 128]
        band = cst[:, C_BAND:C_BAND + 128]
        cos = cst[:, C_COS:C_SIN].rearrange("p (u f) -> p u f", f=4)
        sin = cst[:, C_SIN:C_STRIDE].rearrange("p (u f) -> p u f", f=4)
        stride_rows = cst[:, C_STRIDE:C_STRIDE + 1]
        pad_count = cst[:, C_PAD:C_PAD + 1]
        head_rows = cst[:, C_HEAD:C_HEAD + HG]
        tri = cst[:, C_TRI:C_TRI + 64].rearrange("p (n m) -> p n m", n=8)
        image_mean = cst[:, C_MEAN:C_MEAN + 128]
        half_neg = cst[:, C_HALFNEG:C_HALFNEG + 1]

        x_or_kv = sb("x_or_kv", [128, GROUP * 2 * 2 * HEADS * VAUG])
        emb = sb("emb", [128, GROUP, D])
        h = sb("h", [128, GROUP, D])
        ln = sb("ln", [128, GROUP, D])
        stats = sb("stats", [128, GROUP, 6])
        mean_var = sb("mean_var", [128, GROUP, 2])
        scrap = sb("scrap", [128, 2])
        neg_mr = sb("neg_mr", [128, GROUP])
        var_eps = sb("var_eps", [128, GROUP])
        rstd = sb("rstd", [128, GROUP])
        ln_t = sb("ln_t", [128, 3, GT], F32R)
        qk = sb("qk", [128, GROUP, 2 * HEADS, 32])
        arena = sb("arena", [128, 3 * EXPERTS * MF // 3 * GT])
        vals = sb("vals", [128, GROUP, 2, 2, HALF])
        row_max = sb("row_max", [128, GROUP, HEADS])
        row_sum = sb("row_sum", [128, GROUP, HEADS])
        row_inv = sb("row_inv", [128, GROUP, HEADS])
        o_t = sb("o_t", [128, 2, GT])
        spare = sb("spare", [128, GROUP * (GATE + 256)])
        lgt = sb("lgt", [128, GROUP, 8])
        lgt_m = sb("lgt_m", [128, GROUP])
        lgt_s = sb("lgt_s", [128, GROUP])
        lgt_i = sb("lgt_i", [128, GROUP])
        rank = sb("rank", [128, GROUP, 8])
        picked = sb("picked", [128, GROUP, 8])
        vcat = sb("vcat", [128, GROUP, 2, HEADS, VAUG])
        kvc = sb("kvc", [128, GROUP, NHG, 2, VAUG])
        ao = sb("ao", [AROWS, GROUP, 2 * NHG, VAUG])
        ao_n = sb("ao_n", [AROWS, GROUP, 2 * NHG])
        ao_i = sb("ao_i", [AROWS, GROUP, 2 * NHG])
        nrm = sb("nrm", [128, GROUP, HEADS])
        nrm_i = sb("nrm_i", [128, GROUP, HEADS])
        lin_n = sb("lin_n", [128, GROUP, 2, HEADS])
        lin_i = sb("lin_i", [128, GROUP, 2, HEADS])
        tok_lg = sb("tok_lg", [128, GROUP, 4])
        tlg = sb("tlg", [128, GROUP, 4])

        x_t = x_or_kv[:, 0:KIN * GT].rearrange("p (k n) -> p k n", k=KIN)
        kvb = x_or_kv[:, :].rearrange("p (t b g k h v) -> p t b g k h v", t=GROUP, b=2, g=NHG, k=2, h=HG)
        ln_s = spare[:, 0:GROUP * 2 * D].rearrange("p (t s n) -> p t s n", t=GROUP, s=2)
        gates = spare[:, 0:GROUP * GATE].rearrange("p (t n) -> p t n", t=GROUP)
        down = spare[:, GROUP * GATE:GROUP * (GATE + 128)].rearrange("p (t n) -> p t n", t=GROUP)
        down_t = spare[:, GROUP * (GATE + 128):].rearrange("p (t n) -> p t n", t=GROUP)
        padded = spare[:, 0:GROUP * 2 * D].rearrange("p (t u n) -> p t u n", t=GROUP, n=32)
        v_tok = q_window = o_str = ln
        above, ties = (ln[:, :, :].rearrange("p t n -> p (t n)")[:, n * GROUP * 64:(n + 1) * GROUP * 64]
                       .rearrange("p (t n m) -> p t n m", t=GROUP, n=8) for n in range(2))

        BLOCKS = 2 * HEADS * SEQ
        q_t = arena[:, 0:2 * NHG * TILE].rearrange("p (s g n) -> p s g n", s=2, g=NHG)
        k_blk = arena[:, 768:768 + 2 * BLOCKS].rearrange("p (s b g n) -> p s b g n", s=2, b=2, g=NHG)
        prob = arena[:, 3840:3840 + GROUP * 768].rearrange("p (g n) -> p g n", g=GROUP)
        prob_t = arena[:, 6912:6912 + 2 * 768].rearrange("p (s c n) -> p s c n", s=2, c=6)
        qk_t = arena[:, 0:GROUP * 6 * TILE].rearrange("p (g c n) -> p g c n", g=GROUP, c=6)
        q_blk = arena[:, 3072:6144].rearrange("p (s g n) -> p s g n", s=2, g=NHG)
        loc_t = arena[:, 6144:9216].rearrange("p (s h n) -> p s h n", s=2, h=HEADS)
        fe = arena[:, 3072:3072 + GROUP * 2 * D].rearrange("p (g n) -> p g n", g=GROUP)
        fr = arena[:, 3072 + GROUP * 2 * D:3072 + GROUP * 4 * D].rearrange("p (g n) -> p g n", g=GROUP)
        bands_t = arena[:, 3072:3072 + NHG * GT].rearrange("p (g n) -> p g n", g=NHG)
        hid = arena[:, :].rearrange("p (u n) -> p u n", u=EXPERTS * MF)

        QK_AT = 2 * EXPERTS * FF
        w1_raw = arena[:, 0:QK_AT].rearrange("p (c n) -> p c n", c=2)
        qkv_raw = [arena[:, QK_AT + i * 6 * D:QK_AT + (i + 1) * 6 * D].rearrange("p (c n) -> p c n", c=2)
                   for i in range(3)]
        GATE_AT = QK_AT + 18 * D
        gate_raw = arena[:, GATE_AT:GATE_AT + 2 * GATE].rearrange("p (c n) -> p c n", c=2)
        TOP_AT = GATE_AT + 2 * GATE
        top_raw = arena[:, TOP_AT:TOP_AT + 8].rearrange("p (c n) -> p c n", c=2)
        ANC_AT = TOP_AT + 8
        anc_km = arena[:, ANC_AT:ANC_AT + NHG * AROWS].rearrange("p (g n) -> p g n", g=NHG)
        BM_AT = ANC_AT + NHG * AROWS
        anc_bm = arena[0:AROWS, BM_AT:BM_AT + NHG * 128].rearrange("p (g n) -> p g n", g=NHG)
        anc_ke = spare[:, 0:NHG * AROWS].rearrange("p (g n) -> p g n", g=NHG)
        anc_be = spare[0:AROWS, 144:144 + NHG * 128].rearrange("p (g n) -> p g n", g=NHG)
        rot_a = spare[:, 528:720].rearrange("p (u s f) -> p u s f", s=2, f=4)
        rot_b = spare[:, 720:912].rearrange("p (u s f) -> p u s f", s=2, f=4)
        split_w = [(qkv_raw[1], qkv_w[1]), (gate_raw, gate_w), (qkv_raw[2], qkv_w[2]), (qkv_raw[0], qkv_w[0])] \
            + [(w1_raw[:, :, n:n + FF], w1[:, :, n:n + FF]) for n in range(0, EXPERTS * FF, FF)] + [(top_raw, top_w)]

        ps = [ctx.enter_context(nc.psum_tensor(f"ps{i}", [128, 4 * BANK], F32)) for i in range(2)]

        def slot(n, cols):
            return ps[n // 2][:, n % 2 * 2 * BANK:n % 2 * 2 * BANK + cols]

        def steps(count):
            return [count + t + 1 for t in range(GROUP)]

        def tok_bank(t):
            at = 3 * BANK + t // 2 * D
            return ps[t % 2][:, at:at + D]

        def norm_bank(s, t):
            return ps[t % 2][:, (3 if s is LN[0] else t // 2 * 2) * BANK:][:, 0:3 * TILE]

        def lora_bank(t, k, n):
            at = (t // 2 * 2 + k) * BANK
            return ps[t % 2][:, at:at + n]

        def window_bank(t):
            at = 3 * BANK + t // 2 * D
            return ps[t % 2][:, at:at + D]

        def q_bank(t):
            at = (0, 0, 3, 3)[t] * BANK
            return ps[t % 2][:, at:at + NHG * TILE]

        def lin_bank(t):
            return ps[0 if t == 0 else 1][:, 3 * BANK:3 * BANK + 2 * HEADS * VAUG]

        def bands_bank(t):
            at = (3, 3, 0, 0)[t] * BANK
            return ps[(0, 0, 0, 1)[t]][:, at:at + NHG * TILE]

        anchor_bank = ps[0][0:AROWS, 3 * BANK:3 * BANK + GROUP * 2 * NHG * VAUG]
        global_bank = ps[1][:, 3 * BANK:3 * BANK + GROUP * 2 * NHG * VAUG]

        x_loaded, tok_w_loaded, weights_loaded, mlp_w_loaded, unsplit_loaded, stored = (
            sem(n) for n in "x_loaded tok_w_loaded weights_loaded mlp_w_loaded unsplit_loaded stored".split())
        setup = sem("setup")
        setup_anchor_exp, setup_anchor_relu = sem("setup_anchor_exp"), sem("setup_anchor_relu")
        rotated = sem("rotated")
        setup_dve, setup_band_exp = sem("setup_dve"), sem("setup_band_exp")
        tok_mm, embedded = sem("tok_mm"), sem("embedded")
        LN = [sems(f"ln{i}_", "stats aggr eps rstd shift high full split turned copied") for i in range(4)]
        AT = [sems(f"at{i}_", "qkv copied laid turned q_copied k_laid scores max shifted exp sums inv normed "
                              "probs_turned probs_copied av") for i in range(2)]
        w_high, w_low = sem("w_high"), sem("w_low")
        OUT = [sems(f"out{i}_", "turned copied mm added") for i in range(3)]
        RT = sems("route_", "mm copied biased chain shifted exp down turned turned_copied")
        LA = sems("la_", "qkv relu copied strided heads turned turned_copied window multiplied n_sum n_max n_inv n_w "
                         "scaled blocks_turned blocks local local_masked kv kvb kvc anchors anchor_n anchor_i ao "
                         "globals gbd lin l_max l_inv l_w glob str sum")
        ML = sems("ml_", "gate gathered mean logits chain shifted exp biased acc0 acc1 up gelu outputs down")

        block = ctx.enter_context(nc.Block())
        N_W, N_UNSPLIT = 10, 11

        @block.sync
        def _(sp):
            sp.dma_start(x_t, a["x"][0]).then_inc(x_loaded, 16)
            sp.dma_start(tok_w[:, :, :], a["tok_w"]).then_inc(tok_w_loaded, 16)
            sp.dma_start(tok_b[:, :], a["tok_b"]).then_inc(tok_w_loaded, 16)
            sp.dma_start(cst[:, :], a["cst"]).then_inc(weights_loaded, 16)
            for dst, src in ([(qkv_raw[i], f"qkv_w{i}") for i in (1, 2, 0)]
                             + [(gate_raw, "gate_w"), (anc_k[:, :, :], "anc_k"), (anc_b[:, :, :], "anc_b"),
                                (band_w[:, :], "band_w"), (anc_km, "anc_km"), (anc_bm, "anc_bm")]):
                sp.dma_start(dst, a[src]).then_inc(weights_loaded, 16)
            for dst, src in ((w1_raw, "w1"), (top_raw, "top_w")):
                sp.dma_start(dst, a[src]).then_inc(mlp_w_loaded, 16)
            for dst, src in ([(causal[:, :], "causal"), (identb[:, :], "identb")]
                             + [(out_w[i][:, :, :], f"out_w{i}") for i in range(3)]
                             + [(gate_b[:, :], "gate_b"), (lora_up[:, :], "lora_up"), (qkv_b[:, :], "qkv_b"),
                                (b1[:, :], "b1"), (w2[:, :, :, :], "w2"), (b2[:, :, :], "b2")]):
                sp.dma_start(dst, a[src]).then_inc(unsplit_loaded, 16)

            def step(i, last):
                for s in AT:
                    sp.wait_ge(s.copied, i * GROUP + GROUP)
                    for b in range(2):
                        for e in range(2):
                            sp.dma_start(vals[64 * e:64 * e + 64, :, b, e, :],
                                         v_tok[64 * b:64 * b + 64, :, e * HALF:(e + 1) * HALF]).then_inc(s.laid, 16)
                if not last:
                    sp.wait_ge(LA.lin, i * GROUP + GROUP)
                    sp.dma_start(x_t, a["x"][bass.ds(i + 1, 1)].rearrange("o p k n -> (o p) k n")).then_inc(x_loaded, 16)
                for t in range(GROUP):
                    sp.wait_ge(ML.down, i * GROUP + (t + 2))
                    sp.dma_start(a["out"][bass.ds(i * GROUP + t, 1)].rearrange("o p n -> (o p) n"),
                                 h[:, t, :]).then_inc(stored, 16)

            with sp.Fori(0, STEPS - 1) as i:
                step(i, False)
            step(STEPS - 1, True)
            sp.wait_ge(stored, 16 * STEPS * GROUP + 16)

        @block.tensor
        def _(pe):
            def bank(t, k, n=BANK):
                return ps[t % 2][:, k * BANK:k * BANK + n]

            def tok(t):
                return slice(t * TILE, (t + 1) * TILE)

            def products(dst, act_cols, w, w_cols, stop=True):
                for n, (x_c, w_c, rows) in enumerate(TERMS):
                    mm = pe.matmul(dst, ln_t[0:rows, x_c, act_cols], w[0:rows, w_c, w_cols], start=(n == 0),
                                   stop=stop and n == len(TERMS) - 1)
                return mm

            def turn_heads(dst, t):
                for c in range(6):
                    mm = pe.transpose(dst[:, c // NHG * BANK + c % NHG * TILE:][:, 0:TILE],
                                      qk[:, t, 4 * c:4 * c + 4, :].rearrange("p a b -> p (a b)"), ident)
                return mm

            def attention(s, o_s, out_wt, causal_mask, bias_row, laid):
                def turn(t):
                    pe.wait_ge(s.copied, done[t])
                    if t >= 2:
                        pe.wait_ge(s.q_copied, done[t - 2])
                        if t == 2:
                            pe.wait_ge(s.k_laid, done[3])
                    else:
                        pe.wait_ge(s.copied, done[2])
                    turn_heads(slot(t % 2, 2 * BANK), t).then_inc(s.turned, 1)

                def scores(t):
                    dst = slot(2 + t % 2, HEADS * SEQ)
                    pe.wait_ge(s.q_copied, done[t])
                    if t == 0:
                        pe.wait_ge(s.k_laid, done[3])
                    pe.wait_ge(*(s.shifted, done[t - 2]) if t >= 2 else (s.copied, done[3]))
                    if causal_mask:
                        for n in (0, BANK):
                            cols = slice(n, min(n + BANK, HEADS * SEQ))
                            pe.matmul(dst[:, cols], identb[:, :], causal[:, 0:cols.stop - n], start=True, stop=False,
                                      skip_group_check=True)
                    for g in range(NHG):
                        for b in range(2):
                            mm = pe.matmul(dst[64 * b:64 * b + 64, g * HG * SEQ:(g + 1) * HG * SEQ],
                                           q_t[:, t % 2, g, b * SEQ:(b + 1) * SEQ], k_blk[:, t % 2, b, g, :],
                                           start=not causal_mask, stop=True, skip_group_check=True)
                    mm.then_inc(s.scores, 1)

                def turn_probs(t):
                    dst = slot(t % 2, 6 * TILE)
                    pe.wait_ge(s.normed, done[t])
                    pe.wait_ge(*(s.probs_copied, done[t - 2]) if t >= 2 else (s.q_copied, done[t + 2]))
                    for c in range(6):
                        mm = pe.transpose(dst[:, c * TILE:(c + 1) * TILE], prob[:, t, c * TILE:(c + 1) * TILE], ident)
                    mm.then_inc(s.probs_turned, 1)

                def weigh_values(t):
                    dst = slot(2 + t % 2, 2 * TILE)
                    pe.wait_ge(s.probs_copied, done[t])
                    pe.wait_ge(*(o_s.copied, done[t - 2]) if t >= 2 else (s.shifted, done[t + 2]))
                    if t == 0:
                        pe.wait_ge(s.laid, laid)
                    for c in range(6):
                        at = 32 * (c % HG)
                        for b in range(2):
                            mm = pe.matmul(dst[at:at + 32, c // HG * TILE + b * SEQ:c // HG * TILE + (b + 1) * SEQ],
                                           vals[:, t, b, :, :].rearrange("p e n -> p (e n)")[:, c::HEADS // 2],
                                           prob_t[:, t % 2, c, b * SEQ:(b + 1) * SEQ],
                                           start=True, stop=True, skip_group_check=True)
                    mm.then_inc(s.av, 1)

                turn(0)
                turn(1)
                scores(0)
                turn(2)
                scores(1)
                turn(3)
                scores(2)
                scores(3)
                turn_probs(0)
                turn_probs(1)
                weigh_values(0)
                weigh_values(1)
                turn_probs(2)
                turn_probs(3)
                weigh_values(2)
                project(0, o_s, out_wt, bias_row)
                project(1, o_s, out_wt, bias_row)
                weigh_values(3)
                project(2, o_s, out_wt, bias_row)
                project(3, o_s, out_wt, bias_row)

            def project(t, o_s, out_wt, bias_row):
                pe.wait_ge(o_s.copied, done[t])
                if t >= 2:
                    pe.wait_ge(o_s.added, done[t - 2])
                rows = slice(0, 65 if bias_row else 64)
                pe.matmul(bank(t, 1, D), o_t[:, 0, tok(t)], out_wt[:, 0, :], start=True, stop=False)
                pe.matmul(bank(t, 1, D), o_t[rows, 1, tok(t)], out_wt[rows, 1, :],
                          start=False, stop=True).then_inc(o_s.mm, 1)

            def norm_stage(s, work, between=None):
                if s is LN[0]:
                    pe.wait_ge(embedded, done[3])
                for p in (0, 2):
                    for t in (p, p + 1):
                        pe.wait_ge(s.split, done[t])
                        for c in range(3):
                            mm = pe.transpose(norm_bank(s, t)[:, c * TILE:(c + 1) * TILE],
                                              ln_s[:, t, :, :].rearrange("p s n -> p (s n)")[:, c * 128:(c + 1) * 128],
                                              ident)
                        mm.then_inc(s.turned, 1)
                    if between:
                        between(p)
                    for t in (p, p + 1):
                        pe.wait_ge(s.copied, done[t])
                        work(t)

            def project_qkv(s, w, mlp_done=None):
                def work(t):
                    if t == 0 and mlp_done is not None:
                        pe.wait_ge(ML.down, mlp_done)
                    if t >= 2:
                        pe.wait_ge(s.copied, done[t - 2])
                    products(bank(t, 0, 2 * D), tok(t), w, slice(0, 2 * D))
                    if s is LA and t < 2:
                        pe.wait_ge(OUT[1].added, done[t + 2])
                    products(bank(t, 1, D), tok(t), w, slice(2 * D, 3 * D)).then_inc(s.qkv, 1)
                return work

            def tokens(t):
                for k in range(KIN):
                    mm = pe.matmul(tok_bank(t), x_t[:, k, tok(t)], tok_w[:, k, :], start=(k == 0), stop=(k == KIN - 1),
                                   skip_group_check=True)
                if t == GROUP - 1:
                    mm.then_inc(tok_mm, GROUP)

            done = [0] * GROUP

            def step(i, last):
                at = (lambda count: count) if last else pe.snap
                done[:] = [at(count) for count in steps(i * GROUP)]
                laid = at(i * 64 + 64)
                norm_stage(LN[0], project_qkv(AT[0], qkv_w[0], at(i * GROUP + 1)))
                attention(AT[0], OUT[0], out_w[0], True, False, laid)
                def base_qk(t):
                    products(lora_bank(t, 0, 2 * D), tok(t), qkv_w[1], slice(0, 2 * D), stop=False)

                def base_v(t):
                    products(lora_bank(t, 1, D), tok(t), qkv_w[1], slice(2 * D, 3 * D), stop=False)

                def route(t):
                    if t >= 2:
                        pe.wait_ge(RT.copied, done[t - 2])
                    products(bank(t, 3, GATE), tok(t), gate_w, slice(0, GATE)).then_inc(RT.mm, 1)
                    if t == 1:
                        base_qk(0)
                        base_qk(1)

                norm_stage(LN[1], route)
                pe.wait_ge(OUT[0].added, done[3])
                base_v(0)
                base_v(1)
                base_qk(2)
                pe.wait_ge(RT.copied, done[3])
                base_v(2)
                for t in range(GROUP):
                    pe.wait_ge(RT.down, done[t])
                    mm = pe.transpose(ps[1][:, 3 * BANK + t * TILE:3 * BANK + (t + 1) * TILE], down[:, t, :], ident)
                mm.then_inc(RT.turned, GROUP)
                base_qk(3)
                pe.wait_ge(RT.turned_copied, done[3])
                base_v(3)
                for t in range(GROUP):
                    pe.matmul(lora_bank(t, 0, 2 * D), down_t[:, t, :], lora_up[:, 0:2 * D], start=False, stop=True)
                    pe.matmul(lora_bank(t, 1, D), down_t[:, t, :], lora_up[:, 2 * D:], start=False,
                              stop=True).then_inc(AT[1].qkv, 1)
                attention(AT[1], OUT[1], out_w[1], False, True, laid)
                norm_stage(LN[2], project_qkv(LA, qkv_w[2]))
                for t in range(GROUP):
                    pe.wait_ge(LA.heads, done[t])
                    pe.wait_ge(*(LA.turned_copied, done[t - 2]) if t >= 2 else (LA.copied, done[t + 2]))
                    turn_heads(ps[t % 2], t).then_inc(LA.turned, 1)
                    if t == 1:
                        pe.wait_ge(LA.heads, done[3])
                        for n in range(GROUP):
                            mm = pe.matmul(window_bank(n), band, qk[:, n, HEADS:, 0:HD], start=True, stop=True,
                                           skip_group_check=True)
                        mm.then_inc(LA.window, GROUP)

                def keys_values(t):
                    pe.wait_ge(LA.strided, done[t])
                    pe.wait_ge(*(LA.kvb, done[t - 2]) if t >= 2 else (LA.multiplied, done[t + 2]))
                    for g in range(NHG):
                        for b in range(2):
                            r = slice(64 * b, 64 * b + 64)
                            mm = pe.matmul(bank(t, 2 + b)[:, g * 136:(g + 1) * 136],
                                           qk[r, t, HEADS + HG * g:HEADS + HG * (g + 1), :].rearrange("p a b -> p (a b)"),
                                           vcat[r, t, :, HG * g:HG * (g + 1), :].rearrange("p k h v -> p k (h v)"),
                                           start=True, stop=True, skip_group_check=True)
                    mm.then_inc(LA.kv, 1)

                def turn_scaled(t):
                    pe.wait_ge(LA.scaled, done[t])
                    pe.wait_ge(*(LA.kvb, done[t]) if t >= 2 else (LA.turned_copied, done[t + 2]))
                    for g in range(NHG):
                        mm = pe.transpose(q_bank(t)[:, g * TILE:(g + 1) * TILE],
                                          padded[:, t, HG * g:HG * (g + 1), :].rearrange("p a b -> p (a b)"), ident)
                    mm.then_inc(LA.blocks_turned, 1)

                def local(t):
                    pe.wait_ge(LA.turned_copied, done[t])
                    pe.wait_ge(LA.blocks, done[t])
                    pe.wait_ge(*(LA.local_masked, done[t - 2]) if t >= 2 else (LA.kvb, done[t + 2]))
                    for g in range(NHG):
                        mm = pe.matmul(bank(t, g), qk_t[:, t, NHG + g, :], q_blk[:, t % 2, g, :], start=True, stop=True)
                    mm.then_inc(LA.local, 1)

                def anchors():
                    pe.wait_ge(LA.kvc, done[3])
                    pe.wait_ge(LA.blocks, done[2])
                    for t in range(GROUP):
                        for g in range(NHG):
                            at = (t * NHG + g) * 34
                            mm = pe.matmul(anchor_bank[:, at:at + 34], anc_k[:, g, :],
                                           kvc[:, t, g, :, :].rearrange("p b v -> p (b v)"),
                                           start=True, stop=True, skip_group_check=True)
                    mm.then_inc(LA.anchors, GROUP)

                def global_states():
                    pe.wait_ge(LA.ao, done[3])
                    pe.wait_ge(LA.blocks, done[3])
                    for t in range(GROUP):
                        for g in range(NHG):
                            at = (t * NHG + g) * 34
                            mm = pe.matmul(global_bank[:, at:at + 34], anc_b[:, g, :],
                                           ao[:, t, 2 * g:2 * g + 2, :].rearrange("p b v -> p (b v)"),
                                           start=True, stop=True, skip_group_check=True)
                    mm.then_inc(LA.globals, GROUP)

                def anchored_strided(t):
                    pe.wait_ge(LA.gbd, done[0 if t == 0 else 3])
                    if t >= 2:
                        pe.wait_ge(LA.str, done[t - 1])
                    for g in range(NHG):
                        for b in range(2):
                            mm = pe.matmul(lin_bank(t)[64 * b:64 * b + 64, g * 136:(g + 1) * 136],
                                           qk_t[:, t, g, b * SEQ:(b + 1) * SEQ],
                                           kvb[:, t, b, g, :, :, :].rearrange("p k h v -> p (k h v)"),
                                           start=True, stop=True, skip_group_check=True)
                    mm.then_inc(LA.lin, 1)

                def three_bands(t):
                    pe.wait_ge(LA.sum, done[t])
                    pe.wait_ge(LA.local_masked, done[t])
                    if t == 1:
                        pe.wait_ge(OUT[2].copied, done[0])
                    for g in range(NHG):
                        cols = slice(g * TILE, (g + 1) * TILE)
                        pe.matmul(bands_bank(t)[:, cols], padded[:, t, HG * g:HG * (g + 1), :].rearrange("p a b -> p (a b)"),
                                  ident, start=True, stop=False, skip_group_check=True)
                        for j in range(HG):
                            mm = pe.matmul(bands_bank(t)[32 * j:32 * j + HD, cols], vcat[:, t, 0, HG * g + j, 0:HD],
                                           loc_t[:, t % 2, HG * g + j, :], start=False, stop=(j == HG - 1),
                                           skip_group_check=True)
                    mm.then_inc(OUT[2].turned, 1)

                def project_bands(t):
                    pe.wait_ge(OUT[2].copied, done[t])
                    pe.wait_ge(*(OUT[2].added, done[t - 2]) if t >= 2 else (LA.local_masked, done[t + 2]))
                    for g in range(NHG):
                        mm = pe.matmul(bank(t, 1, D), bands_t[:, g, tok(t)], out_w[2][:, g, :], start=(g == 0),
                                       stop=(g == NHG - 1))
                    mm.then_inc(OUT[2].mm, 1)

                keys_values(0)
                keys_values(1)
                keys_values(2)
                turn_scaled(0)
                turn_scaled(1)
                keys_values(3)
                local(0)
                turn_scaled(2)
                turn_scaled(3)
                local(1)
                anchors()
                local(2)
                global_states()
                local(3)
                anchored_strided(0)
                anchored_strided(1)
                three_bands(0)
                anchored_strided(2)
                three_bands(1)
                anchored_strided(3)
                three_bands(2)
                project_bands(0)
                project_bands(1)
                three_bands(3)
                project_bands(2)
                project_bands(3)
                def top_gate(t):
                    if t >= 2:
                        pe.wait_ge(ML.gathered, done[t - 2])
                    products(bank(t, 0, 4), tok(t), top_w, slice(0, 4)).then_inc(ML.gate, 1)

                def tokens_between(p):
                    tokens(p // 2 + 1)

                if not last:
                    pe.wait_ge(x_loaded, at(i * 16 + 32))
                    tokens(0)
                norm_stage(LN[3], top_gate, None if last else tokens_between)
                if not last:
                    tokens(3)
                units = at(i * (EXPERTS * MF))
                for u in range(EXPERTS * MF):
                    if u >= 2:
                        pe.wait_ge(ML.gelu, units + (u - 1))
                    else:
                        pe.wait_ge(ML.gathered, done[u + 2])
                    if u == 2:
                        pe.matmul(bank(0, 1, GROUP * 4), image_mean, tok_lg[:, :, :].rearrange("p t n -> p (t n)"),
                                  start=True, stop=True).then_inc(ML.mean, GROUP)
                    for n, (x_c, w_c, rows) in enumerate(TERMS):
                        mm = pe.matmul(bank(u, 0), w1[0:rows, w_c, u * 128:(u + 1) * 128], ln_t[0:rows, x_c, :],
                                       start=(n == 0), stop=(n == len(TERMS) - 1))
                    mm.then_inc(ML.up, 1)
                pe.wait_ge(ML.gelu, units + EXPERTS * MF)
                for t in range(GROUP):
                    if t >= 2:
                        pe.wait_ge(ML.down, at(i * GROUP + t))
                    for e in range(EXPERTS):
                        for m in range(MF):
                            mm = pe.matmul(bank(t, e, D), hid[:, e * MF + m, tok(t)], w2[:, e, m, :],
                                           start=(m == 0), stop=(m == MF - 1))
                    mm.then_inc(ML.outputs, 1)

            pe.wait_ge(tok_w_loaded, 32)
            pe.wait_ge(x_loaded, 16)
            for t in range(GROUP):
                tokens(t)
            pe.wait_ge(weights_loaded, 16 * N_W)
            pe.wait_ge(unsplit_loaded, 16 * N_UNSPLIT)
            pe.wait_ge(setup, 5)
            pe.wait_ge(w_low, len(split_w))
            pe.wait_ge(setup_dve, 11)
            with pe.Fori(0, STEPS - 1) as i:
                step(i, False)
            step(STEPS - 1, True)

        @block.scalar
        def _(act):
            def bank(t, k, n=BANK):
                return ps[t % 2][:, k * BANK:k * BANK + n]

            def tok(t):
                return slice(t * TILE, (t + 1) * TILE)

            def split_high(s, src, pair, done):
                for t in pair:
                    act.wait_ge(s.shift, done[t])
                    act.activation(ln_s[:, t, 0, :].bitcast(F32R), src[:, t, :], ACT.Identity,
                                   bias=neg_mr[:, t:t + 1], scale=rstd[:, t:t + 1]).then_inc(s.high, 1)

            def norm_stage(s, work):
                def copy(pair):
                    for t in pair:
                        act.wait_ge(s.turned, done[t])
                        act.activation(ln_t[:, :, tok(t)], norm_bank(s, t).rearrange("p (c n) -> p c n", c=3),
                                       ACT.Copy).then_inc(s.copied, 1)

                if s is not LN[0]:
                    split_high(s, h, (0, 1), done)
                copy((0, 1))
                if s is not LN[0]:
                    split_high(s, h, (2, 3), done)
                work(0)
                work(1)
                copy((2, 3))
                work(2)
                work(3)

            def copy_out(t, src, ready, copied):
                act.wait_ge(ready, done[t])
                act.activation(o_t[:, 0, tok(t)], src[:, 0:TILE], ACT.Copy)
                act.activation(o_t[0:64, 1, tok(t)], src[0:64, TILE:2 * TILE], ACT.Copy).then_inc(copied, 1)

            def attention(s, o_s):
                def copy_q(t):
                    act.wait_ge(s.turned, done[t])
                    if t >= 2:
                        act.wait_ge(s.scores, done[t - 2])
                    op = act.activation(q_t[:, t % 2, :, :].rearrange("p g n -> p (g n)"), slot(t % 2, NHG * TILE),
                                   ACT.Copy)
                    if t == 0:
                        op.then_inc(s.q_copied, 1)
                        return
                    for j in range(HG):
                        op = act.activation(k_blk[:, t % 2, :, :, j * SEQ:(j + 1) * SEQ].rearrange("p b g n -> p g b n"),
                                            slot(t % 2, 2 * BANK)[:, BANK:BANK + NHG * TILE]
                                            .rearrange("p (g b n) -> p g b n", g=NHG, b=2),
                                            ACT.Copy, scale=head_rows[:, j:j + 1])
                    op.then_inc(s.q_copied, 1)

                def exponentials(t):
                    act.wait_ge(s.shifted, done[t])
                    act.activation(prob[:, t, :], prob[:, t, :], ACT.Exp, scale=HD ** -0.5).then_inc(s.exp, 1)

                def copy_probs(t):
                    act.wait_ge(s.probs_turned, done[t])
                    if t >= 2:
                        act.wait_ge(s.av, done[t - 2])
                    act.activation(prob_t[:, t % 2, :, :].rearrange("p c n -> p (c n)"), slot(t % 2, 6 * TILE),
                                   ACT.Copy).then_inc(s.probs_copied, 1)

                def copy_output(t):
                    copy_out(t, slot(2 + t % 2, 2 * TILE), s.av, o_s.copied)

                copy_q(0)
                copy_q(1)
                copy_q(2)
                exponentials(0)
                copy_q(3)
                exponentials(1)
                copy_probs(0)
                exponentials(2)
                copy_probs(1)
                exponentials(3)
                copy_output(0)
                copy_output(1)
                copy_probs(2)
                copy_probs(3)
                copy_output(2)
                copy_output(3)

            act.wait_ge(weights_loaded, 16 * N_W)
            act.activation(anc_ke, anc_k[:, :, :], ACT.Exp).then_inc(setup_anchor_exp, 1)
            act.activation(anc_be, anc_b[:, :, :], ACT.Exp).then_inc(setup_anchor_exp, 1)
            act.wait_ge(setup_dve, 2)
            act.activation(band_w[:, :], band_w[:, :], ACT.Exp).then_inc(setup_band_exp, 1)
            for raw, w in split_w:
                if raw is qkv_raw[0]:
                    act.wait_ge(rotated, 4)
                if w is split_w[4][1]:
                    act.wait_ge(mlp_w_loaded, 16 * 2)
                act.activation(w[:, 0:2, :], raw, ACT.Copy).then_inc(w_high, 1)
            act.wait_ge(w_low, len(split_w))
            act.wait_ge(setup, 5)
            act.wait_ge(unsplit_loaded, 16 * N_UNSPLIT)
            split_high(LN[0], emb, range(GROUP), steps(0))
            done = [0] * GROUP

            def step(i, last):
                at = (lambda count: count) if last else act.snap
                done[:] = [at(count) for count in steps(i * GROUP)]

                def take_qkv(t):
                    act.wait_ge(AT[0].qkv, done[t])
                    act.activation(qk[:, t, :, 0:HD], bank(t, 0, 2 * D).rearrange("p (u f) -> p u f", f=HD), ACT.Copy)
                    act.activation(v_tok[:, t, :], bank(t, 1, D), ACT.Copy).then_inc(AT[0].copied, 1)

                norm_stage(LN[0], take_qkv)
                attention(AT[0], OUT[0])
                def take_gates(t):
                    act.wait_ge(RT.mm, done[t])
                    act.activation(gates[:, t, :], bank(t, 3, GATE), ACT.Copy).then_inc(RT.copied, 1)

                norm_stage(LN[1], take_gates)
                act.wait_ge(RT.shifted, done[GROUP - 1])
                act.activation(lgt[:, :, :], lgt[:, :, :], ACT.Exp).then_inc(RT.exp, GROUP)
                act.wait_ge(RT.turned, done[3])
                act.activation(down_t.rearrange("p t n -> p (t n)"), ps[1][:, 3 * BANK:],
                               ACT.Copy).then_inc(RT.turned_copied, GROUP)
                attention(AT[1], OUT[1])
                def take_features(t):
                    act.wait_ge(LA.qkv, done[t])
                    act.activation(fe[:, t, :], bank(t, 0, 2 * D), ACT.Exp)
                    act.activation(fr[:, t, :], bank(t, 0, 2 * D), ACT.Relu).then_inc(LA.relu, 1)
                    act.activation(vcat[:, t, 0, :, 0:HD], bank(t, 1, D).rearrange("p (u f) -> p u f", f=HD),
                                   ACT.Copy).then_inc(LA.copied, 1)

                norm_stage(LN[2], take_features)
                for t in range(GROUP):
                    act.wait_ge(LA.turned, done[t])
                    act.activation(qk_t[:, t, :, :].rearrange("p (s g) n -> p s (g n)", s=2),
                                   ps[t % 2][:, 0:2 * BANK].rearrange("p (s n) -> p s n", s=2)[:, :, 0:NHG * TILE],
                                   ACT.Copy).then_inc(LA.turned_copied, 1)
                for t in range(GROUP):
                    act.wait_ge(LA.blocks_turned, done[t])
                    if t >= 2:
                        act.wait_ge(LA.local, done[t - 2])
                    for j in range(HG):
                        op = act.activation(q_blk[:, t % 2, :, j * TILE:(j + 1) * TILE],
                                            q_bank(t).rearrange("p (g n) -> p g n", g=NHG),
                                            ACT.Copy, scale=head_rows[:, j:j + 1])
                    op.then_inc(LA.blocks, 1)
                for t in range(GROUP):
                    act.wait_ge(OUT[2].turned, done[t])
                    act.activation(bands_t[:, :, tok(t)], bands_bank(t).rearrange("p (g n) -> p g n", g=NHG),
                                   ACT.Copy).then_inc(OUT[2].copied, 1)
                def take_top_gates(t):
                    act.wait_ge(ML.gate, done[t])
                    act.activation(tok_lg[:, t, :], bank(t, 0, 4), ACT.Copy).then_inc(ML.gathered, 1)

                norm_stage(LN[3], take_top_gates)
                units = at(i * (EXPERTS * MF))
                for u in range(EXPERTS * MF):
                    act.wait_ge(ML.up, units + (u + 1))
                    act.activation(hid[:, u, :], bank(u, 0), ACT.Gelu, bias=b1[:, u:u + 1]).then_inc(ML.gelu, 1)
                    if u == 1:
                        act.wait_ge(ML.mean, done[3])
                        act.activation(tlg[:, :, :].rearrange("p t n -> p (t n)"), bank(0, 1, GROUP * 4),
                                       ACT.Copy).then_inc(ML.logits, GROUP)
                    if u == 4:
                        act.wait_ge(ML.shifted, done[3])
                        act.activation(lgt[:, :, 0:EXPERTS], lgt[:, :, 0:EXPERTS], ACT.Exp).then_inc(ML.exp, GROUP)
                if not last:
                    split_high(LN[0], emb, range(GROUP), [at(count) for count in steps(i * GROUP + GROUP)])

            with act.Fori(0, STEPS - 1) as i:
                step(i, False)
            step(STEPS - 1, True)

        @block.gpsimd
        def _(pool):
            margins = ((o_t[64:65, 1, :], 1.0), (qk[:, :, :, HD:32], 0.0),
                       (vals[:, :, :, :, :], 0.0), (vcat[:, :, 0, :, HD:VAUG], 1.0), (ao[:, :, :, HD:VAUG], 1.0))
            for n, (margin, value) in enumerate(margins):
                if n:
                    pool.wait_ge(setup, n)
                pool.memset(margin, value).then_inc(setup, 1)
            pool.wait_ge(weights_loaded, 16 * N_W)
            pool.wait_ge(setup, 5)

            def root(s, done):
                for p in range(0, GROUP, 2):
                    pool.wait_ge(s.eps, done[p + 1])
                    pool.tensor_tensor(rstd[:, p:p + 2], var_eps[:, p:p + 2], half_neg.to_broadcast([128, 2]),
                                       ALU.pow).then_inc(s.rstd, 2)

            def divide(s):
                for t in range(GROUP - 2):
                    weights = prob[:, t, :].rearrange("p (h k) -> p h k", h=HEADS)
                    pool.wait_ge(s.inv, done[t])
                    pool.tensor_tensor(weights, weights, row_inv[:, t, :].unsqueeze(2)
                                       .to_broadcast([128, HEADS, SEQ]), ALU.mult).then_inc(s.normed, 1)

            root(LN[0], steps(0))
            done = [0] * GROUP

            def step(i, last):
                at = (lambda count: count) if last else pool.snap
                done[:] = [at(count) for count in steps(i * GROUP)]
                divide(AT[0])
                root(LN[1], done)
                divide(AT[1])
                root(LN[2], done)
                for t in range(GROUP):
                    pool.wait_ge(LA.copied, done[t])
                    pool.tensor_tensor(vcat[:, t, 1, :, :].rearrange("p h v -> p (h v)"),
                                       vcat[:, t, 0, :, :].rearrange("p h v -> p (h v)"),
                                       stride_rows.to_broadcast([128, HEADS * VAUG]), ALU.mult).then_inc(LA.strided, 1)
                root(LN[3], done)
                if not last:
                    root(LN[0], [at(count) for count in steps(i * GROUP + GROUP)])

            with pool.Fori(0, STEPS - 1) as i:
                step(i, False)
            step(STEPS - 1, True)

        @block.vector
        def _(dve):
            def bank(t, k, n=BANK):
                return ps[t % 2][:, k * BANK:k * BANK + n]

            def all_tiles():
                return range(GROUP)

            def norm_stage(s, mm, psum, src, dst, added, done):
                def add(t):
                    dve.wait_ge(mm, done[t])
                    dve.tensor_tensor(dst[:, t, :], psum(t), src(t), ALU.add).then_inc(added, 1)

                def count(t):
                    dve.wait_ge(added, done[t])
                    dve.bn_stats(stats[:, t, :], dst[:, t, :]).then_inc(s.stats, 1)

                def join(p):
                    for t in (p, p + 1):
                        dve.bn_aggr(mean_var[:, t, :], stats[:, t, :]).then_inc(s.aggr, 1)

                def add_eps(p):
                    dve.wait_ge(s.aggr, done[p + 1])
                    dve.tensor_scalar(var_eps[:, p:p + 2], mean_var[:, p:p + 2, 1], LN_EPS, None,
                                      ALU.add).then_inc(s.eps, 2)

                def shift(p):
                    dve.wait_ge(s.rstd, done[p + 1])
                    dve.scalar_tensor_tensor(out=neg_mr[:, p:p + 2], in0=mean_var[:, p:p + 2, 0], scalar=-1.0,
                                             in1=rstd[:, p:p + 2], op0=ALU.mult, op1=ALU.mult).then_inc(s.shift, 2)

                def normalise(t):
                    dve.tensor_scalar(ln[:, t, :], dst[:, t, :], mean_var[:, t, 0:1], rstd[:, t:t + 1],
                                      ALU.subtract, ALU.mult).then_inc(s.full, 1)

                def low(t):
                    dve.wait_ge(s.high, done[t])
                    dve.wait_ge(s.full, done[t])
                    for dst, src in ((slice(0, REST), slice(128, D)), (slice(REST, D), slice(0, 128))):
                        op = dve.tensor_tensor(ln_s[:, t, 1, dst].bitcast(F32R), ln[:, t, src], ln_s[:, t, 0, src],
                                               ALU.subtract)
                    op.then_inc(s.split, 1)

                for p in (0, 2):
                    add(p)
                    add(p + 1)
                    count(p)
                    count(p + 1)
                    dve.wait_ge(s.stats, done[p + 1])
                    dve.tensor_scalar(scrap[:, :], stats[:, p + 1, 1:3], 1.0, None, ALU.mult)
                    join(p)
                    add_eps(p)
                    shift(p)
                    normalise(p)
                    normalise(p + 1)
                    low(p)
                    low(p + 1)

            def attention(s):
                def lay_k():
                    dve.wait_ge(s.turned, done[0])
                    for b in range(2):
                        cells = [128, NHG, HG, SEQ]
                        k_in = slot(0, 2 * BANK)[:, BANK:BANK + NHG * TILE].rearrange("p (g n) -> p g n", g=NHG)
                        op = dve.tensor_tensor(
                            k_blk[:, 0, b, :, :].rearrange("p g (j n) -> p g j n", j=HG),
                            k_in[:, :, b * SEQ:(b + 1) * SEQ].unsqueeze(2).to_broadcast(cells),
                            head_rows.unsqueeze(1).unsqueeze(3).to_broadcast(cells), ALU.mult)
                    op.then_inc(s.k_laid, GROUP)

                def shift(t):
                    scores = slot(2 + t % 2, HEADS * SEQ).rearrange("p (h k) -> p h k", h=HEADS)
                    dve.wait_ge(s.scores, done[t])
                    dve.tensor_reduce(row_max[:, t, :], scores, AX.X, ALU.max).then_inc(s.max, 1)
                    dve.wait_ge(s.max, done[t])
                    dve.tensor_tensor(prob[:, t, :].rearrange("p (h k) -> p h k", h=HEADS), scores,
                                      row_max[:, t, :].unsqueeze(2).to_broadcast([128, HEADS, SEQ]),
                                      ALU.subtract).then_inc(s.shifted, 1)

                def sums(t):
                    dve.wait_ge(s.exp, done[t])
                    dve.tensor_reduce(row_sum[:, t, :], prob[:, t, :].rearrange("p (h k) -> p h k", h=HEADS),
                                      AX.X, ALU.add).then_inc(s.sums, 1)
                    dve.wait_ge(s.sums, done[t])
                    dve.reciprocal(row_inv[:, t, :], row_sum[:, t, :]).then_inc(s.inv, 1)

                def divide(t):
                    weights = prob[:, t, :].rearrange("p (h k) -> p h k", h=HEADS)
                    dve.wait_ge(s.inv, done[t])
                    if t == 2:
                        dve.wait_ge(s.normed, done[1])
                    dve.tensor_tensor(weights, weights, row_inv[:, t, :].unsqueeze(2).to_broadcast([128, HEADS, SEQ]),
                                      ALU.mult).then_inc(s.normed, 1)

                lay_k()
                shift(0)
                shift(1)
                sums(0)
                shift(2)
                sums(1)
                shift(3)
                sums(2)
                divide(2)
                sums(3)
                divide(3)

            def choose(logits, n, keep, factor, s, at):
                cells = [128, GROUP, n, n]
                lower = tri[:, 0:n, 0:n].unsqueeze(1).to_broadcast(cells)
                rivals = logits.unsqueeze(2).to_broadcast(cells)
                own = logits.unsqueeze(3).to_broadcast(cells)
                n8 = slice(0, n)
                dve.tensor_reduce(lgt_m[:, :], logits, AX.X, ALU.max).then_inc(s.chain, 1)
                dve.tensor_tensor(above[:, :, n8, n8], rivals, own, ALU.is_gt).then_inc(s.chain, 1)
                dve.tensor_tensor(ties[:, :, n8, n8], rivals, own, ALU.is_equal).then_inc(s.chain, 1)
                dve.wait_ge(s.chain, at + 1)
                dve.tensor_tensor(lgt[:, :, n8], logits, lgt_m[:, :].unsqueeze(2).to_broadcast([128, GROUP, n]),
                                  ALU.subtract).then_inc(s.shifted, GROUP)
                dve.wait_ge(s.chain, at + 3)
                dve.tensor_tensor(ties[:, :, n8, n8], ties[:, :, n8, n8], lower, ALU.mult).then_inc(s.chain, 1)
                dve.wait_ge(s.chain, at + 4)
                dve.tensor_tensor(above[:, :, n8, n8], above[:, :, n8, n8], ties[:, :, n8, n8],
                                  ALU.add).then_inc(s.chain, 1)
                dve.wait_ge(s.chain, at + 5)
                dve.tensor_reduce(rank[:, :, n8], above[:, :, n8, n8], AX.X, ALU.add).then_inc(s.chain, 1)
                dve.wait_ge(s.chain, at + 6)
                dve.tensor_scalar(picked[:, :, n8], rank[:, :, n8], keep - 0.5, factor, ALU.is_lt,
                                  ALU.mult).then_inc(s.chain, 1)
                dve.wait_ge(s.exp, done[GROUP - 1])
                dve.tensor_reduce(lgt_s[:, :], lgt[:, :, n8], AX.X, ALU.add).then_inc(s.chain, 1)
                dve.wait_ge(s.chain, at + 7)
                dve.tensor_tensor(picked[:, :, n8], picked[:, :, n8], lgt[:, :, n8], ALU.mult).then_inc(s.chain, 1)
                dve.wait_ge(s.chain, at + 8)
                dve.reciprocal(lgt_i[:, :], lgt_s[:, :]).then_inc(s.chain, 1)
                dve.wait_ge(s.chain, at + 10)
                dve.tensor_tensor(picked[:, :, n8], picked[:, :, n8],
                                  lgt_i[:, :].unsqueeze(2).to_broadcast([128, GROUP, n]), ALU.mult)\
                    .then_inc(s.chain, 1)
                dve.wait_ge(s.chain, at + 11)

            dve.wait_ge(weights_loaded, 16 * N_W)
            for c in range(2):
                pair = qkv_raw[0][:, c, 0:2 * D].rearrange("p (u s f) -> p u s f", s=2, f=HD // 2)[:, :, :, 0:4]
                if c:
                    dve.wait_ge(rotated, 2 * c)
                dve.tensor_tensor(rot_b[:, :, 0, :], pair[:, :, 1, :], sin, ALU.mult)
                dve.tensor_tensor(rot_b[:, :, 1, :], pair[:, :, 0, :], sin, ALU.mult)
                dve.tensor_tensor(rot_a[:, :, 0, :], pair[:, :, 0, :], cos, ALU.mult)
                dve.tensor_tensor(rot_a[:, :, 1, :], pair[:, :, 1, :], cos, ALU.mult).then_inc(rotated, 1)
                dve.wait_ge(rotated, 2 * c + 1)
                dve.tensor_tensor(pair[:, :, 0, :], rot_a[:, :, 0, :], rot_b[:, :, 0, :], ALU.add)
                dve.tensor_tensor(pair[:, :, 1, :], rot_a[:, :, 1, :], rot_b[:, :, 1, :],
                                  ALU.subtract).then_inc(rotated, 1)
            dve.wait_ge(weights_loaded, 16 * N_W)
            dve.tensor_reduce(band_s[:, 0:1], band_w[:, :], AX.X, ALU.max).then_inc(setup_dve, 1)
            dve.wait_ge(setup_dve, 1)
            dve.tensor_scalar(band_w[:, :], band_w[:, :], band_s[:, 0:1], None, ALU.subtract).then_inc(setup_dve, 1)
            dve.wait_ge(setup_anchor_exp, 2)
            for x, e, m in ((anc_k, anc_ke, anc_km), (anc_b, anc_be, anc_bm)):
                n = 3 if x is anc_k else 6
                dve.tensor_scalar(e, e, 1.0, None, ALU.min).then_inc(setup_dve, 1)
                dve.wait_ge(setup_dve, n)
                dve.scalar_tensor_tensor(out=x[:, :, :], in0=x[:, :, :], scalar=0.0, in1=e,
                                         op0=ALU.max, op1=ALU.add).then_inc(setup_dve, 1)
                dve.wait_ge(setup_dve, n + 1)
                dve.tensor_tensor(x[:, :, :], x[:, :, :], m, ALU.mult).then_inc(setup_dve, 1)
            dve.wait_ge(setup_band_exp, 1)
            dve.tensor_reduce(band_s[:, 1:2], band_w[:, :], AX.X, ALU.add).then_inc(setup_dve, 1)
            dve.wait_ge(setup_dve, 9)
            dve.reciprocal(band_s[:, 2:3], band_s[:, 1:2]).then_inc(setup_dve, 1)
            dve.wait_ge(setup_dve, 10)
            dve.tensor_scalar(band_w[:, :], band_w[:, :], band_s[:, 2:3], None, ALU.mult).then_inc(setup_dve, 1)
            dve.wait_ge(setup_dve, 11)
            dve.memset(band_s[:, 3:4], 0.0).then_inc(ML.down, 1)
            dve.memset(band_s[:, 0:1], 0.0).then_inc(stored, 16)
            for n, (raw, w) in enumerate(split_w):
                dve.wait_ge(w_high, n + 1)
                dve.tensor_tensor(w[:, 2:4, :], raw, w[:, 0:2, :].bitcast(F32), ALU.subtract).then_inc(w_low, 1)
            dve.wait_ge(w_low, len(split_w))
            dve.wait_ge(setup, 5)
            dve.wait_ge(tok_w_loaded, 32)

            def embed(done):
                norm_stage(LN[0], tok_mm, tok_bank, lambda t: tok_b[:, :], emb, embedded, done)

            def add_norm(s, o_s, src):
                norm_stage(s, o_s.mm, lambda t: bank(t, 1, D), lambda t: src[:, t, :], h, o_s.added, done)

            embed(steps(0))
            dve.wait_ge(unsplit_loaded, 16 * N_UNSPLIT)
            done = [0] * GROUP

            def step(i, last):
                at = (lambda count: count) if last else dve.snap
                done[:] = [at(count) for count in steps(i * GROUP)]
                attention(AT[0])
                dve.wait_ge(stored, at(i * (16 * GROUP) + 16))
                add_norm(LN[1], OUT[0], emb)
                dve.wait_ge(RT.copied, done[GROUP - 1])
                dve.tensor_tensor(gates[:, :, 0:LORA_EXPERTS], gates[:, :, 0:LORA_EXPERTS],
                                  gate_b[:, :].unsqueeze(1).to_broadcast([128, GROUP, LORA_EXPERTS]),
                                  ALU.add).then_inc(RT.biased, GROUP)
                dve.wait_ge(RT.biased, done[3])
                choose(gates[:, :, 0:LORA_EXPERTS], LORA_EXPERTS, 2, LORA_SCALE, RT, at(i * CHOICE))
                for t in all_tiles():
                    dve.tensor_tensor(down[:, t, :].rearrange("p (n r) -> p n r", r=RANK),
                                      gates[:, t, LORA_EXPERTS:].rearrange("p (n r) -> p n r", r=RANK),
                                      picked[:, t, :].unsqueeze(2).to_broadcast([128, LORA_EXPERTS, RANK]),
                                      ALU.mult).then_inc(RT.down, 1)
                for t in all_tiles():
                    dve.wait_ge(AT[1].qkv, done[t])
                    dve.tensor_tensor(qk[:, t, :, 0:HD], lora_bank(t, 0, 2 * D).rearrange("p (u f) -> p u f", f=HD),
                                      qkv_b[:, 0:2 * D].rearrange("p (u f) -> p u f", f=HD), ALU.add)
                    dve.tensor_tensor(v_tok[:, t, :], lora_bank(t, 1, D), qkv_b[:, 2 * D:], ALU.add).then_inc(AT[1].copied, 1)
                attention(AT[1])
                add_norm(LN[2], OUT[1], h)
                for t in all_tiles():
                    dve.wait_ge(LA.relu, done[t])
                    dve.scalar_tensor_tensor(out=qk[:, t, :, 0:HD], in0=fe[:, t, :].rearrange("p (u f) -> p u f", f=HD),
                                             scalar=1.0, in1=fr[:, t, :].rearrange("p (u f) -> p u f", f=HD),
                                             op0=ALU.min, op1=ALU.add).then_inc(LA.heads, 1)
                dve.wait_ge(LA.window, done[3])
                for t in all_tiles():
                    dve.scalar_tensor_tensor(out=q_window[:, t, :].rearrange("p (h f) -> p h f", f=HD),
                                             in0=window_bank(t).rearrange("p (h f) -> p h f", f=HD), scalar=pad_count,
                                             in1=qk[:, t, 0:HEADS, 0:HD], op0=ALU.add,
                                             op1=ALU.mult).then_inc(LA.multiplied, 1)
                dve.wait_ge(LA.multiplied, done[3])
                dve.tensor_reduce(nrm[:, :, :], q_window[:, :, :].rearrange("p t (h f) -> p t h f", f=HD),
                                  AX.X, ALU.add).then_inc(LA.n_sum, GROUP)

                def lay_states(t):
                    dve.wait_ge(LA.kv, done[t])
                    for b in range(2):
                        op = dve.tensor_tensor(
                            kvb[:, t, b, :, :, :, :].rearrange("p g k h v -> p (g k) h v"),
                            bank(t, 2 + b, 408).rearrange("p (g h v) -> p g h v", h=HG, v=VAUG),
                            head_rows.unsqueeze(1).unsqueeze(3).to_broadcast([128, 2 * NHG, HG, VAUG]), ALU.mult)
                    op.then_inc(LA.kvb, 1)

                def scale(t):
                    dve.tensor_tensor(padded[:, t, :, :], qk[:, t, 0:HEADS, :],
                                      nrm_i[:, t, :].unsqueeze(2).to_broadcast([128, HEADS, 32]),
                                      ALU.mult).then_inc(LA.scaled, 1)

                dve.wait_ge(LA.n_sum, done[3])
                dve.tensor_scalar(nrm[:, :, :], nrm[:, :, :], NORM_MIN, None, ALU.max).then_inc(LA.n_max, GROUP)
                dve.wait_ge(LA.n_max, done[3])
                dve.reciprocal(nrm_i[:, :, :], nrm[:, :, :]).then_inc(LA.n_inv, GROUP)
                lay_states(0)
                dve.wait_ge(LA.n_inv, done[3])
                dve.tensor_scalar(nrm_i[:, :, :], nrm_i[:, :, :], band_w[:, 0:1], None,
                                  ALU.mult).then_inc(LA.n_w, GROUP)
                dve.wait_ge(LA.n_w, done[3])
                scale(0)
                scale(1)
                lay_states(1)
                scale(2)
                scale(3)
                lay_states(2)
                lay_states(3)
                for t in all_tiles():
                    dve.wait_ge(LA.kvb, done[t])
                    for b in range(2):
                        op = dve.tensor_reduce(kvc[:, t, :, b, :],
                                               kvb[:, t, b, :, 0, :, :].rearrange("p g h v -> p g v h"), AX.X, ALU.add)
                    op.then_inc(LA.kvc, 1)

                def mask(t):
                    dve.wait_ge(LA.local, done[t])
                    if t >= 2:
                        dve.wait_ge(OUT[2].turned, done[t - 2])
                    dve.tensor_tensor(loc_t[:, t % 2, :, :],
                                      ps[t % 2][:, 0:HEADS * TILE].rearrange("p (h n) -> p h n", h=HEADS),
                                      band.unsqueeze(1).to_broadcast([128, HEADS, TILE]),
                                      ALU.mult).then_inc(LA.local_masked, 1)

                def anchor_outputs():
                    anc = anchor_bank.rearrange("p (t u v) -> p t u v", t=GROUP, v=VAUG)
                    dve.wait_ge(LA.anchors, done[3])
                    dve.tensor_scalar(ao_n[:, :, :], anc[:, :, :, HD], NORM_MIN, None, ALU.max).then_inc(LA.anchor_n, GROUP)
                    dve.wait_ge(LA.anchor_n, done[3])
                    dve.reciprocal(ao_i[:, :, :], ao_n[:, :, :]).then_inc(LA.anchor_i, GROUP)
                    dve.wait_ge(LA.anchor_i, done[3])
                    dve.tensor_tensor(ao[:, :, :, 0:HD], anc[:, :, :, 0:HD],
                                      ao_i[:, :, :].unsqueeze(3).to_broadcast([AROWS, GROUP, 2 * NHG, HD]),
                                      ALU.mult).then_inc(LA.ao, GROUP)

                def lay_globals(t):
                    dve.wait_ge(LA.globals, done[3])
                    dve.wait_ge(LA.kvc, done[t])
                    for b in range(2):
                        op = dve.tensor_tensor(
                            kvb[:, t, b, :, 0, :, :],
                            global_bank.rearrange("p (t g b v) -> p t g b v", t=GROUP, b=2, v=VAUG)[:, t, :, b, :]
                            .unsqueeze(2).to_broadcast([128, NHG, HG, VAUG]),
                            head_rows.unsqueeze(1).unsqueeze(3).to_broadcast([128, NHG, HG, VAUG]), ALU.mult)
                    op.then_inc(LA.gbd, 1)

                def combine(t):
                    lin = lin_bank(t).rearrange("p (g k h v) -> p g k h v", k=2, h=HG, v=VAUG)
                    by_group = lambda x: x.rearrange("p (g h) -> p g h", h=HG)
                    dve.wait_ge(LA.lin, done[t])
                    for k in range(2):
                        op = dve.tensor_scalar(by_group(lin_n[:, t, k, :]), lin[:, :, k, :, HD], NORM_MIN, None, ALU.max)
                    op.then_inc(LA.l_max, 1)
                    dve.wait_ge(LA.l_max, done[t])
                    dve.reciprocal(lin_i[:, t, :, :], lin_n[:, t, :, :]).then_inc(LA.l_inv, 1)
                    dve.wait_ge(LA.l_inv, done[t])
                    dve.tensor_tensor(lin_i[:, t, :, :], lin_i[:, t, :, :],
                                      band_w[:, 1:3].unsqueeze(2).to_broadcast([128, 2, HEADS]), ALU.mult).then_inc(LA.l_w, 1)
                    dve.wait_ge(LA.l_w, done[t])
                    for k, dst, n in ((0, padded[:, t, :, 0:HD].rearrange("p (g h) f -> p g h f", h=HG), LA.glob),
                                      (1, o_str[:, t, :].rearrange("p (g h f) -> p g h f", h=HG, f=HD), LA.str)):
                        dve.tensor_tensor(dst, lin[:, :, k, :, 0:HD], by_group(lin_i[:, t, k, :]).unsqueeze(3)
                                          .to_broadcast([128, NHG, HG, HD]), ALU.mult).then_inc(n, 1)
                    dve.wait_ge(LA.glob, done[t])
                    dve.wait_ge(LA.str, done[t])
                    dve.tensor_tensor(padded[:, t, :, 0:HD], padded[:, t, :, 0:HD],
                                      o_str[:, t, :].rearrange("p (h f) -> p h f", f=HD), ALU.add).then_inc(LA.sum, 1)

                mask(0)
                mask(1)
                anchor_outputs()
                for t in all_tiles():
                    lay_globals(t)
                combine(0)
                combine(1)
                mask(2)
                combine(2)
                mask(3)
                combine(3)
                add_norm(LN[3], OUT[2], h)
                dve.wait_ge(ML.logits, done[GROUP - 1])
                choose(tlg[:, :, 0:EXPERTS], EXPERTS, 1, 1.0, ML, at(i * CHOICE))
                biases = at(i * (EXPERTS * GROUP))
                for e in range(EXPERTS):
                    for t in all_tiles():
                        if e:
                            dve.wait_ge(ML.biased, biases + ((e - 1) * GROUP + t + 1))
                        dve.scalar_tensor_tensor(out=h[:, t, :], in0=b2[:, e, :], scalar=picked[:, t, e:e + 1],
                                                 in1=h[:, t, :], op0=ALU.mult, op1=ALU.add).then_inc(ML.biased, 1)
                if not last:
                    embed([at(count) for count in steps(i * GROUP + GROUP)])
                for t in all_tiles():
                    dve.wait_ge(ML.outputs, done[t])
                    dve.wait_ge(ML.biased, biases + ((EXPERTS - 1) * GROUP + t + 1))
                    for e in range(EXPERTS):
                        if e:
                            dve.wait_ge((ML.acc0, ML.acc1)[e - 1], done[t])
                        dve.scalar_tensor_tensor(out=h[:, t, :], in0=bank(t, e, D), scalar=picked[:, t, e:e + 1],
                                                 in1=h[:, t, :], op0=ALU.mult, op1=ALU.add)\
                            .then_inc((ML.acc0, ML.acc1, ML.down)[e], 1)

            with dve.Fori(0, STEPS - 1) as i:
                step(i, False)
            step(STEPS - 1, True)


def kernel(**inp):
    import ml_dtypes
    import concourse.bacc as bacc
    from concourse.bass_utils import run_bass_kernel_spmd

    f = {k: np.asarray(v) for k, v in inp.items()}
    one = np.float32

    x = f["x"].reshape(BATCH, CHANNELS, 8, PATCH, 8, PATCH).transpose(0, 1, 2, 4, 3, 5).reshape(TOKENS, D_IN)
    x = np.ascontiguousarray(x.reshape(STEPS, GT, KIN, 128).transpose(0, 3, 2, 1))
    tok_w = f["L0_tok_W"].reshape(D, CHANNELS, 256).transpose(2, 1, 0).reshape(KIN, 128, D).transpose(1, 0, 2)

    def chunks(w):
        out = np.zeros((128, 2, w.shape[1]), one)
        out[:, 0], out[0:REST, 1], out[REST:, 1] = w[0:128], w[128:], w[128:]
        return out

    def by_head(w):
        return w.reshape(w.shape[0], 3, HEADS, HD)

    def softmax_columns(w):
        b = by_head(w)
        v = b[:, 2].reshape(-1, HEADS // 2, 2, HD).transpose(0, 2, 3, 1).reshape(-1, HEADS, HD)
        return np.concatenate([b[:, 0], b[:, 1], v], 1).reshape(w.shape[0], 3 * D)

    def rows_128(w, bias=None):
        out = np.zeros((128, 2, D), one)
        out[:, 0], out[0:64, 1] = w[0:128], w[128:]
        if bias is not None:
            out[64, 1] = bias
        return out

    def by_place(w):
        out = np.zeros((NHG, HG, 32, D), one)
        out[:, :, 0:HD] = w.reshape(NHG, HG, HD, D)
        return out.reshape(NHG, 128, D).transpose(1, 0, 2)

    lora_up = f["L0_ffn_B_lora"].transpose(0, 2, 1).reshape(128, 3 * D)
    gate = np.concatenate([f["L0_ffn_W_gate"].T, f["L0_ffn_A"].reshape(128, D).T], 1)
    aq = f["L1_attn_anchor_q"].reshape(HEADS, ANCHORS, HD)
    anc_k = np.zeros((128, NHG, AROWS), one)
    anc_km = np.zeros_like(anc_k)
    for g in range(NHG):
        for j in range(HG):
            anc_k[32 * j:32 * j + HD, g, j * ANCHORS:(j + 1) * ANCHORS] = aq[HG * g + j].T
            anc_km[32 * j:32 * j + HD, g, j * ANCHORS:(j + 1) * ANCHORS] = 1.0
    w1 = f["L1_ffn_W1"].reshape(EXPERTS, D, FF).transpose(1, 0, 2).reshape(D, EXPERTS * FF)

    pos = np.arange(128) % SEQ
    img = np.arange(128) // SEQ
    freq = (1.0 / 10000.0) ** np.linspace(0.0, 1.0, HD // 4, dtype=one)
    theta = (np.tile(np.arange(HEADS, dtype=one), 2)[:, None] * freq[None, :]).astype(one).reshape(-1)
    cst = np.zeros((128, C_END), one)
    cst[:, C_ID:C_ID + 128] = np.eye(128)
    off = pos[:, None] - pos[None, :]
    cst[:, C_BAND:C_BAND + 128] = (off >= -(WINDOW // 2)) & (off < WINDOW - WINDOW // 2) & (img[:, None] == img[None, :])
    cst[:, C_COS:C_SIN], cst[:, C_SIN:C_STRIDE] = np.cos(theta), np.sin(theta)
    cst[:, C_STRIDE] = pos % STRIDE == 0
    cst[:, C_PAD] = np.maximum(WINDOW // 2 - pos, 0) + np.maximum(pos + WINDOW - WINDOW // 2 - SEQ, 0)
    cst[:, C_HEAD:C_HEAD + HG] = np.arange(128)[:, None] // 32 == np.arange(HG)[None, :]
    cst[:, C_TRI:C_TRI + 64] = (np.arange(8)[None, :] < np.arange(8)[:, None]).reshape(64)
    cst[:, C_HALFNEG] = -0.5
    cst[:, C_MEAN:C_MEAN + 128] = (img[:, None] == img[None, :]) / SEQ
    causal = np.where(np.arange(SEQ)[None, :] > pos[:, None], MASKED, 0.0)

    arrays = {
        "x": x, "tok_w": tok_w, "tok_b": np.broadcast_to(f["L0_tok_b"], (128, D)), "cst": cst,
        "qkv_w0": chunks(softmax_columns(f["L0_attn_w_qkv"])),
        "qkv_w1": chunks(softmax_columns(f["L0_ffn_W_qkv"].T)),
        "qkv_w2": chunks(f["L1_attn_qkv_w"].T),
        "out_w0": rows_128(f["L0_attn_w_o"]),
        "out_w1": rows_128(f["L0_ffn_W_proj"].T, f["L0_ffn_b_proj"]),
        "out_w2": by_place(f["L1_attn_out_w"].T),
        "causal": np.tile(causal, (1, BANK // SEQ)).astype(ml_dtypes.bfloat16), "identb": np.eye(128).astype(ml_dtypes.bfloat16),
        "qkv_b": np.broadcast_to(softmax_columns(f["L0_ffn_b_qkv"][None])[0], (128, 3 * D)),
        "gate_w": chunks(gate), "gate_b": np.broadcast_to(f["L0_ffn_b_gate"], (128, LORA_EXPERTS)), "lora_up": softmax_columns(lora_up),
        "anc_k": anc_k, "anc_b": anc_k.transpose(2, 1, 0), "anc_km": anc_km, "anc_bm": anc_km.transpose(2, 1, 0),
        "band_w": np.broadcast_to(np.stack([f["L1_attn_w_local"], f["L1_attn_w_global"], f["L1_attn_w_stride"]]), (128, 3)),
        "top_w": chunks(np.pad(f["L1_ffn_Wg"].T, ((0, 0), (0, 1)))), "w1": chunks(w1), "b1": f["L1_ffn_b1"].reshape(EXPERTS * MF, 128).T,
        "w2": f["L1_ffn_W2"].reshape(EXPERTS, MF, 128, D).transpose(2, 0, 1, 3),
        "b2": np.broadcast_to(f["L1_ffn_b2"], (128, EXPERTS, D)),
    }
    nc = bacc.Bacc("TRN2", target_bir_lowering=False, num_devices=1)
    feed, aps = {}, {}
    for name, v in arrays.items():
        v = np.ascontiguousarray(v)
        feed["in_" + name] = v
        aps[name] = nc.dram_tensor("in_" + name, v.shape, mybir.dt.from_np(v.dtype), kind="ExternalInput").ap()
    aps["out"] = nc.dram_tensor("out_h", (TOKENS // TILE, TILE, D), F32, kind="ExternalOutput").ap()
    build(nc, aps)
    r = run_bass_kernel_spmd(nc, [feed], core_ids=[0])
    return r.results[0]["out_h"].reshape(BATCH, SEQ, D)
```
